# Optimizing a Trainium2 kernel written in Bass

```python
import numpy as np
import jax
import jax.numpy as jnp

def _softmax(x, axis=-1):
    return jax.nn.softmax(x, axis=axis)

def _gelu(x):
    return jax.nn.gelu(x, approximate=True)

def _silu(x):
    return jax.nn.silu(x)

def _sigmoid(x):
    return jax.nn.sigmoid(x)

def _layernorm(x, axis=-1, eps=1e-05):
    m = jnp.mean(x, axis=axis, keepdims=True)
    v = jnp.var(x, axis=axis, keepdims=True)
    return (x - m) / jnp.sqrt(v + eps)

def _scatter_add(tgt, idx, src, axis=0):
    return tgt.at[idx].add(src)

def _segment_sum(src, seg, n):
    return jax.ops.segment_sum(src, seg, n)
kernel_name = 'mk_lm_tower_d2_tok_ids512_r4_673670'

def setup_inputs(seed: int=0):
    np.random.seed(seed)
    _w = jnp.asarray

    def _rec_inputs():
        import jax
        import jax.numpy as jnp
        _rk = jax.random.key(seed)
        x = jax.random.randint(jax.random.fold_in(_rk, 1), (8, 256), 0, 12564, jnp.int32)
        return x
    x = _rec_inputs()

    def _L0_tok_setup():
        import jax, jax.numpy as jnp
        import numpy as np
        VOCAB, D, B, S, E = (50257, 128, 8, 512, 5)
        L_CONST = 1000000000.0
        key = jax.random.key(seed)
        k = jax.random.split(key, 5)
        return {'input_ids': jax.random.randint(k[0], (B, S), 0, VOCAB, dtype=jnp.int64), 'emb_table': jax.random.normal(k[1], (VOCAB, D), dtype=jnp.float32), 'gate_table': jax.random.uniform(k[2], (VOCAB, 1), dtype=jnp.float32, minval=0.001, maxval=1.0), 'expert_w': jax.random.normal(k[3], (E, D, D), dtype=jnp.float32) * 0.02, 'expert_b': jax.random.normal(k[4], (E, D), dtype=jnp.float32) * 0.02}
    _L0_tok_all = _L0_tok_setup()
    _L0_tok_in = {k: v for k, v in _L0_tok_all.items() if k in ('emb_table', 'gate_table', 'expert_w', 'expert_b')}
    del _L0_tok_all

    def _L0_attn_setup():
        import jax, jax.numpy as jnp
        import numpy as np
        CHUNK = 64
        GATE_NORM = 16.0

        def _short_conv(x, w):
            K = w.shape[-1]
            y = jax.lax.conv_general_dilated(jnp.swapaxes(x, 1, 2), w, window_strides=(1,), padding=[(K - 1, 0)], feature_group_count=w.shape[0], dimension_numbers=('NCH', 'OIH', 'NCH'))
            return jnp.swapaxes(y, 1, 2)

        def _gla_chunkwise(q, k, v, alpha, chunk=CHUNK):
            B, L, H, D = q.shape
            N = L // chunk

            def to_chunks(t):
                return t.reshape(B, N, chunk, H, D).transpose(1, 0, 3, 2, 4)
            Qs, Ks, Vs, As = map(to_chunks, (q, k, v, alpha))
            S0 = jnp.zeros((B, H, D, D), jnp.float32)

            def step(S, inp):
                Q, K, V, A = inp
                ca = jnp.cumsum(A, axis=2)
                e = jnp.exp(ca)
                Qe = Q * e
                Ke = K * jnp.exp(-ca)
                W = jnp.tril(Qe @ jnp.swapaxes(Ke, -1, -2))
                O = Qe @ S + W @ V
                end = ca[:, :, -1, :]
                S_new = jnp.exp(end)[:, :, :, None] * S + jnp.swapaxes(jnp.exp(end[:, :, None, :] - ca) * K, -1, -2) @ V
                return (S_new, O)
            _, Os = jax.lax.scan(step, S0, (Qs, Ks, Vs, As))
            return Os.transpose(1, 0, 3, 2, 4).reshape(B, L, H, D)
        key = jax.random.key(seed)
        ks = jax.random.split(key, 12)
        B, L, D = (2, 4096, 128)
        GR, CK = (16, 4)
        s = 0.02
        return {'hidden_states': jax.random.normal(ks[0], (B, L, D), jnp.float32), 'Wk': jax.random.normal(ks[1], (D, D), jnp.float32) * s, 'Wq': jax.random.normal(ks[2], (D, D), jnp.float32) * s, 'Wv': jax.random.normal(ks[3], (D, D), jnp.float32) * s, 'conv_k': jax.random.normal(ks[4], (D, 1, CK), jnp.float32) * 0.3, 'conv_q': jax.random.normal(ks[5], (D, 1, CK), jnp.float32) * 0.3, 'conv_v': jax.random.normal(ks[6], (D, 1, CK), jnp.float32) * 0.3, 'Wg1': jax.random.normal(ks[7], (GR, D), jnp.float32) * s, 'Wg2': jax.random.normal(ks[8], (D, GR), jnp.float32) * s, 'bg2': jax.random.normal(ks[9], (D,), jnp.float32) * 0.1, 'norm_w': jnp.ones((D,), jnp.float32), 'Wo': jax.random.normal(ks[10], (D, D), jnp.float32) * s}
    _L0_attn_all = _L0_attn_setup()
    _L0_attn_in = {k: v for k, v in _L0_attn_all.items() if k in ('Wk', 'Wq', 'Wv', 'conv_k', 'conv_q', 'conv_v', 'Wg1', 'Wg2', 'bg2', 'norm_w', 'Wo')}
    del _L0_attn_all

    def _L0_ffn_setup():
        import jax, jax.numpy as jnp
        import numpy as np
        TOP_K = 2
        key = jax.random.key(seed)
        ks = jax.random.split(key, 4)
        b, t, d, e, h = (2, 512, 128, 8, 256)
        scale = 0.02
        return {'x': jax.random.normal(ks[0], (b, t, d), dtype=jnp.float32), 'router_w': jax.random.normal(ks[1], (e, d), dtype=jnp.float32) * scale, 'router_b': jnp.zeros((e,), dtype=jnp.float32), 'fc1_w': jax.random.normal(ks[2], (e, 2 * h, d), dtype=jnp.float32) * scale, 'fc1_b': jnp.zeros((e, 2 * h), dtype=jnp.float32), 'fc2_w': jax.random.normal(ks[3], (e, d, h), dtype=jnp.float32) * scale, 'fc2_b': jnp.zeros((e, d), dtype=jnp.float32)}
    _L0_ffn_all = _L0_ffn_setup()
    _L0_ffn_in = {k: v for k, v in _L0_ffn_all.items() if k in ('router_w', 'router_b', 'fc1_w', 'fc1_b', 'fc2_w', 'fc2_b')}
    del _L0_ffn_all

    def _L1_attn_setup():
        import jax, jax.numpy as jnp
        import numpy as np
        D_MODEL = 128
        NHEAD = 8
        WINDOW = 64
        key = jax.random.key(seed)
        ks = jax.random.split(key, 5)
        B, T, D = (4, 2048, D_MODEL)
        x = jax.random.normal(ks[0], (B, T, D), jnp.float32)
        Wqkv = jax.random.normal(ks[1], (D, 3 * D), jnp.float32) * 0.02
        bqkv = jnp.zeros((3 * D,), jnp.float32)
        Wo = jax.random.normal(ks[2], (D, D), jnp.float32) * 0.02
        bo = jnp.zeros((D,), jnp.float32)
        rel_pos_bias = jax.random.normal(ks[3], (WINDOW, NHEAD), jnp.float32) * 0.02
        return {'x': x, 'Wqkv': Wqkv, 'bqkv': bqkv, 'Wo': Wo, 'bo': bo, 'rel_pos_bias': rel_pos_bias}
    _L1_attn_all = _L1_attn_setup()
    _L1_attn_in = {k: v for k, v in _L1_attn_all.items() if k in ('Wqkv', 'bqkv', 'Wo', 'bo', 'rel_pos_bias')}
    del _L1_attn_all

    def _L1_ffn_setup():
        import jax, jax.numpy as jnp
        import numpy as np
        E = 64
        K = 6
        NS = 2
        D = 128
        F = 128

        def _swiglu_ffn(x, wg, wu, wd):
            return jax.nn.silu(x @ wg) * (x @ wu) @ wd
        key = jax.random.key(seed)
        ks = jax.random.split(key, 8)
        s = 0.02
        return {'hidden_states': jax.random.normal(ks[0], (2, 256, D), dtype=jnp.float32), 'Wr': jax.random.normal(ks[1], (D, E), dtype=jnp.float32) * s, 'sWg': jax.random.normal(ks[2], (NS, D, F), dtype=jnp.float32) * s, 'sWu': jax.random.normal(ks[3], (NS, D, F), dtype=jnp.float32) * s, 'sWd': jax.random.normal(ks[4], (NS, F, D), dtype=jnp.float32) * s, 'Wg': jax.random.normal(ks[5], (E, D, F), dtype=jnp.float32) * s, 'Wu': jax.random.normal(ks[6], (E, D, F), dtype=jnp.float32) * s, 'Wd': jax.random.normal(ks[7], (E, F, D), dtype=jnp.float32) * s}
    _L1_ffn_all = _L1_ffn_setup()
    _L1_ffn_in = {k: v for k, v in _L1_ffn_all.items() if k in ('Wr', 'sWg', 'sWu', 'sWd', 'Wg', 'Wu', 'Wd')}
    del _L1_ffn_all
    return {'x': x, 'L0_tok_emb_table': _L0_tok_in['emb_table'], 'L0_tok_gate_table': _L0_tok_in['gate_table'], 'L0_tok_expert_w': _L0_tok_in['expert_w'], 'L0_tok_expert_b': _L0_tok_in['expert_b'], 'L0_attn_Wk': _L0_attn_in['Wk'], 'L0_attn_Wq': _L0_attn_in['Wq'], 'L0_attn_Wv': _L0_attn_in['Wv'], 'L0_attn_conv_k': _L0_attn_in['conv_k'], 'L0_attn_conv_q': _L0_attn_in['conv_q'], 'L0_attn_conv_v': _L0_attn_in['conv_v'], 'L0_attn_Wg1': _L0_attn_in['Wg1'], 'L0_attn_Wg2': _L0_attn_in['Wg2'], 'L0_attn_bg2': _L0_attn_in['bg2'], 'L0_attn_norm_w': _L0_attn_in['norm_w'], 'L0_attn_Wo': _L0_attn_in['Wo'], 'L0_ffn_router_w': _L0_ffn_in['router_w'], 'L0_ffn_router_b': _L0_ffn_in['router_b'], 'L0_ffn_fc1_w': _L0_ffn_in['fc1_w'], 'L0_ffn_fc1_b': _L0_ffn_in['fc1_b'], 'L0_ffn_fc2_w': _L0_ffn_in['fc2_w'], 'L0_ffn_fc2_b': _L0_ffn_in['fc2_b'], 'L1_attn_Wqkv': _L1_attn_in['Wqkv'], 'L1_attn_bqkv': _L1_attn_in['bqkv'], 'L1_attn_Wo': _L1_attn_in['Wo'], 'L1_attn_bo': _L1_attn_in['bo'], 'L1_attn_rel_pos_bias': _L1_attn_in['rel_pos_bias'], 'L1_ffn_Wr': _L1_ffn_in['Wr'], 'L1_ffn_sWg': _L1_ffn_in['sWg'], 'L1_ffn_sWu': _L1_ffn_in['sWu'], 'L1_ffn_sWd': _L1_ffn_in['sWd'], 'L1_ffn_Wg': _L1_ffn_in['Wg'], 'L1_ffn_Wu': _L1_ffn_in['Wu'], 'L1_ffn_Wd': _L1_ffn_in['Wd']}

def reference(x, L0_tok_emb_table, L0_tok_gate_table, L0_tok_expert_w, L0_tok_expert_b, L0_attn_Wk, L0_attn_Wq, L0_attn_Wv, L0_attn_conv_k, L0_attn_conv_q, L0_attn_conv_v, L0_attn_Wg1, L0_attn_Wg2, L0_attn_bg2, L0_attn_norm_w, L0_attn_Wo, L0_ffn_router_w, L0_ffn_router_b, L0_ffn_fc1_w, L0_ffn_fc1_b, L0_ffn_fc2_w, L0_ffn_fc2_b, L1_attn_Wqkv, L1_attn_bqkv, L1_attn_Wo, L1_attn_bo, L1_attn_rel_pos_bias, L1_ffn_Wr, L1_ffn_sWg, L1_ffn_sWu, L1_ffn_sWd, L1_ffn_Wg, L1_ffn_Wu, L1_ffn_Wd):
    import jax
    import jax.numpy as jnp

    def _L0_tok_ref(input_ids, emb_table, gate_table, expert_w, expert_b):
        import jax, jax.numpy as jnp
        import numpy as np
        VOCAB, D, B, S, E = (50257, 128, 8, 512, 5)
        L_CONST = 1000000000.0
        d = emb_table.shape[1]
        n_exp = expert_w.shape[0]
        data = emb_table[input_ids]
        gate = gate_table[input_ids] * d
        idx_arr = jnp.arange(d, dtype=gate.dtype)
        frac = (L_CONST * gate - jnp.floor(L_CONST * gate)) / L_CONST
        mask = (idx_arr[None, None, :] < gate).astype(gate.dtype) + frac
        divisor = float(d // n_exp)
        eidx = jnp.clip(jnp.floor_divide(mask.sum(-1), divisor).astype(jnp.int32), 0, n_exp - 1)
        xm = data * mask
        y_all = jnp.einsum('bsd,eod->bseo', xm, expert_w) + expert_b[None, None]
        onehot = jax.nn.one_hot(eidx, n_exp, dtype=xm.dtype)
        return jnp.einsum('bseo,bse->bso', y_all, onehot)

    def _L0_attn_ref(hidden_states, Wk, Wq, Wv, conv_k, conv_q, conv_v, Wg1, Wg2, bg2, norm_w, Wo):
        import jax, jax.numpy as jnp
        import numpy as np
        CHUNK = 64
        GATE_NORM = 16.0

        def _short_conv(x, w):
            K = w.shape[-1]
            y = jax.lax.conv_general_dilated(jnp.swapaxes(x, 1, 2), w, window_strides=(1,), padding=[(K - 1, 0)], feature_group_count=w.shape[0], dimension_numbers=('NCH', 'OIH', 'NCH'))
            return jnp.swapaxes(y, 1, 2)

        def _gla_chunkwise(q, k, v, alpha, chunk=CHUNK):
            B, L, H, D = q.shape
            N = L // chunk

            def to_chunks(t):
                return t.reshape(B, N, chunk, H, D).transpose(1, 0, 3, 2, 4)
            Qs, Ks, Vs, As = map(to_chunks, (q, k, v, alpha))
            S0 = jnp.zeros((B, H, D, D), jnp.float32)

            def step(S, inp):
                Q, K, V, A = inp
                ca = jnp.cumsum(A, axis=2)
                e = jnp.exp(ca)
                Qe = Q * e
                Ke = K * jnp.exp(-ca)
                W = jnp.tril(Qe @ jnp.swapaxes(Ke, -1, -2))
                O = Qe @ S + W @ V
                end = ca[:, :, -1, :]
                S_new = jnp.exp(end)[:, :, :, None] * S + jnp.swapaxes(jnp.exp(end[:, :, None, :] - ca) * K, -1, -2) @ V
                return (S_new, O)
            _, Os = jax.lax.scan(step, S0, (Qs, Ks, Vs, As))
            return Os.transpose(1, 0, 3, 2, 4).reshape(B, L, H, D)
        B, L, D = hidden_states.shape
        x = hidden_states
        k = jax.nn.silu(_short_conv(x @ Wk.T, conv_k))
        q = jax.nn.silu(_short_conv(x @ Wq.T, conv_q))
        v = jax.nn.silu(_short_conv(x @ Wv.T, conv_v))
        gate = x @ Wg1.T @ Wg2.T + bg2
        alpha = jax.nn.log_sigmoid(gate) / GATE_NORM
        k = k / (jnp.linalg.norm(k, axis=-1, keepdims=True) + 1e-05)
        q = q / (jnp.linalg.norm(q, axis=-1, keepdims=True) + 1e-05)
        H = 1
        qh = q.reshape(B, L, H, D)
        kh = k.reshape(B, L, H, D)
        vh = v.reshape(B, L, H, D)
        ah = alpha.reshape(B, L, H, D)
        o = _gla_chunkwise(qh, kh, vh, ah)
        o = o.reshape(B, L, D)
        o = o * jax.lax.rsqrt(jnp.mean(o * o, axis=-1, keepdims=True) + 1e-06) * norm_w
        return o @ Wo.T

    def _L0_ffn_ref(x, router_w, router_b, fc1_w, fc1_b, fc2_w, fc2_b):
        import jax, jax.numpy as jnp
        import numpy as np
        TOP_K = 2
        n_experts = router_w.shape[0]
        temp = 1.0
        logits = (jnp.einsum('btd,ed->bte', x, router_w) + router_b) / temp
        topk_val, topk_idx = jax.lax.top_k(logits, TOP_K)
        weights = jax.nn.softmax(topk_val, axis=-1)
        onehot = jax.nn.one_hot(topk_idx, n_experts, dtype=x.dtype)
        cw = jnp.einsum('btk,btke->bte', weights, onehot)
        h = jnp.einsum('btd,efd->btef', x, fc1_w) + fc1_b
        h1, h2 = jnp.split(h, 2, axis=-1)
        a = jax.nn.silu(h1) * h2
        y = jnp.einsum('bteh,edh->bted', a, fc2_w) + fc2_b
        out = jnp.einsum('bted,bte->btd', y, cw)
        return out

    def _L1_attn_ref(x, Wqkv, bqkv, Wo, bo, rel_pos_bias):
        import jax, jax.numpy as jnp
        import numpy as np
        D_MODEL = 128
        NHEAD = 8
        WINDOW = 64
        B, T, D = x.shape
        H, W = (NHEAD, WINDOW)
        Dh = D // H
        nb = T // W
        qkv = x @ Wqkv + bqkv
        q, k, v = jnp.split(qkv, 3, axis=-1)
        blk = lambda a: a.reshape(B, nb, W, H, Dh)
        q, k, v = (blk(q), blk(k), blk(v))

        def with_prev(a):
            prev = jnp.concatenate([jnp.zeros_like(a[:, :1]), a[:, :-1]], axis=1)
            return jnp.concatenate([prev, a], axis=2)
        k2, v2 = (with_prev(k), with_prev(v))
        scores = jnp.einsum('bnuhd,bnjhd->bnujh', q, k2) / jnp.sqrt(jnp.float32(Dh))
        u = jnp.arange(W)[:, None]
        j = jnp.arange(2 * W)[None, :]
        w_idx = j - u - 1
        band = (w_idx >= 0) & (w_idx < W)
        bias = rel_pos_bias[jnp.clip(w_idx, 0, W - 1)]
        i = jnp.arange(nb)[:, None, None]
        keypos_ok = (i - 1) * W + j[None] >= 0
        valid = band[None] & keypos_ok
        scores = scores + bias[None, None]
        scores = jnp.where(valid[None, :, :, :, None], scores, -jnp.inf)
        attn = jax.nn.softmax(scores, axis=3)
        ctx = jnp.einsum('bnujh,bnjhd->bnuhd', attn, v2).reshape(B, T, D)
        return ctx @ Wo + bo

    def _L1_ffn_ref(hidden_states, Wr, sWg, sWu, sWd, Wg, Wu, Wd):
        import jax, jax.numpy as jnp
        import numpy as np
        E = 64
        K = 6
        NS = 2
        D = 128
        F = 128

        def _swiglu_ffn(x, wg, wu, wd):
            return jax.nn.silu(x @ wg) * (x @ wu) @ wd
        B, S, d = hidden_states.shape
        x = hidden_states.reshape(-1, d)
        N = x.shape[0]
        shared = jnp.zeros_like(x)
        for e in range(NS):
            shared = shared + _swiglu_ffn(x, sWg[e], sWu[e], sWd[e])
        logits = x @ Wr
        probs = jax.nn.softmax(logits, axis=-1)
        top_w, top_i = jax.lax.top_k(probs, K)
        top_w = top_w / jnp.sum(top_w, axis=-1, keepdims=True)
        gate = jnp.zeros((N, E), dtype=x.dtype).at[jnp.arange(N)[:, None], top_i].set(top_w)
        routed = jnp.zeros_like(x)
        for e in range(E):
            routed = routed + _swiglu_ffn(x, Wg[e], Wu[e], Wd[e]) * gate[:, e:e + 1]
        out = (shared + routed + x).reshape(B, S, d)
        return out
    h = _L0_tok_ref(x, L0_tok_emb_table, L0_tok_gate_table, L0_tok_expert_w, L0_tok_expert_b)
    h = h + _L0_attn_ref(_layernorm(h, axis=-1), L0_attn_Wk, L0_attn_Wq, L0_attn_Wv, L0_attn_conv_k, L0_attn_conv_q, L0_attn_conv_v, L0_attn_Wg1, L0_attn_Wg2, L0_attn_bg2, L0_attn_norm_w, L0_attn_Wo)
    h = h + _L0_ffn_ref(_layernorm(h, axis=-1), L0_ffn_router_w, L0_ffn_router_b, L0_ffn_fc1_w, L0_ffn_fc1_b, L0_ffn_fc2_w, L0_ffn_fc2_b)
    h = h + _L1_attn_ref(_layernorm(h, axis=-1), L1_attn_Wqkv, L1_attn_bqkv, L1_attn_Wo, L1_attn_bo, L1_attn_rel_pos_bias)
    h = h + _L1_ffn_ref(_layernorm(h, axis=-1), L1_ffn_Wr, L1_ffn_sWg, L1_ffn_sWu, L1_ffn_sWd, L1_ffn_Wg, L1_ffn_Wu, L1_ffn_Wd)
    return h

_drawn_inputs = setup_inputs


def setup_inputs(seed=0):
    import zlib

    import numpy as np

    out = dict(_drawn_inputs(seed))
    spreads = {'L0_attn_norm_w': (1.0, 0.2),
     'L0_ffn_router_b': (0.0, 0.1),
     'L0_ffn_fc1_b': (0.0, 0.631),
     'L0_ffn_fc2_b': (0.0, 0.1),
     'L1_attn_bqkv': (0.0, 0.1),
     'L1_attn_bo': (0.0, 0.1)}
    factors = {'L0_attn_Wg1': 8.0,
     'L0_attn_Wg2': 6.049,
     'L1_attn_rel_pos_bias': 48.985,
     'L1_ffn_Wr': 8.0,
     'L1_ffn_sWg': 8.0,
     'L1_ffn_sWu': 8.0,
     'L1_ffn_sWd': 8.0,
     'L1_ffn_Wg': 8.0,
     'L1_ffn_Wu': 8.0,
     'L1_ffn_Wd': 8.0}
    for name, (base, spread) in spreads.items():
        noise = np.random.default_rng([zlib.crc32(name.encode()), seed]).standard_normal(out[name].shape)
        drawn = base * np.exp(spread * noise) if base else spread * noise
        out[name] = jnp.asarray(drawn.astype(out[name].dtype))
    for name, factor in factors.items():
        out[name] = (out[name] * factor).astype(out[name].dtype)
    return out
```

```python
from contextlib import ExitStack

import concourse.bass as bass
from concourse import mybir
from concourse.alu_op_type import AluOpType as ALU

F32 = mybir.dt.float32
I32 = mybir.dt.int32
U32 = mybir.dt.uint32
ACT = mybir.ActivationFunctionType
AX = mybir.AxisListType
ds = bass.ds

P = 128
D = 128
B, L = 8, 256
N = B * L
T = N // P
QT = 4
QN = QT * P
NQ = T // QT
SQ = QN // L
EPS_LN = 1e-5

E_TOK = 5
CHUNK = 64
NC_SEQ = L // CHUNK
GATE_NORM = 16.0
TAPS = 4
RANK = 16

E0, F0 = 8, 256
W0COLS = 2 * F0 + 2 * D + 4
HEADS, DH, WIN = 8, 16, 64
KW = P + WIN
NEG = -1.0e30

E1, F1, TOPK1, NS1 = 64, 128, 6, 2
EXP1 = E1 + NS1
W1COLS = 3 * D

_cols = {}
WCOLS = 0
for _name, _n in (("tok_w", E_TOK * D), ("tok_b", D), ("wk", D), ("wq", D), ("wv", D), ("wo0", D), ("wg1", RANK),
                  ("wg2", D), ("conv_k", TAPS), ("conv_q", TAPS), ("conv_v", TAPS), ("bg2", 1), ("norm_w", 1),
                  ("rw0", E0), ("rb0", E0), ("fc2_b", D), ("aq", 2 * P), ("ak", 2 * P), ("av", D), ("abq", 2),
                  ("abk", 2), ("abv", D), ("awo", D), ("abo", D), ("wr1", E1)):
    _cols[_name] = (WCOLS, _n)
    WCOLS += _n
_ccols = {}
CCOLS = 0
for _name, _n in (("ident", P), ("iota", P), ("reset", QN), ("ones", P), ("thr", QT * (E_TOK + 1))):
    _ccols[_name] = (CCOLS, _n)
    CCOLS += _n


def tower_kernel(nc, ids, emb_gate, weights, consts, causal, rel, w0, w1, out, last_stage=5):
    ctx = ExitStack()
    with ctx:
        def sb(name, shape, dt=F32, scope=ctx):
            return scope.enter_context(nc.sbuf_tensor(name, shape, dt))

        def sem(name):
            return ctx.enter_context(nc.semaphore(name))

        ps = ctx.enter_context(nc.psum_tensor("ps", [P, 8, 512], F32))
        h = sb("h", [P, T, D])
        wsb = sb("wsb", [P, WCOLS])
        csb = sb("csb", [P, CCOLS])
        causal_sb = sb("causal_sb", [P, P], U32)
        band = sb("band", [P, HEADS, KW])
        carrier = sb("carrier", [P, 1])

        def W(name, rows=P):
            o, n = _cols[name]
            return wsb[0:rows, o:o + n]

        def C(name, rows=P):
            o, n = _ccols[name]
            return csb[0:rows, o:o + n]

        ident = C("ident")
        ones_col = C("ones")[:, 0:1]
        ones_row = C("ones", 1)

        loaded = sem("loaded")
        band_made = sem("band_made")

        def ln_stats(dve, stats, mv, rstd, tiles, i, var_ready):
            for j in range(tiles):
                dve.bn_stats(stats[:, j, :], h[:, ds(i * tiles + j, 1), :])
            dve.drain()
            for j in range(tiles):
                dve.bn_aggr(mv[:, j, :], stats[:, j, :])
            dve.drain()
            dve.tensor_scalar(rstd[:, 0:tiles], mv[:, 0:tiles, 1], EPS_LN, None, ALU.add).then_inc(var_ready, 1)

        def ln_rstd(pool, rstd, neghalf, tiles):
            return pool.tensor_tensor(rstd[:, 0:tiles], rstd[:, 0:tiles], neghalf[:, 0:tiles], ALU.pow)

        def ln_apply(dve, xn, mv, rstd, tiles, i):
            for j in range(tiles):
                last = dve.tensor_scalar(xn[:, j, :], h[:, ds(i * tiles + j, 1), :], mv[:, j, 0:1], rstd[:, j:j + 1],
                                         ALU.subtract, ALU.mult)
            return last

        def token_stage():
            with ExitStack() as st:
                idx = sb("idx", [P, T], I32, st)
                emb = sb("emb", [P, T, D + 1], F32, st)
                gate = sb("gate", [P, NQ, QT], F32, st)
                scaled = sb("scaled", [P, NQ, QT], F32, st)
                whole_i = sb("whole_i", [P, NQ, QT], I32, st)
                whole = sb("whole", [P, NQ, QT], F32, st)
                frac = sb("frac", [P, NQ, QT], F32, st)
                above = sb("above", [P, NQ, QT, E_TOK + 1], F32, st)
                onehot = sb("onehot", [P, NQ, QT, E_TOK], F32, st)
                mask = sb("mask", [P, QT, D], F32, st)
                xm = sb("xm", [P, 2, QT, D], F32, st)
                xmT = sb("xmT", [P, 2, QN], F32, st)
                ohT = sb("ohT", [E_TOK, 2, QN], F32, st)
                ids_in = sem("ids_in")
                emb_in = [sem(f"emb_in{q}") for q in range(NQ)]
                xm_ready = sem("xm_ready")
                turned = sem("tok_turned")
                moved = sem("tok_moved")
                tok_mm = sem("tok_mm")
                bias_in_h = sem("bias_in_h")
                h_ready = sem("tok_h_ready")
                neg_fill = sem("neg_fill")
                neg_out = sem("neg_out")
                diag_out = sem("diag_out")
                thr = C("thr").rearrange("p (t e) -> p t e", t=QT)
                scratch = nc.dram_tensor("band_scratch", (P, HEADS, KW), F32, kind="Internal").ap()

                block = st.enter_context(nc.Block())

                @block.sync
                def _(sp):
                    sp.dma_start(idx[:, :], ids).then_inc(ids_in, 16)
                    sp.dma_start(csb[:, :], consts).then_inc(loaded, 16)
                    sp.dma_start(wsb[:, :], weights).then_inc(loaded, 16)
                    sp.dma_start(causal_sb[:, :], causal).then_inc(loaded, 16)
                    sp.wait_ge(neg_fill, 1)
                    sp.dma_start(scratch, band[:, :, :]).then_inc(neg_out, 16)
                    sp.wait_ge(neg_out, 16)
                    diagonal = bass.AP(scratch.tensor, 1, [[HEADS * KW + 1, P], [KW, HEADS], [1, WIN]])
                    source = bass.AP(rel.tensor, 0, [[0, P], [WIN, HEADS], [1, WIN]])
                    sp.dma_start(diagonal, source).then_inc(diag_out, 16)
                    sp.wait_ge(diag_out, 16)
                    sp.dma_start(band[:, :, :], scratch).then_inc(band_made, 16)

                @block.gpsimd
                def _(pool):
                    pool.wait_ge(ids_in, 16)
                    for t in range(T):
                        pool.indirect_dma_start(emb[:, t, :], None, emb_gate,
                                                bass.IndirectOffsetOnAxis(ap=idx[:, t:t + 1], axis=0)
                                                ).then_inc(emb_in[t // QT], 16)
                        if t == 0:
                            pool.memset(band[:, :, :], NEG).then_inc(neg_fill, 1)

                def select(dve, q):
                    dve.wait_ge(tok_mm, q + 1)
                    dve.wait_ge(bias_in_h, q + 1)
                    for e in range(E_TOK):
                        for j in range(QT):
                            y = ps[:, j, e * D:(e + 1) * D] if e < 4 else ps[:, 4, j * D:(j + 1) * D]
                            t = QT * q + j
                            last = dve.scalar_tensor_tensor(h[:, t, :], y, onehot[:, q, j, e:e + 1], h[:, t, :],
                                                            ALU.mult, ALU.add)
                        if e < E_TOK - 1:
                            dve.drain()
                    last.then_inc(h_ready, 1)

                @block.vector
                def _(dve):
                    dve.wait_ge(loaded, 48)
                    for q in range(NQ):
                        dve.wait_ge(emb_in[q], 16 * QT)
                        raw = emb[:, QT * q:QT * (q + 1), D]
                        dve.tensor_scalar(gate[:, q, :], raw, float(D), None, ALU.mult)
                        dve.drain()
                        dve.tensor_scalar(scaled[:, q, :], gate[:, q, :], 1.0e9, float(2 ** 23), ALU.mult, ALU.min)
                        dve.tensor_tensor(above[:, q], gate[:, q, :].unsqueeze(2).to_broadcast([P, QT, E_TOK + 1]),
                                          thr, ALU.is_gt)
                        dve.drain()
                        dve.tensor_copy(whole_i[:, q, :], scaled[:, q, :])
                        dve.tensor_tensor(onehot[:, q], above[:, q, :, 0:E_TOK], above[:, q, :, 1:E_TOK + 1],
                                          ALU.subtract)
                        dve.drain()
                        dve.tensor_copy(whole[:, q, :], whole_i[:, q, :])
                        dve.drain()
                        dve.tensor_tensor(frac[:, q, :], scaled[:, q, :], whole[:, q, :], ALU.subtract)
                        dve.drain()
                        dve.scalar_tensor_tensor(frac[:, q, :], frac[:, q, :], 0.0, frac[:, q, :], ALU.is_lt, ALU.add)
                        dve.drain()
                        dve.tensor_scalar(frac[:, q, :], frac[:, q, :], 1.0e-9, None, ALU.mult)
                        dve.drain()
                        for j in range(QT):
                            dve.tensor_scalar(mask[:, j, :], C("iota"), gate[:, q, j:j + 1], frac[:, q, j:j + 1],
                                              ALU.is_lt, ALU.add)
                        dve.drain()
                        if q >= 2:
                            dve.wait_ge(turned, q - 1)
                        dve.tensor_tensor(xm[:, q % 2], emb[:, QT * q:QT * (q + 1), 0:D], mask[:, :, :],
                                          ALU.mult).then_inc(xm_ready, 1)
                        if q >= 1:
                            select(dve, q - 1)
                    select(dve, NQ - 1)

                @block.tensor
                def _(pe):
                    for q in range(NQ):
                        pe.wait_ge(xm_ready, q + 1)
                        if q >= 1:
                            pe.wait_ge(moved, q)
                        for j in range(QT):
                            pe.transpose(ps[:, 6, j * P:(j + 1) * P], xm[:, q % 2, j, :], ident)
                        for j in range(QT):
                            last = pe.transpose(ps[0:E_TOK, 7, j * P:(j + 1) * P], onehot[:, q, j, :], ident)
                        last.then_inc(turned, 1)
                        pe.wait_ge(moved, q + 1)
                        if q >= 1:
                            pe.wait_ge(h_ready, q)
                            pe.wait_ge(bias_in_h, q)
                        for j in range(QT):
                            x = xmT[:, q % 2, j * P:(j + 1) * P]
                            pe.matmul(ps[:, j, :], x, W("tok_w")[:, 0:4 * D], start=True, stop=True)
                            pe.matmul(ps[:, 4, j * D:(j + 1) * D], x, W("tok_w")[:, 4 * D:5 * D], start=True, stop=True)
                            last = pe.matmul(ps[:, 5, j * D:(j + 1) * D], ohT[:, q % 2, j * P:(j + 1) * P],
                                             W("tok_b", E_TOK), start=True, stop=True)
                        last.then_inc(tok_mm, 1)

                @block.scalar
                def _(act):
                    for q in range(NQ):
                        act.wait_ge(turned, q + 1)
                        act.copy(xmT[:, q % 2, :], ps[:, 6, :])
                        act.copy(ohT[:, q % 2, :], ps[0:E_TOK, 7, :]).then_inc(moved, 1)
                        act.wait_ge(tok_mm, q + 1)
                        act.copy(h[:, QT * q:QT * (q + 1), :],
                                 ps[:, 5, :].rearrange("p (t d) -> p t d", t=QT)).then_inc(bias_in_h, 1)

        def gla_stage():
            with ExitStack() as st:
                kT = sb("kT", [P, N], F32, st)
                qT = sb("qT", [P, N], F32, st)
                vT = sb("vT", [P, N], F32, st)
                gT = sb("gT", [P, N], F32, st)
                gla_projections(kT, qT, vT, gT)
                gla_chunks(kT, qT, vT, gT)

        def gla_projections(kT, qT, vT, gT):
            with ExitStack() as st:
                stats = sb("a_stats", [P, QT, 6], F32, st)
                mv = sb("a_mv", [P, QT, 2], F32, st)
                rstd = sb("a_rstd", [P, QT], F32, st)
                neghalf = sb("a_neghalf", [P, QT], F32, st)
                xn = sb("a_xn", [P, QT, D], F32, st)
                xT = sb("a_xT", [P, QN], F32, st)
                g1 = sb("a_g1", [RANK, QN], F32, st)
                cv = sb("a_cv", [P, 3, SQ, L], F32, st)
                var_ready = sem("a_var_ready")
                rstd_ready = sem("a_rstd_ready")
                xn_ready = sem("a_xn_ready")
                turned = sem("a_turned")
                xT_ready = sem("a_xT_ready")
                projected = sem("a_projected")
                g1_ready = sem("a_g1_ready")
                g_mm = sem("a_g_mm")
                tap_ready = sem("a_tap_ready")
                g_stored = sem("a_g_stored")
                conv_done = sem("a_conv_done")
                stored = sem("a_stored")
                block = st.enter_context(nc.Block())

                @block.vector
                def _(dve):
                    with dve.Fori(0, NQ) as i:
                        ln_stats(dve, stats, mv, rstd, QT, i, var_ready)
                        dve.wait_ge(rstd_ready, i + 1)
                        ln_apply(dve, xn, mv, rstd, QT, i).then_inc(xn_ready, 1)
                        dve.wait_ge(tap_ready, i + 1)
                        for back in range(1, TAPS):
                            for z, w in enumerate(("conv_k", "conv_q", "conv_v")):
                                src = ps[:, 1 + z, :].rearrange("p (s l) -> p s l", s=SQ)[:, :, 0:L - back]
                                dst = cv[:, z, :, back:L]
                                last = dve.scalar_tensor_tensor(dst, src, W(w)[:, TAPS - 1 - back:TAPS - back], dst,
                                                                ALU.mult, ALU.add)
                            if back < TAPS - 1:
                                dve.drain()
                        last.then_inc(conv_done, 1)

                @block.gpsimd
                def _(pool):
                    pool.memset(neghalf[:, :], -0.5)
                    pool.drain()
                    with pool.Fori(0, NQ) as i:
                        pool.wait_ge(var_ready, i + 1)
                        ln_rstd(pool, rstd, neghalf, QT).then_inc(rstd_ready, 1)

                @block.tensor
                def _(pe):
                    pe.sem_inc(conv_done, 1)
                    with pe.Fori(0, NQ) as i:
                        pe.wait_ge(xn_ready, i + 1)
                        for j in range(QT):
                            last = pe.transpose(ps[:, 0, j * P:(j + 1) * P], xn[:, j, :], ident)
                        last.then_inc(turned, 1)
                        pe.wait_ge(xT_ready, i + 1)
                        pe.matmul(ps[0:RANK, 4, :], W("wg1"), xT[:, :], start=True, stop=True).then_inc(projected, 1)
                        pe.wait_ge(conv_done, i + 1)
                        for z, w in enumerate(("wk", "wq", "wv")):
                            pe.matmul(ps[:, 1 + z, :], W(w), xT[:, :], start=True, stop=True).then_inc(projected, 1)
                        pe.wait_ge(g1_ready, i + 1)
                        pe.matmul(ps[:, 5, :], W("wg2", RANK), g1[:, :], start=True, stop=True).then_inc(g_mm, 1)

                @block.scalar
                def _(act):
                    act.preload_act_table(ACT.Silu)
                    with act.Fori(0, NQ) as i:
                        act.wait_ge(turned, i + 1)
                        act.copy(xT[:, :], ps[:, 0, :]).then_inc(xT_ready, 1)
                        act.wait_ge(projected, i * 4 + 1)
                        act.copy(g1[:, :], ps[0:RANK, 4, :]).then_inc(g1_ready, 1)
                        act.wait_ge(projected, i * 4 + 4)
                        for z, w in enumerate(("conv_k", "conv_q", "conv_v")):
                            last = act.activation(cv[:, z], ps[:, 1 + z, :].rearrange("p (s l) -> p s l", s=SQ),
                                                  ACT.Copy, scale=W(w)[:, TAPS - 1:TAPS])
                        last.then_inc(tap_ready, 1)
                        act.wait_ge(g_mm, i + 1)
                        act.activation(gT[:, ds(i * QN, QN)], ps[:, 5, :], ACT.Identity, bias=W("bg2"))
                        act.wait_ge(conv_done, i + 2)
                        for z, dst in enumerate((kT, qT, vT)):
                            act.activation(dst[:, ds(i * QN, QN)], cv[:, z].rearrange("p s l -> p (s l)"), ACT.Silu)

        def gla_chunks(kT, qT, vT, gT):
            with ExitStack() as st:
                v_in = sb("c_v_in", [P, QN], F32, st)
                mag = sb("c_mag", [P, QN], F32, st)
                soft = sb("c_soft", [P, QN], F32, st)
                logsig = sb("c_logsig", [P, QN], F32, st)
                cum = sb("c_cum", [P, QN], F32, st)
                up = sb("c_up", [P, QN], F32, st)
                down = sb("c_down", [P, QN], F32, st)
                sq = sb("c_sq", [P, 2, QN], F32, st)
                qe = sb("c_qe", [P, QN], F32, st)
                ke = sb("c_ke", [P, QN], F32, st)
                norms = sb("c_norms", [P, 2 * QT], F32, st)
                inv = sb("c_inv", [P, 2 * QT], F32, st)
                half = sb("c_half", [P, 2 * QT], F32, st)
                neghalf = sb("c_neghalf", [P, QT], F32, st)
                v_tok = sb("c_v_tok", [P, QT, D], F32, st)
                ke_tok = sb("c_ke_tok", [P, QT, D], F32, st)
                wT = sb("c_wT", [P, QT, P], F32, st)
                state = sb("c_state", [P, NC_SEQ - 1, SQ, D], F32, st)
                oT = sb("c_oT", [P, QN], F32, st)
                osq = sb("c_osq", [P, QN], F32, st)
                ms = sb("c_ms", [P, QT], F32, st)
                fac = sb("c_fac", [P, QT], F32, st)
                v_copied = sem("c_v_copied")
                soft_ready = sem("c_soft_ready")
                cum_ready = sem("c_cum_ready")
                exps_ready = sem("c_exps_ready")
                sq_ready = sem("c_sq_ready")
                qk_ready = sem("c_qk_ready")
                norm_mm = sem("c_norm_mm")
                norms_out = sem("c_norms_out")
                root_ready = sem("c_root_ready")
                v_turned = sem("c_v_turned")
                ke_turned = sem("c_ke_turned")
                v_ready = sem("c_v_ready")
                ke_ready = sem("c_ke_ready")
                w_ready = sem("c_w_ready")
                outer_mm = sem("c_outer_mm")
                state_ready = sem("c_state_ready")
                o_mm = sem("c_o_mm")
                o_ready = sem("c_o_ready")
                ss_mm = sem("c_ss_mm")
                ms_ready = sem("c_ms_ready")
                fac_ready = sem("c_fac_ready")
                out_mm = sem("c_out_mm")
                h_done = sem("c_h_done")
                block = st.enter_context(nc.Block())

                @block.gpsimd
                def _(pool):
                    pool.memset(half[:, :], 0.5)
                    pool.memset(neghalf[:, :], -0.5)
                    pool.drain()
                    pool.sem_inc(h_done, 1)
                    with pool.Fori(0, NQ) as i:
                        pool.wait_ge(h_done, i + 1)
                        pool.tensor_copy(v_in[:, :], vT[:, ds(i * QN, QN)]).then_inc(v_copied, 1)
                        pool.wait_ge(norms_out, i + 1)
                        pool.tensor_tensor(norms[:, :], norms[:, :], half[:, :], ALU.pow)
                        pool.drain()
                        pool.tensor_scalar(norms[:, :], norms[:, :], 1e-5, None, ALU.add).then_inc(root_ready, 1)
                        pool.wait_ge(ms_ready, i + 1)
                        pool.tensor_tensor(ms[:, :], ms[:, :], neghalf[:, :], ALU.pow).then_inc(fac_ready, 1)

                @block.scalar
                def _(act):
                    act.preload_act_table(ACT.Ln)
                    with act.Fori(0, NQ) as i:
                        act.wait_ge(h_done, i + 1)
                        act.activation(mag[:, :], gT[:, ds(i * QN, QN)], ACT.Abs)
                        act.drain()
                        act.activation(soft[:, :], mag[:, :], ACT.Exp, scale=-1.0)
                        act.drain()
                        act.activation(soft[:, :], soft[:, :], ACT.Ln, bias=1.0).then_inc(soft_ready, 1)
                        act.activation(sq[:, 0, :], kT[:, ds(i * QN, QN)], ACT.Square)
                        act.activation(sq[:, 1, :], qT[:, ds(i * QN, QN)], ACT.Square).then_inc(sq_ready, 1)
                        act.wait_ge(cum_ready, i + 1)
                        act.activation(down[:, :], cum[:, :], ACT.Exp, scale=1.0 / GATE_NORM)
                        act.activation(up[:, :], cum[:, :], ACT.Exp, scale=-1.0 / GATE_NORM).then_inc(exps_ready, 1)
                        act.wait_ge(ke_turned, i + 1)
                        act.copy(ke_tok[:, :, :].rearrange("p t d -> p (t d)"), ps[:, 2, :]).then_inc(ke_ready, 1)
                        act.wait_ge(o_mm, i + 1)
                        act.activation(osq[:, :], ps[:, 6, :], ACT.Square)
                        act.activation(oT[:, :], ps[:, 6, :], ACT.Copy, scale=W("norm_w")).then_inc(o_ready, 1)

                @block.vector
                def _(dve):
                    dve.memset(wT[:, :, :], 0.0)
                    dve.drain()
                    with dve.Fori(0, NQ) as i:
                        dve.wait_ge(soft_ready, i + 1)
                        dve.scalar_tensor_tensor(logsig[:, :], gT[:, ds(i * QN, QN)], 0.0, soft[:, :],
                                                 ALU.min, ALU.subtract)
                        dve.drain()
                        dve.tensor_tensor_scan(cum[:, :], C("reset"), logsig[:, :], 0.0, ALU.mult,
                                               ALU.add).then_inc(cum_ready, 1)
                        dve.wait_ge(norm_mm, i + 1)
                        dve.tensor_copy(norms[:, :], ps[:, 0, 0:2 * QT]).then_inc(norms_out, 1)
                        dve.wait_ge(exps_ready, i + 1)
                        dve.tensor_tensor(ke[:, :], kT[:, ds(i * QN, QN)], up[:, :], ALU.mult)
                        dve.tensor_tensor(qe[:, :], qT[:, ds(i * QN, QN)], down[:, :], ALU.mult).then_inc(qk_ready, 1)
                        dve.wait_ge(root_ready, i + 1)
                        dve.reciprocal(inv[:, :], norms[:, :])
                        dve.drain()
                        dve.wait_ge(v_turned, i + 1)
                        for j in range(QT):
                            last = dve.tensor_scalar(v_tok[:, j, :], ps[:, 1, j * D:(j + 1) * D], inv[:, j:j + 1],
                                                     None, ALU.mult)
                        last.then_inc(v_ready, 1)
                        dve.wait_ge(outer_mm, i + 1)
                        ends = down[:, :].rearrange("p (s c l) -> p s c l", s=SQ, c=NC_SEQ)
                        for c in range(NC_SEQ - 1):
                            if c % 2 == 0:
                                prod = ps[:, 4, :].rearrange("p (s c d) -> p s c d", s=SQ, c=2)[:, :, c // 2, :]
                            else:
                                prod = ps[:, 5, 0:SQ * D].rearrange("p (s d) -> p s d", s=SQ)
                            end = ends[:, :, c, CHUNK - 1:CHUNK].to_broadcast([P, SQ, D])
                            if c == 0:
                                dve.tensor_tensor(state[:, c], prod, end, ALU.mult)
                                dve.copy_predicated(wT[:, :, :],
                                                    causal_sb[:, :].unsqueeze(1).to_broadcast([P, QT, P]),
                                                    ps[:, 3, :].rearrange("p (t q) -> p t q", t=QT)
                                                    ).then_inc(w_ready, 1)
                            else:
                                dve.drain()
                                dve.tensor_tensor(state[:, c], state[:, c - 1], prod, ALU.add)
                                dve.drain()
                                last = dve.tensor_tensor(state[:, c], state[:, c], end, ALU.mult)
                        last.then_inc(state_ready, 1)
                        dve.wait_ge(ss_mm, i + 1)
                        dve.tensor_tensor(fac[:, :], inv[:, QT:2 * QT], inv[:, QT:2 * QT], ALU.mult)
                        dve.drain()
                        dve.tensor_tensor(ms[:, :], ps[:, 0, 2 * QT:3 * QT], fac[:, :], ALU.mult)
                        dve.drain()
                        dve.tensor_scalar(ms[:, :], ms[:, :], 1.0 / D, 1e-6, ALU.mult, ALU.add).then_inc(ms_ready, 1)
                        dve.wait_ge(fac_ready, i + 1)
                        dve.tensor_tensor(fac[:, :], ms[:, :], inv[:, QT:2 * QT], ALU.mult)
                        dve.drain()
                        dve.wait_ge(out_mm, i + 1)
                        for j in range(QT):
                            hj = h[:, ds(i * QT + j, 1), :].rearrange("p t d -> p (t d)")
                            last = dve.scalar_tensor_tensor(hj, ps[:, 7, j * D:(j + 1) * D], fac[:, j:j + 1], hj,
                                                            ALU.mult, ALU.add)
                        last.then_inc(h_done, 1)

                @block.tensor
                def _(pe):
                    with pe.Fori(0, NQ) as i:
                        pe.wait_ge(v_copied, i + 1)
                        for j in range(QT):
                            last = pe.transpose(ps[:, 1, j * P:(j + 1) * P], v_in[:, j * P:(j + 1) * P], ident)
                        last.then_inc(v_turned, 1)
                        pe.wait_ge(sq_ready, i + 1)
                        for z in range(2):
                            for j in range(QT):
                                last = pe.matmul(ps[:, 0, z * QT + j:z * QT + j + 1], sq[:, z, j * P:(j + 1) * P],
                                                 ones_col, start=True, stop=True)
                        last.then_inc(norm_mm, 1)
                        pe.wait_ge(qk_ready, i + 1)
                        for j in range(QT):
                            last = pe.transpose(ps[:, 2, j * P:(j + 1) * P], ke[:, j * P:(j + 1) * P], ident)
                        last.then_inc(ke_turned, 1)
                        for j in range(QT):
                            last = pe.matmul(ps[:, 3, j * P:(j + 1) * P], ke[:, j * P:(j + 1) * P],
                                             qe[:, j * P:(j + 1) * P], start=True, stop=True)
                        pe.wait_ge(ke_ready, i + 1)
                        pe.wait_ge(v_ready, i + 1)
                        for s in range(SQ):
                            for c in range(NC_SEQ - 1):
                                rows = slice(CHUNK * (c % 2), CHUNK * (c % 2) + CHUNK)
                                tile = 2 * s + c // 2
                                at = (2 * s + c // 2) * D if c % 2 == 0 else s * D
                                last = pe.matmul(ps[:, 4 + c % 2, at:at + D], ke_tok[rows, tile, :],
                                                 v_tok[rows, tile, :], start=True, stop=True)
                        last.then_inc(outer_mm, 1)
                        pe.wait_ge(w_ready, i + 1)
                        pe.wait_ge(state_ready, i + 1)
                        for j in range(QT):
                            s = j // 2
                            pe.matmul(ps[:, 6, j * P:(j + 1) * P], v_tok[:, j, :], wT[:, j, :], start=True,
                                      stop=False, skip_group_check=True)
                            for half_ in range(2):
                                c = 2 * (j % 2) + half_
                                if c:
                                    at = j * P + half_ * CHUNK
                                    last = pe.matmul(ps[:, 6, at:at + CHUNK], state[:, c - 1, s, :],
                                                     qe[:, at:at + CHUNK], start=False, stop=True,
                                                     skip_group_check=True)
                        last.then_inc(o_mm, 1)
                        pe.wait_ge(o_ready, i + 1)
                        for j in range(QT):
                            last = pe.matmul(ps[:, 0, 2 * QT + j:2 * QT + j + 1], osq[:, j * P:(j + 1) * P], ones_col,
                                             start=True, stop=True)
                        last.then_inc(ss_mm, 1)
                        for j in range(QT):
                            last = pe.matmul(ps[:, 7, j * D:(j + 1) * D], oT[:, j * P:(j + 1) * P], W("wo0"),
                                             start=True, stop=True)
                        last.then_inc(out_mm, 1)

        def moe0_stage():
            with ExitStack() as st:
                xT = sb("m_xT", [P, N], F32, st)
                gates = sb("m_gates", [P, T, E0], F32, st)
                ring = sb("m_ring", [P, 2, W0COLS], F32, st)
                slot_in = [sem("m_slot_in0"), sem("m_slot_in1")]
                slot_free = sem("m_slot_free")
                moe0_router(xT, gates)
                moe0_experts(xT, gates, ring, slot_in, slot_free)

        def moe0_router(xT, gates):
            with ExitStack() as st:
                stats = sb("r_stats", [P, QT, 6], F32, st)
                mv = sb("r_mv", [P, QT, 2], F32, st)
                rstd = sb("r_rstd", [P, QT], F32, st)
                neghalf = sb("r_neghalf", [P, QT], F32, st)
                xn = sb("r_xn", [P, QT, D], F32, st)
                xs = sb("r_xs", [P, QN], F32, st)
                logits = sb("r_logits", [P, QT, E0], F32, st)
                top = sb("r_top", [P, QT, 8], F32, st)
                topi = sb("r_topi", [P, QT, 8], U32, st)
                topf = sb("r_topf", [P, QT, 8], F32, st)
                gap = sb("r_gap", [P, QT], F32, st)
                ex = sb("r_ex", [P, QT], F32, st)
                den = sb("r_den", [P, QT], F32, st)
                wts = sb("r_wts", [P, 2, QT], F32, st)
                g2 = sb("r_g2", [P, 2, QT, E0], F32, st)
                gq = sb("r_gq", [P, QT, E0], F32, st)
                gqT = sb("r_gqT", [E0, QN], F32, st)
                var_ready = sem("r_var_ready")
                rstd_ready = sem("r_rstd_ready")
                xn_ready = sem("r_xn_ready")
                turned = sem("r_turned")
                xs_ready = sem("r_xs_ready")
                xT_stored = sem("r_xT_stored")
                logit_mm = sem("r_logit_mm")
                gap_ready = sem("r_gap_ready")
                ex_ready = sem("r_ex_ready")
                gq_ready = sem("r_gq_ready")
                g_turned = sem("r_g_turned")
                gT_ready = sem("r_gT_ready")
                bias_mm = sem("r_bias_mm")
                h_done = sem("r_h_done")
                block = st.enter_context(nc.Block())

                @block.vector
                def _(dve):
                    dve.sem_inc(h_done, 1)
                    with dve.Fori(0, NQ) as i:
                        ln_stats(dve, stats, mv, rstd, QT, i, var_ready)
                        dve.wait_ge(rstd_ready, i + 1)
                        ln_apply(dve, xn, mv, rstd, QT, i).then_inc(xn_ready, 1)
                        dve.wait_ge(logit_mm, i + 1)
                        dve.tensor_copy(logits[:, :, :], ps[:, 1, 0:QT * E0].rearrange("p (t e) -> p t e", t=QT))
                        dve.drain()
                        for j in range(QT):
                            dve.max(top[:, j, :], logits[:, j, :])
                        dve.drain()
                        for j in range(QT):
                            dve.max_index(topi[:, j, :], top[:, j, :], logits[:, j, :])
                        dve.tensor_tensor(gap[:, :], top[:, :, 1], top[:, :, 0], ALU.subtract).then_inc(gap_ready, 1)
                        dve.drain()
                        dve.tensor_copy(topf[:, :, :], topi[:, :, :])
                        dve.wait_ge(ex_ready, i + 1)
                        dve.tensor_scalar(den[:, :], ex[:, :], 1.0, None, ALU.add)
                        dve.drain()
                        dve.reciprocal(wts[:, 0, :], den[:, :])
                        dve.drain()
                        dve.tensor_tensor(wts[:, 1, :], wts[:, 0, :], ex[:, :], ALU.mult)
                        dve.drain()
                        for k in range(2):
                            for j in range(QT):
                                dve.tensor_scalar(g2[:, k, j, :], C("iota")[:, 0:E0], topf[:, j, k:k + 1],
                                                  wts[:, k, j:j + 1], ALU.is_equal, ALU.mult)
                        dve.drain()
                        dve.tensor_tensor(gq[:, :, :], g2[:, 0], g2[:, 1], ALU.add).then_inc(gq_ready, 1)
                        dve.drain()
                        dve.tensor_copy(gates[:, ds(i * QT, QT), :], gq[:, :, :])
                        dve.wait_ge(bias_mm, i + 1)
                        dve.tensor_tensor(h[:, ds(i * QT, QT), :], h[:, ds(i * QT, QT), :],
                                          ps[:, 3, :].rearrange("p (t d) -> p t d", t=QT), ALU.add).then_inc(h_done, 1)

                @block.gpsimd
                def _(pool):
                    pool.memset(neghalf[:, :], -0.5)
                    pool.drain()
                    with pool.Fori(0, NQ) as i:
                        pool.wait_ge(var_ready, i + 1)
                        ln_rstd(pool, rstd, neghalf, QT).then_inc(rstd_ready, 1)
                        pool.wait_ge(xs_ready, i + 1)
                        pool.tensor_copy(xT[:, ds(i * QN, QN)], xs[:, :]).then_inc(xT_stored, 1)

                @block.scalar
                def _(act):
                    act.preload_act_table(ACT.Exp)
                    act.sem_inc(xT_stored, 1)
                    with act.Fori(0, NQ) as i:
                        act.wait_ge(xT_stored, i + 1)
                        act.wait_ge(turned, i + 1)
                        act.copy(xs[:, :], ps[:, 0, :]).then_inc(xs_ready, 1)
                        act.wait_ge(gap_ready, i + 1)
                        act.activation(ex[:, :], gap[:, :], ACT.Exp).then_inc(ex_ready, 1)
                        act.wait_ge(g_turned, i + 1)
                        act.copy(gqT[:, :], ps[0:E0, 2, :]).then_inc(gT_ready, 1)

                @block.tensor
                def _(pe):
                    with pe.Fori(0, NQ) as i:
                        pe.wait_ge(h_done, i + 1)
                        pe.wait_ge(xn_ready, i + 1)
                        for j in range(QT):
                            last = pe.transpose(ps[:, 0, j * P:(j + 1) * P], xn[:, j, :], ident)
                        last.then_inc(turned, 1)
                        pe.wait_ge(xs_ready, i + 1)
                        for j in range(QT):
                            pe.matmul(ps[:, 1, j * E0:(j + 1) * E0], xs[:, j * P:(j + 1) * P], W("rw0"), start=True,
                                      stop=False)
                            last = pe.matmul(ps[:, 1, j * E0:(j + 1) * E0], ones_row, W("rb0", 1), start=False,
                                             stop=True)
                        last.then_inc(logit_mm, 1)
                        pe.wait_ge(gq_ready, i + 1)
                        for j in range(QT):
                            last = pe.transpose(ps[0:E0, 2, j * P:(j + 1) * P], gq[:, j, :], ident)
                        last.then_inc(g_turned, 1)
                        pe.wait_ge(gT_ready, i + 1)
                        for j in range(QT):
                            last = pe.matmul(ps[:, 3, j * D:(j + 1) * D], gqT[:, j * P:(j + 1) * P], W("fc2_b", E0),
                                             start=True, stop=True)
                        last.then_inc(bias_mm, 1)

        def moe0_experts(xT, gates, ring, slot_in, slot_free):
            with ExitStack() as st:
                act1 = sb("x_act1", [P, 2, QN], F32, st)
                a = sb("x_a", [P, 2, 2, QN], F32, st)
                hid_mm = sem("x_hid_mm")
                silu_done = sem("x_silu_done")
                a_ready = sem("x_a_ready")
                y_mm = sem("x_y_mm")
                y_used = sem("x_y_used")
                STEPS = 2 * NQ
                block = st.enter_context(nc.Block())

                @block.sync
                def _(sp):
                    sp.sem_inc(slot_free, 2)
                    with sp.Fori(0, E0 // 2) as pair:
                        e = pair * 2
                        for s in range(2):
                            sp.wait_ge(slot_free, e + s + 1)
                            sp.dma_start(ring[:, s, :], w0[:, ds(e + s, 1), :]).then_inc(slot_in[s], 16)

                def w1_of(s, part, f):
                    o = part * F0 + f * P
                    return ring[:, s, o:o + P]

                def bias_of(s, part, f):
                    o = 2 * F0 + 2 * D + part * 2 + f
                    return ring[:, s, o:o + 1]

                @block.tensor
                def _(pe):
                    pe.sem_inc(a_ready, 2)
                    pe.sem_inc(y_mm, 2)
                    pe.sem_inc(y_used, 2)

                    def hidden(e, n):
                        s, c = n // NQ, n % NQ
                        if c == 0:
                            pe.wait_ge(slot_in[s], e * 8 + 16)
                        for f in range(2):
                            pe.wait_ge(a_ready, e * (2 * NQ) + 2 * n + f + 1)
                            for part in range(2):
                                last = pe.matmul(ps[:, 2 * f + part, :], w1_of(s, part, f),
                                                 xT[:, c * QN:(c + 1) * QN], start=True, stop=True)
                            last.then_inc(hid_mm, 1)

                    def output(e, n):
                        s = n // NQ
                        pe.wait_ge(a_ready, e * (2 * NQ) + 2 * n + 4)
                        pe.wait_ge(y_used, e * NQ + n + 1)
                        for j in range(QT):
                            for f in range(2):
                                o = 2 * F0 + f * D
                                last = pe.matmul(ps[:, 4 + n % 2, j * D:(j + 1) * D], a[:, n % 2, f, j * P:(j + 1) * P],
                                                 ring[:, s, o:o + D], start=(f == 0), stop=(f == 1))
                        last.then_inc(y_mm, 1)

                    with pe.Fori(0, E0 // 2) as pair:
                        e = pair * 2
                        for n in range(STEPS):
                            hidden(e, n)
                            if n:
                                output(e, n - 1)
                        output(e, STEPS - 1)

                @block.scalar
                def _(act):
                    act.preload_act_table(ACT.Silu)
                    with act.Fori(0, E0 // 2) as pair:
                        e = pair * 2
                        for n in range(STEPS):
                            s = n // NQ
                            for f in range(2):
                                act.wait_ge(hid_mm, e * (2 * NQ) + 2 * n + f + 1)
                                act.wait_ge(a_ready, e * (2 * NQ) + 2 * n + f + 1)
                                act.activation(act1[:, f, :], ps[:, 2 * f, :], ACT.Silu,
                                               bias=bias_of(s, 0, f)).then_inc(silu_done, 1)

                @block.vector
                def _(dve):
                    def combine(e, n):
                        dve.wait_ge(y_mm, e * NQ + n + 3)
                        s, c = n // NQ, n % NQ
                        for j in range(QT):
                            t = c * QT + j
                            last = dve.scalar_tensor_tensor(h[:, t, :], ps[:, 4 + n % 2, j * D:(j + 1) * D],
                                                            gates[:, t, ds(e + s, 1)], h[:, t, :], ALU.mult, ALU.add)
                        last.then_inc(y_used, 1)
                        if c == NQ - 1:
                            dve.sem_inc(slot_free, 1)

                    with dve.Fori(0, E0 // 2) as pair:
                        e = pair * 2
                        for n in range(STEPS):
                            s = n // NQ
                            dve.wait_ge(y_mm, e * NQ + n + 1)
                            for f in range(2):
                                dve.wait_ge(silu_done, e * (2 * NQ) + 2 * n + f + 1)
                                dve.scalar_tensor_tensor(a[:, n % 2, f, :], ps[:, 2 * f + 1, :], bias_of(s, 1, f),
                                                         act1[:, f, :], ALU.add, ALU.mult).then_inc(a_ready, 1)
                            if n:
                                combine(e, n - 1)
                        combine(e, STEPS - 1)

        def attention_stage():
            with ExitStack() as st:
                AT = 2
                stats = sb("w_stats", [P, AT, 6], F32, st)
                mv = sb("w_mv", [P, AT, 2], F32, st)
                rstd = sb("w_rstd", [P, AT], F32, st)
                neghalf = sb("w_neghalf", [P, AT], F32, st)
                xn = sb("w_xn", [P, AT, D], F32, st)
                xs = sb("w_xs", [P, L], F32, st)
                bq4 = sb("w_bq4", [P, 2], F32, st)
                qs = sb("w_qs", [P, 2, L], F32, st)
                ks = sb("w_ks", [P, 2, L], F32, st)
                vs = sb("w_vs", [P, AT, D], F32, st)
                sc = sb("w_sc", [P, 2, 2, KW], F32, st)
                mx = sb("w_mx", [P, AT, 2, 4], F32, st)
                nm = sb("w_nm", [P, AT, 2, 4], F32, st)
                rs = sb("w_rs", [P, AT, 2, 4], F32, st)
                pr = sb("w_pr", [P, AT, HEADS, L], F32, st)
                pT = sb("w_pT", [P, 2, 2, 2, P], F32, st)
                rr = sb("w_rr", [P, AT, 2, 4], F32, st)
                cx = sb("w_cx", [P, AT, D], F32, st)
                cxT = sb("w_cxT", [P, L], F32, st)
                var_ready = sem("w_var_ready")
                rstd_ready = sem("w_rstd_ready")
                xn_ready = sem("w_xn_ready")
                turned = sem("w_turned")
                xs_ready = sem("w_xs_ready")
                proj_mm = sem("w_proj_mm")
                qk_ready = sem("w_qk_ready")
                v_ready = sem("w_v_ready")
                score_mm = sem("w_score_mm")
                score_used = sem("w_score_used")
                nm_ready = sem("w_nm_ready")
                exp_done = sem("w_exp_done")
                p_turned = sem("w_p_turned")
                pT_ready = sem("w_pT_ready")
                pv_mm = sem("w_pv_mm")
                cx_ready = sem("w_cx_ready")
                cx_turned = sem("w_cx_turned")
                cxT_ready = sem("w_cxT_ready")
                out_mm = sem("w_out_mm")
                h_done = sem("w_h_done")
                zeroed = sem("w_zeroed")
                UNITS = [(tile, s) for tile in range(AT) for s in range(4)]
                NU = len(UNITS)
                block = st.enter_context(nc.Block())

                def key_cols(tile):
                    return (0, P, WIN) if tile == 0 else (WIN, L, 0)

                @block.gpsimd
                def _(pool):
                    pool.memset(neghalf[:, :], -0.5)
                    pool.memset(pr[:, :, :, :], 0.0).then_inc(zeroed, 1)
                    pool.drain()
                    with pool.Fori(0, B) as i:
                        pool.wait_ge(var_ready, i + 1)
                        ln_rstd(pool, rstd, neghalf, AT).then_inc(rstd_ready, 1)

                def copy_pT(dve, i, n):
                    nb = UNITS[n][0] + 1
                    dve.wait_ge(p_turned, i * NU + n + 1)
                    if n >= 2:
                        dve.wait_ge(pv_mm, i * NU + n - 1)
                    dve.tensor_copy(pT[:, n % 2, 0:nb].rearrange("p b g q -> p (b g q)"),
                                    ps[:, 5 + n % 2, 0:nb * 2 * P]).then_inc(pT_ready, 1)

                @block.vector
                def _(dve):
                    dve.wait_ge(band_made, 16)
                    dve.tensor_scalar(bq4[:, :], W("abq"), 0.25, None, ALU.mult)
                    dve.drain().then_inc(zeroed, 1)
                    dve.sem_inc(h_done, 1)
                    with dve.Fori(0, B) as i:
                        ln_stats(dve, stats, mv, rstd, AT, i, var_ready)
                        dve.wait_ge(rstd_ready, i + 1)
                        ln_apply(dve, xn, mv, rstd, AT, i).then_inc(xn_ready, 1)
                        dve.wait_ge(proj_mm, i * 3 + 3)
                        dve.tensor_copy(vs[:, :, :], ps[:, 7, 0:L].rearrange("p (t d) -> p t d", t=AT)
                                        ).then_inc(v_ready, 1)
                        for n, (tile, s) in enumerate(UNITS):
                            lo, hi, b0 = key_cols(tile)
                            w = hi - lo
                            dve.wait_ge(score_mm, i * NU + n + 1)
                            if n >= 2:
                                dve.wait_ge(exp_done, i * NU + n - 1)
                            dve.memset(carrier[:, :], 0.0)
                            for g in range(2):
                                last = dve.tensor_tensor_reduce(sc[:, n % 2, g, 0:w], ps[:, s, 256 * g:256 * g + w],
                                                                band[:, 4 * g + s, b0:b0 + w], 1.0, NEG, ALU.add,
                                                                ALU.max, mx[:, tile, g, s:s + 1])
                            last.then_inc(score_used, 1)
                            dve.drain()
                            dve.tensor_scalar(nm[:, tile, :, s], mx[:, tile, :, s], -1.0, None,
                                              ALU.mult).then_inc(nm_ready, 1)
                            if n:
                                copy_pT(dve, i, n - 1)
                        copy_pT(dve, i, NU - 1)
                        dve.wait_ge(exp_done, i * NU + NU)
                        dve.reciprocal(rr[:, :, :, :], rs[:, :, :, :])
                        dve.drain()
                        dve.wait_ge(pv_mm, i * NU + NU)
                        dve.tensor_tensor(cx[:, :, :].rearrange("p t (h d) -> p (t h) d", h=HEADS),
                                          ps[:, 7, L:2 * L].rearrange("p (t d) -> p t d", d=DH),
                                          rr[:, :, :, :].rearrange("p t g s -> p (t g s)").unsqueeze(2)
                                          .to_broadcast([P, AT * HEADS, DH]), ALU.mult).then_inc(cx_ready, 1)
                        dve.wait_ge(out_mm, i + 1)
                        dve.tensor_tensor(h[:, ds(i * AT, AT), :], h[:, ds(i * AT, AT), :],
                                          ps[:, 4, L:2 * L].rearrange("p (t d) -> p t d", t=AT), ALU.add
                                          ).then_inc(h_done, 1)

                @block.scalar
                def _(act):
                    act.preload_act_table(ACT.Exp)
                    act.wait_ge(zeroed, 2)
                    with act.Fori(0, B) as i:
                        act.wait_ge(turned, i + 1)
                        act.copy(xs[:, :], ps[:, 4, 0:L]).then_inc(xs_ready, 1)
                        act.wait_ge(proj_mm, i * 3 + 2)
                        for g in range(2):
                            act.activation(qs[:, g, :], ps[:, 5, g * L:(g + 1) * L], ACT.Identity, scale=0.25,
                                           bias=bq4[:, g:g + 1])
                            last = act.activation(ks[:, g, :], ps[:, 6, g * L:(g + 1) * L], ACT.Identity,
                                                  bias=W("abk")[:, g:g + 1])
                        last.then_inc(qk_ready, 1)
                        for n, (tile, s) in enumerate(UNITS):
                            lo, hi, b0 = key_cols(tile)
                            act.wait_ge(nm_ready, i * NU + n + 1)
                            for g in range(2):
                                last = act.activation(pr[:, tile, 4 * g + s, lo:hi], sc[:, n % 2, g, 0:hi - lo],
                                                      ACT.Exp, bias=nm[:, tile, g, s:s + 1],
                                                      accum_out=rs[:, tile, g, s:s + 1])
                            last.then_inc(exp_done, 1)
                        act.wait_ge(cx_turned, i + 1)
                        act.copy(cxT[:, :], ps[:, 4, 0:L]).then_inc(cxT_ready, 1)

                @block.tensor
                def _(pe):
                    pe.sem_inc(score_used, 4)

                    def scores(i, n):
                        tile, s = UNITS[n]
                        lo, hi, b0 = key_cols(tile)
                        rows = slice(32 * s, 32 * s + DH)
                        pe.wait_ge(score_used, i * NU + n + 1)
                        for g in range(2):
                            last = pe.matmul(ps[:, s, 256 * g:256 * g + hi - lo], qs[rows, g, tile * P:(tile + 1) * P],
                                             ks[rows, g, lo:hi], start=True, stop=True)
                        last.then_inc(score_mm, 1)

                    def turn(i, n):
                        tile, s = UNITS[n]
                        pe.wait_ge(exp_done, i * NU + n + 1)
                        if n >= 2:
                            pe.wait_ge(pT_ready, i * NU + n - 1)
                        for b in range(tile + 1):
                            for g in range(2):
                                at = (2 * b + g) * P
                                last = pe.transpose(ps[:, 5 + n % 2, at:at + P],
                                                    pr[:, tile, 4 * g + s, b * P:(b + 1) * P], ident)
                        last.then_inc(p_turned, 1)

                    def weigh(i, n):
                        tile, s = UNITS[n]
                        pe.wait_ge(pT_ready, i * NU + n + 1)
                        for g in range(2):
                            hd = 4 * g + s
                            at = L + tile * D + hd * DH
                            for b in range(tile + 1):
                                last = pe.matmul(ps[:, 7, at:at + DH], pT[:, n % 2, b, g, :],
                                                 vs[:, b, hd * DH:(hd + 1) * DH], start=(b == 0), stop=(b == tile))
                        last.then_inc(pv_mm, 1)

                    pe.wait_ge(zeroed, 2)
                    with pe.Fori(0, B) as i:
                        pe.wait_ge(xn_ready, i + 1)
                        pe.wait_ge(h_done, i + 1)
                        for j in range(AT):
                            last = pe.transpose(ps[:, 4, j * P:(j + 1) * P], xn[:, j, :], ident)
                        last.then_inc(turned, 1)
                        pe.wait_ge(xs_ready, i + 1)
                        for b, w in ((5, "aq"), (6, "ak")):
                            for g in range(2):
                                last = pe.matmul(ps[:, b, g * L:(g + 1) * L], W(w)[:, g * P:(g + 1) * P], xs[:, :],
                                                 start=True, stop=True)
                            last.then_inc(proj_mm, 1)
                        for j in range(AT):
                            pe.matmul(ps[:, 7, j * D:(j + 1) * D], xs[:, j * P:(j + 1) * P], W("av"), start=True,
                                      stop=False)
                            last = pe.matmul(ps[:, 7, j * D:(j + 1) * D], ones_row, W("abv", 1), start=False, stop=True)
                        last.then_inc(proj_mm, 1)
                        pe.wait_ge(qk_ready, i + 1)
                        pe.wait_ge(v_ready, i + 1)
                        for n in range(3):
                            scores(i, n)
                        for n in range(NU):
                            if n + 3 < NU:
                                scores(i, n + 3)
                            turn(i, n)
                            if n:
                                weigh(i, n - 1)
                        weigh(i, NU - 1)
                        pe.wait_ge(cx_ready, i + 1)
                        for j in range(AT):
                            last = pe.transpose(ps[:, 4, j * P:(j + 1) * P], cx[:, j, :], ident)
                        last.then_inc(cx_turned, 1)
                        pe.wait_ge(cxT_ready, i + 1)
                        for j in range(AT):
                            at = L + j * D
                            pe.matmul(ps[:, 4, at:at + D], cxT[:, j * P:(j + 1) * P], W("awo"), start=True, stop=False)
                            last = pe.matmul(ps[:, 4, at:at + D], ones_row, W("abo", 1), start=False, stop=True)
                        last.then_inc(out_mm, 1)

        def moe1_stage():
            with ExitStack() as st:
                xT = sb("n_xT", [P, N], F32, st)
                gates = sb("n_gates", [P, T, EXP1], F32, st)
                ring = sb("n_ring", [P, 2, W1COLS], F32, st)
                slot_in = [sem("n_slot_in0"), sem("n_slot_in1")]
                slot_free = sem("n_slot_free")
                moe1_router(xT, gates)
                moe1_experts(xT, gates, ring, slot_in, slot_free)

        def moe1_router(xT, gates):
            with ExitStack() as st:
                stats = sb("s_stats", [P, QT, 6], F32, st)
                mv = sb("s_mv", [P, QT, 2], F32, st)
                rstd = sb("s_rstd", [P, QT], F32, st)
                neghalf = sb("s_neghalf", [P, QT], F32, st)
                xn = sb("s_xn", [P, QT, D], F32, st)
                xs = sb("s_xs", [P, QN], F32, st)
                nmx = sb("s_nmx", [P, QT], F32, st)
                ex = sb("s_ex", [P, QT, E1], F32, st)
                top = sb("s_top", [P, QT, 8], F32, st)
                topi = sb("s_topi", [P, QT, 8], U32, st)
                topf = sb("s_topf", [P, QT, 8], F32, st)
                tot = sb("s_tot", [P, QT], F32, st)
                wts = sb("s_wts", [P, QT, TOPK1], F32, st)
                gk = sb("s_gk", [P, QT, TOPK1, E1], F32, st)
                var_ready = sem("s_var_ready")
                rstd_ready = sem("s_rstd_ready")
                xn_ready = sem("s_xn_ready")
                turned = sem("s_turned")
                xs_ready = sem("s_xs_ready")
                xT_stored = sem("s_xT_stored")
                logit_mm = sem("s_logit_mm")
                nmx_ready = sem("s_nmx_ready")
                ex_ready = sem("s_ex_ready")
                block = st.enter_context(nc.Block())

                @block.vector
                def _(dve):
                    dve.memset(gates[:, :, E1:EXP1], 1.0)
                    with dve.Fori(0, NQ) as i:
                        ln_stats(dve, stats, mv, rstd, QT, i, var_ready)
                        dve.wait_ge(rstd_ready, i + 1)
                        ln_apply(dve, xn, mv, rstd, QT, i).then_inc(xn_ready, 1)
                        dve.drain()
                        dve.tensor_tensor(h[:, ds(i * QT, QT), :], h[:, ds(i * QT, QT), :], xn[:, :, :], ALU.add)
                        dve.wait_ge(logit_mm, i + 1)
                        lg = ps[:, 1, 0:QT * E1].rearrange("p (t e) -> p t e", t=QT)
                        dve.tensor_reduce(nmx[:, :], lg, AX.X, ALU.max)
                        dve.drain()
                        dve.tensor_scalar(nmx[:, :], nmx[:, :], -1.0, None, ALU.mult).then_inc(nmx_ready, 1)
                        dve.wait_ge(ex_ready, i + 1)
                        dve.memset(carrier[:, :], 0.0)
                        for j in range(QT):
                            dve.max(top[:, j, :], ex[:, j, :])
                        dve.drain()
                        for j in range(QT):
                            dve.max_index(topi[:, j, :], top[:, j, :], ex[:, j, :])
                        dve.tensor_reduce(tot[:, :], top[:, :, 0:TOPK1], AX.X, ALU.add)
                        dve.drain()
                        dve.reciprocal(tot[:, :], tot[:, :])
                        dve.tensor_copy(topf[:, :, :], topi[:, :, :])
                        dve.drain()
                        dve.tensor_tensor(wts[:, :, :], top[:, :, 0:TOPK1],
                                          tot[:, :].unsqueeze(2).to_broadcast([P, QT, TOPK1]), ALU.mult)
                        dve.drain()
                        for j in range(QT):
                            for k in range(TOPK1):
                                dve.tensor_scalar(gk[:, j, k, :], C("iota")[:, 0:E1], topf[:, j, k:k + 1],
                                                  wts[:, j, k:k + 1], ALU.is_equal, ALU.mult)
                        dve.drain()
                        dve.tensor_reduce(gates[:, ds(i * QT, QT), 0:E1], gk[:, :, :, :].rearrange("p t k e -> p t e k"),
                                          AX.X, ALU.add)

                @block.gpsimd
                def _(pool):
                    pool.memset(neghalf[:, :], -0.5)
                    pool.drain()
                    with pool.Fori(0, NQ) as i:
                        pool.wait_ge(var_ready, i + 1)
                        ln_rstd(pool, rstd, neghalf, QT).then_inc(rstd_ready, 1)
                        pool.wait_ge(xs_ready, i + 1)
                        pool.tensor_copy(xT[:, ds(i * QN, QN)], xs[:, :]).then_inc(xT_stored, 1)

                @block.scalar
                def _(act):
                    act.preload_act_table(ACT.Exp)
                    act.sem_inc(xT_stored, 1)
                    with act.Fori(0, NQ) as i:
                        act.wait_ge(xT_stored, i + 1)
                        act.wait_ge(turned, i + 1)
                        act.copy(xs[:, :], ps[:, 0, :]).then_inc(xs_ready, 1)
                        act.wait_ge(nmx_ready, i + 1)
                        for j in range(QT):
                            last = act.activation(ex[:, j, :], ps[:, 1, j * E1:(j + 1) * E1], ACT.Exp,
                                                  bias=nmx[:, j:j + 1])
                        last.then_inc(ex_ready, 1)

                @block.tensor
                def _(pe):
                    with pe.Fori(0, NQ) as i:
                        pe.wait_ge(xn_ready, i + 1)
                        for j in range(QT):
                            last = pe.transpose(ps[:, 0, j * P:(j + 1) * P], xn[:, j, :], ident)
                        last.then_inc(turned, 1)
                        pe.wait_ge(xs_ready, i + 1)
                        for j in range(QT):
                            last = pe.matmul(ps[:, 1, j * E1:(j + 1) * E1], xs[:, j * P:(j + 1) * P], W("wr1"),
                                             start=True, stop=True)
                        last.then_inc(logit_mm, 1)

        def moe1_experts(xT, gates, ring, slot_in, slot_free):
            with ExitStack() as st:
                act1 = sb("y_act1", [P, 2, QN], F32, st)
                a = sb("y_a", [P, 2, QN], F32, st)
                hid_mm = sem("y_hid_mm")
                silu_done = sem("y_silu_done")
                a_ready = sem("y_a_ready")
                y_mm = sem("y_y_mm")
                y_used = sem("y_y_used")
                STEPS = 2 * NQ
                block = st.enter_context(nc.Block())

                @block.sync
                def _(sp):
                    sp.sem_inc(slot_free, 2)
                    with sp.Fori(0, EXP1 // 2) as pair:
                        e = pair * 2
                        for s in range(2):
                            sp.wait_ge(slot_free, e + s + 1)
                            sp.dma_start(ring[:, s, :], w1[:, ds(e + s, 1), :]).then_inc(slot_in[s], 16)

                @block.tensor
                def _(pe):
                    pe.sem_inc(a_ready, 2)
                    pe.sem_inc(y_mm, 2)
                    pe.sem_inc(y_used, 2)

                    def hidden(e, n):
                        s, c = n // NQ, n % NQ
                        if c == 0:
                            pe.wait_ge(slot_in[s], e * 8 + 16)
                        pe.wait_ge(a_ready, e * NQ + n + 1)
                        for part in range(2):
                            last = pe.matmul(ps[:, 2 * (n % 2) + part, :], ring[:, s, part * D:(part + 1) * D],
                                             xT[:, c * QN:(c + 1) * QN], start=True, stop=True)
                        last.then_inc(hid_mm, 1)

                    def output(e, n):
                        s = n // NQ
                        pe.wait_ge(a_ready, e * NQ + n + 3)
                        pe.wait_ge(y_used, e * NQ + n + 1)
                        for j in range(QT):
                            last = pe.matmul(ps[:, 4 + n % 2, j * D:(j + 1) * D], a[:, n % 2, j * P:(j + 1) * P],
                                             ring[:, s, 2 * D:3 * D], start=True, stop=True)
                        last.then_inc(y_mm, 1)

                    with pe.Fori(0, EXP1 // 2) as pair:
                        e = pair * 2
                        for n in range(STEPS):
                            hidden(e, n)
                            if n:
                                output(e, n - 1)
                        output(e, STEPS - 1)

                @block.scalar
                def _(act):
                    act.preload_act_table(ACT.Silu)
                    with act.Fori(0, EXP1 // 2) as pair:
                        e = pair * 2
                        for n in range(STEPS):
                            act.wait_ge(hid_mm, e * NQ + n + 1)
                            act.wait_ge(a_ready, e * NQ + n + 1)
                            act.activation(act1[:, n % 2, :], ps[:, 2 * (n % 2), :], ACT.Silu).then_inc(silu_done, 1)

                @block.vector
                def _(dve):
                    def combine(e, n):
                        dve.wait_ge(y_mm, e * NQ + n + 3)
                        s, c = n // NQ, n % NQ
                        for j in range(QT):
                            t = c * QT + j
                            last = dve.scalar_tensor_tensor(h[:, t, :], ps[:, 4 + n % 2, j * D:(j + 1) * D],
                                                            gates[:, t, ds(e + s, 1)], h[:, t, :], ALU.mult, ALU.add)
                        last.then_inc(y_used, 1)
                        if c == NQ - 1:
                            dve.sem_inc(slot_free, 1)

                    with dve.Fori(0, EXP1 // 2) as pair:
                        e = pair * 2
                        for n in range(STEPS):
                            dve.wait_ge(silu_done, e * NQ + n + 1)
                            dve.wait_ge(y_mm, e * NQ + n + 1)
                            dve.tensor_tensor(a[:, n % 2, :], act1[:, n % 2, :], ps[:, 2 * (n % 2) + 1, :],
                                              ALU.mult).then_inc(a_ready, 1)
                            if n:
                                combine(e, n - 1)
                        combine(e, STEPS - 1)

        for n, stage in enumerate((token_stage, gla_stage, moe0_stage, attention_stage, moe1_stage)):
            if n < last_stage:
                stage()

        stored_out = sem("stored_out")
        with nc.Block() as block:
            @block.sync
            def _(sp):
                sp.wait_ge(loaded, 48)
                sp.wait_ge(band_made, 16)
                sp.dma_start(out, h[:, :, :]).then_inc(stored_out, 16)
                sp.wait_ge(stored_out, 16)


def layouts(inputs):
    import numpy as np

    g = {k: np.asarray(v) for k, v in inputs.items()}
    weights = np.zeros((P, WCOLS), np.float32)

    def put(name, a):
        o, n = _cols[name]
        assert a.shape[1] == n, (name, a.shape)
        weights[0:a.shape[0], o:o + n] = a

    put("tok_w", g["L0_tok_expert_w"].transpose(2, 0, 1).reshape(D, E_TOK * D))
    put("tok_b", g["L0_tok_expert_b"])
    put("wk", g["L0_attn_Wk"].T)
    put("wq", g["L0_attn_Wq"].T)
    put("wv", g["L0_attn_Wv"].T)
    put("wo0", g["L0_attn_Wo"].T)
    put("wg1", g["L0_attn_Wg1"].T)
    put("wg2", g["L0_attn_Wg2"].T)
    for z in "kqv":
        put("conv_" + z, g["L0_attn_conv_" + z][:, 0, :])
    put("bg2", g["L0_attn_bg2"][:, None])
    put("norm_w", g["L0_attn_norm_w"][:, None])
    put("rw0", g["L0_ffn_router_w"].T)
    put("rb0", g["L0_ffn_router_b"][None])
    put("fc2_b", g["L0_ffn_fc2_b"])
    qkv, bqkv = g["L1_attn_Wqkv"], g["L1_attn_bqkv"]
    for name, bname, part in (("aq", "abq", 0), ("ak", "abk", 1)):
        w = qkv[:, part * D:(part + 1) * D].reshape(D, 2, 4, DH)
        b = bqkv[part * D:(part + 1) * D].reshape(2, 4, DH)
        put(name, np.pad(w, ((0, 0), (0, 0), (0, 0), (0, 32 - DH))).reshape(D, 2 * P))
        put(bname, np.pad(b, ((0, 0), (0, 0), (0, 32 - DH))).reshape(2, P).T)
    put("av", qkv[:, 2 * D:3 * D])
    put("abv", bqkv[None, 2 * D:3 * D])
    put("awo", g["L1_attn_Wo"])
    put("abo", g["L1_attn_bo"][None])
    put("wr1", g["L1_ffn_Wr"])

    consts = np.zeros((P, CCOLS), np.float32)

    def cput(name, a):
        o, n = _ccols[name]
        consts[:, o:o + n] = a

    cput("ident", np.eye(P))
    cput("iota", np.arange(P)[None])
    cput("reset", (np.arange(QN) % CHUNK != 0)[None])
    cput("ones", 1.0)
    step = D // E_TOK
    cput("thr", np.tile([-3.0e38] + [step * e - 1 for e in range(1, E_TOK)] + [3.0e38], QT)[None])
    j, i = np.arange(P)[:, None], np.arange(P)[None]
    causal = ((j <= i) & (j // CHUNK == i // CHUNK)).astype(np.uint32)

    fc1 = g["L0_ffn_fc1_w"].transpose(2, 0, 1)
    fc2 = g["L0_ffn_fc2_w"].reshape(E0, D, 2, P).transpose(3, 0, 2, 1).reshape(P, E0, 2 * D)
    b1 = g["L0_ffn_fc1_b"].reshape(E0, 4, P).transpose(2, 0, 1)
    w0 = np.concatenate([fc1, fc2, b1], axis=2)
    w1 = np.concatenate([
        np.concatenate([g["L1_ffn_Wg"], g["L1_ffn_sWg"]]), np.concatenate([g["L1_ffn_Wu"], g["L1_ffn_sWu"]]),
        np.concatenate([g["L1_ffn_Wd"], g["L1_ffn_sWd"]])], axis=2).transpose(1, 0, 2)
    return {
        "ids": g["x"].reshape(T, P).T,
        "emb_gate": np.concatenate([g["L0_tok_emb_table"], g["L0_tok_gate_table"]], axis=1),
        "weights": weights,
        "consts": consts,
        "causal": causal,
        "rel": g["L1_attn_rel_pos_bias"].T,
        "w0": w0,
        "w1": w1,
    }


LAST_STAGE = 5


def kernel(**inputs):
    import numpy as np
    import concourse.bacc as bacc
    from concourse.bass_utils import run_bass_kernel_spmd

    nc = bacc.Bacc("TRN2", target_bir_lowering=False, num_devices=1)
    arrays, args = {}, []
    for name, a in layouts(inputs).items():
        a = np.ascontiguousarray(a)
        arrays["in_" + name] = a
        args.append(nc.dram_tensor("in_" + name, a.shape, mybir.dt.from_np(a.dtype), kind="ExternalInput").ap())
    out = nc.dram_tensor("out_0", (P, T, D), F32, kind="ExternalOutput").ap()
    tower_kernel(nc, *args, out, last_stage=LAST_STAGE)
    r = run_bass_kernel_spmd(nc, [arrays], core_ids=[0])
    return r.results[0]["out_0"].transpose(1, 0, 2).reshape(B, L, D)
```

```python
from contextlib import ExitStack

import concourse.bass as bass
from concourse import mybir
from concourse.alu_op_type import AluOpType as ALU

F32 = mybir.dt.float32
I32 = mybir.dt.int32
U32 = mybir.dt.uint32
ACT = mybir.ActivationFunctionType
AX = mybir.AxisListType
ds = bass.ds

P = 128
D = 128
B, L = 8, 256
N = B * L
T = N // P
QT = 4
QN = QT * P
NQ = T // QT
SQ = QN // L
EPS_LN = 1e-5

E_TOK = 5
CHUNK = 64
NC_SEQ = L // CHUNK
GATE_NORM = 16.0
TAPS = 4
RANK = 16

E0, F0 = 8, 256
W0COLS = 2 * F0 + 2 * D + 4
HEADS, DH, WIN = 8, 16, 64
KW = P + WIN
NEG = -1.0e30

E1, F1, TOPK1, NS1 = 64, 128, 6, 2
EXP1 = E1 + NS1
W1COLS = 3 * D
NTILE = -(-((N * TOPK1 - E1) // P + E1) // (2 * QT)) * 2 * QT
ZCOLS = 1024
ZFILLS = NTILE * D // ZCOLS
WLOADS = 8

_cols = {}
WCOLS = 0
for _name, _n in (("tok_w", E_TOK * D), ("tok_b", D), ("wk", D), ("wq", D), ("wv", D), ("wo0", D), ("wg1", RANK),
                  ("wg2", D), ("conv_k", TAPS), ("conv_q", TAPS), ("conv_v", TAPS), ("bg2", 1), ("norm_w", 1),
                  ("rw0", E0), ("rb0", E0), ("fc2_b", D), ("aq", 2 * P), ("ak", 2 * P), ("av", D), ("abq", 2),
                  ("abk", 2), ("abv", D), ("awo", D), ("abo", D), ("wr1", E1)):
    _cols[_name] = (WCOLS, _n)
    WCOLS += _n
_ccols = {}
CCOLS = 0
for _name, _n in (("ident", P), ("iota", P), ("reset", QN), ("ones", P), ("full", P), ("earlier", P), ("iota_tiles", NTILE), ("thr", QT * (E_TOK + 1))):
    _ccols[_name] = (CCOLS, _n)
    CCOLS += _n


def tower_kernel(nc, ids, emb_gate, weights, consts, causal, rel, w0, w1, out):
    ctx = ExitStack()
    with ctx:
        def sb(name, shape, dt=F32, scope=ctx):
            return scope.enter_context(nc.sbuf_tensor(name, shape, dt))

        def sem(name):
            return ctx.enter_context(nc.semaphore(name))

        ps = ctx.enter_context(nc.psum_tensor("ps", [P, 8, 512], F32))
        h = sb("h", [P, T, D])
        wsb = sb("wsb", [P, WCOLS])
        csb = sb("csb", [P, CCOLS])
        causal_sb = sb("causal_sb", [P, P], U32)
        band = sb("band", [P, HEADS, KW])
        carrier = sb("carrier", [P, 1])

        def W(name, rows=P):
            o, n = _cols[name]
            return wsb[0:rows, o:o + n]

        def C(name, rows=P):
            o, n = _ccols[name]
            return csb[0:rows, o:o + n]

        ident = C("ident")
        ones_col = C("ones")[:, 0:1]
        ones_row = C("ones", 1)

        loaded = sem("loaded")
        band_made = sem("band_made")

        def ln_stats(dve, stats, mv, rstd, tiles, i, var_ready):
            for j in range(tiles):
                dve.bn_stats(stats[:, j, :], h[:, ds(i * tiles + j, 1), :])
            dve.drain()
            for j in range(tiles):
                dve.bn_aggr(mv[:, j, :], stats[:, j, :])
            dve.drain()
            dve.tensor_scalar(rstd[:, 0:tiles], mv[:, 0:tiles, 1], EPS_LN, None, ALU.add).then_inc(var_ready, 1)

        def ln_rstd(pool, rstd, neghalf, tiles):
            return pool.tensor_tensor(rstd[:, 0:tiles], rstd[:, 0:tiles], neghalf[:, 0:tiles], ALU.pow)

        def ln_apply(dve, xn, mv, rstd, tiles, i):
            for j in range(tiles):
                last = dve.tensor_scalar(xn[:, j, :], h[:, ds(i * tiles + j, 1), :], mv[:, j, 0:1], rstd[:, j:j + 1],
                                         ALU.subtract, ALU.mult)
            return last

        def token_stage():
            with ExitStack() as st:
                idx = sb("idx", [P, T], I32, st)
                emb = sb("emb", [P, T, D + 1], F32, st)
                gate = sb("gate", [P, NQ, QT], F32, st)
                scaled = sb("scaled", [P, NQ, QT], F32, st)
                whole_i = sb("whole_i", [P, NQ, QT], I32, st)
                whole = sb("whole", [P, NQ, QT], F32, st)
                frac = sb("frac", [P, NQ, QT], F32, st)
                above = sb("above", [P, NQ, QT, E_TOK + 1], F32, st)
                onehot = sb("onehot", [P, NQ, QT, E_TOK], F32, st)
                mask = sb("mask", [P, QT, D], F32, st)
                xm = sb("xm", [P, 2, QT, D], F32, st)
                xmT = sb("xmT", [P, 2, QN], F32, st)
                ohT = sb("ohT", [E_TOK, 2, QN], F32, st)
                ids_in = sem("ids_in")
                emb_in = [sem(f"emb_in{q}") for q in range(NQ)]
                xm_ready = sem("xm_ready")
                turned = sem("tok_turned")
                moved = sem("tok_moved")
                tok_mm = sem("tok_mm")
                bias_in_h = sem("bias_in_h")
                h_ready = sem("tok_h_ready")
                neg_fill = sem("neg_fill")
                neg_out = sem("neg_out")
                diag_out = sem("diag_out")
                thr = C("thr").rearrange("p (t e) -> p t e", t=QT)
                scratch = nc.dram_tensor("band_scratch", (P, HEADS, KW), F32, kind="Internal").ap()

                block = st.enter_context(nc.Block())

                @block.sync
                def _(sp):
                    sp.dma_start(idx[:, :], ids).then_inc(ids_in, 16)
                    sp.dma_start(csb[:, :], consts).then_inc(loaded, 16)
                    sp.dma_start(wsb[:, :], weights).then_inc(loaded, 16)
                    sp.dma_start(causal_sb[:, :], causal).then_inc(loaded, 16)
                    sp.wait_ge(neg_fill, 1)
                    sp.dma_start(scratch, band[:, :, :]).then_inc(neg_out, 16)
                    sp.wait_ge(neg_out, 16)
                    diagonal = bass.AP(scratch.tensor, 1, [[HEADS * KW + 1, P], [KW, HEADS], [1, WIN]])
                    source = bass.AP(rel.tensor, 0, [[0, P], [WIN, HEADS], [1, WIN]])
                    sp.dma_start(diagonal, source).then_inc(diag_out, 16)
                    sp.wait_ge(diag_out, 16)
                    sp.dma_start(band[:, :, :], scratch).then_inc(band_made, 16)

                @block.gpsimd
                def _(pool):
                    pool.wait_ge(ids_in, 16)
                    for t in range(T):
                        pool.indirect_dma_start(emb[:, t, :], None, emb_gate,
                                                bass.IndirectOffsetOnAxis(ap=idx[:, t:t + 1], axis=0)
                                                ).then_inc(emb_in[t // QT], 16)
                        if t == 0:
                            pool.memset(band[:, :, :], NEG).then_inc(neg_fill, 1)

                def select(dve, q):
                    dve.wait_ge(tok_mm, q + 1)
                    dve.wait_ge(bias_in_h, q + 1)
                    for e in range(E_TOK):
                        for j in range(QT):
                            y = ps[:, j, e * D:(e + 1) * D] if e < 4 else ps[:, 4, j * D:(j + 1) * D]
                            t = QT * q + j
                            last = dve.scalar_tensor_tensor(h[:, t, :], y, onehot[:, q, j, e:e + 1], h[:, t, :],
                                                            ALU.mult, ALU.add)
                        if e < E_TOK - 1:
                            dve.drain()
                    last.then_inc(h_ready, 1)

                @block.vector
                def _(dve):
                    dve.wait_ge(loaded, 48)
                    for q in range(NQ):
                        dve.wait_ge(emb_in[q], 16 * QT)
                        raw = emb[:, QT * q:QT * (q + 1), D]
                        dve.tensor_scalar(gate[:, q, :], raw, float(D), None, ALU.mult)
                        dve.drain()
                        dve.tensor_scalar(scaled[:, q, :], gate[:, q, :], 1.0e9, float(2 ** 23), ALU.mult, ALU.min)
                        dve.tensor_tensor(above[:, q], gate[:, q, :].unsqueeze(2).to_broadcast([P, QT, E_TOK + 1]),
                                          thr, ALU.is_gt)
                        dve.drain()
                        dve.tensor_copy(whole_i[:, q, :], scaled[:, q, :])
                        dve.tensor_tensor(onehot[:, q], above[:, q, :, 0:E_TOK], above[:, q, :, 1:E_TOK + 1],
                                          ALU.subtract)
                        dve.drain()
                        dve.tensor_copy(whole[:, q, :], whole_i[:, q, :])
                        dve.drain()
                        dve.tensor_tensor(frac[:, q, :], scaled[:, q, :], whole[:, q, :], ALU.subtract)
                        dve.drain()
                        dve.scalar_tensor_tensor(frac[:, q, :], frac[:, q, :], 0.0, frac[:, q, :], ALU.is_lt, ALU.add)
                        dve.drain()
                        dve.tensor_scalar(frac[:, q, :], frac[:, q, :], 1.0e-9, None, ALU.mult)
                        dve.drain()
                        for j in range(QT):
                            dve.tensor_scalar(mask[:, j, :], C("iota"), gate[:, q, j:j + 1], frac[:, q, j:j + 1],
                                              ALU.is_lt, ALU.add)
                        dve.drain()
                        if q >= 2:
                            dve.wait_ge(turned, q - 1)
                        dve.tensor_tensor(xm[:, q % 2], emb[:, QT * q:QT * (q + 1), 0:D], mask[:, :, :],
                                          ALU.mult).then_inc(xm_ready, 1)
                        if q >= 1:
                            select(dve, q - 1)
                    select(dve, NQ - 1)

                @block.tensor
                def _(pe):
                    for q in range(NQ):
                        pe.wait_ge(xm_ready, q + 1)
                        if q >= 1:
                            pe.wait_ge(moved, q)
                        for j in range(QT):
                            pe.transpose(ps[:, 6, j * P:(j + 1) * P], xm[:, q % 2, j, :], ident)
                        for j in range(QT):
                            last = pe.transpose(ps[0:E_TOK, 7, j * P:(j + 1) * P], onehot[:, q, j, :], ident)
                        last.then_inc(turned, 1)
                        pe.wait_ge(moved, q + 1)
                        if q >= 1:
                            pe.wait_ge(h_ready, q)
                            pe.wait_ge(bias_in_h, q)
                        for j in range(QT):
                            x = xmT[:, q % 2, j * P:(j + 1) * P]
                            pe.matmul(ps[:, j, :], x, W("tok_w")[:, 0:4 * D], start=True, stop=True)
                            pe.matmul(ps[:, 4, j * D:(j + 1) * D], x, W("tok_w")[:, 4 * D:5 * D], start=True, stop=True)
                            last = pe.matmul(ps[:, 5, j * D:(j + 1) * D], ohT[:, q % 2, j * P:(j + 1) * P],
                                             W("tok_b", E_TOK), start=True, stop=True)
                        last.then_inc(tok_mm, 1)

                @block.scalar
                def _(act):
                    for q in range(NQ):
                        act.wait_ge(turned, q + 1)
                        act.copy(xmT[:, q % 2, :], ps[:, 6, :])
                        act.copy(ohT[:, q % 2, :], ps[0:E_TOK, 7, :]).then_inc(moved, 1)
                        act.wait_ge(tok_mm, q + 1)
                        act.copy(h[:, QT * q:QT * (q + 1), :],
                                 ps[:, 5, :].rearrange("p (t d) -> p t d", t=QT)).then_inc(bias_in_h, 1)

        def gla_stage():
            with ExitStack() as st:
                kT = sb("kT", [P, N], F32, st)
                qT = sb("qT", [P, N], F32, st)
                vT = sb("vT", [P, N], F32, st)
                gT = sb("gT", [P, N], F32, st)
                gla_projections(kT, qT, vT, gT)
                gla_chunks(kT, qT, vT, gT)

        def gla_projections(kT, qT, vT, gT):
            with ExitStack() as st:
                stats = sb("a_stats", [P, QT, 6], F32, st)
                mv = sb("a_mv", [P, QT, 2], F32, st)
                rstd = sb("a_rstd", [P, QT], F32, st)
                neghalf = sb("a_neghalf", [P, QT], F32, st)
                xn = sb("a_xn", [P, QT, D], F32, st)
                xT = sb("a_xT", [P, QN], F32, st)
                g1 = sb("a_g1", [RANK, QN], F32, st)
                cv = sb("a_cv", [P, 3, SQ, L], F32, st)
                var_ready = sem("a_var_ready")
                rstd_ready = sem("a_rstd_ready")
                xn_ready = sem("a_xn_ready")
                turned = sem("a_turned")
                xT_ready = sem("a_xT_ready")
                projected = sem("a_projected")
                g1_ready = sem("a_g1_ready")
                g_mm = sem("a_g_mm")
                tap_ready = sem("a_tap_ready")
                g_stored = sem("a_g_stored")
                conv_done = sem("a_conv_done")
                stored = sem("a_stored")
                block = st.enter_context(nc.Block())

                @block.vector
                def _(dve):
                    with dve.Fori(0, NQ) as i:
                        ln_stats(dve, stats, mv, rstd, QT, i, var_ready)
                        dve.wait_ge(rstd_ready, i + 1)
                        ln_apply(dve, xn, mv, rstd, QT, i).then_inc(xn_ready, 1)
                        dve.wait_ge(tap_ready, i + 1)
                        for back in range(1, TAPS):
                            for z, w in enumerate(("conv_k", "conv_q", "conv_v")):
                                src = ps[:, 1 + z, :].rearrange("p (s l) -> p s l", s=SQ)[:, :, 0:L - back]
                                dst = cv[:, z, :, back:L]
                                last = dve.scalar_tensor_tensor(dst, src, W(w)[:, TAPS - 1 - back:TAPS - back], dst,
                                                                ALU.mult, ALU.add)
                            if back < TAPS - 1:
                                dve.drain()
                        last.then_inc(conv_done, 1)

                @block.gpsimd
                def _(pool):
                    pool.memset(neghalf[:, :], -0.5)
                    pool.drain()
                    with pool.Fori(0, NQ) as i:
                        pool.wait_ge(var_ready, i + 1)
                        ln_rstd(pool, rstd, neghalf, QT).then_inc(rstd_ready, 1)

                @block.tensor
                def _(pe):
                    pe.sem_inc(conv_done, 1)
                    with pe.Fori(0, NQ) as i:
                        pe.wait_ge(xn_ready, i + 1)
                        for j in range(QT):
                            last = pe.transpose(ps[:, 0, j * P:(j + 1) * P], xn[:, j, :], ident)
                        last.then_inc(turned, 1)
                        pe.wait_ge(xT_ready, i + 1)
                        pe.matmul(ps[0:RANK, 4, :], W("wg1"), xT[:, :], start=True, stop=True).then_inc(projected, 1)
                        pe.wait_ge(conv_done, i + 1)
                        for z, w in enumerate(("wk", "wq", "wv")):
                            pe.matmul(ps[:, 1 + z, :], W(w), xT[:, :], start=True, stop=True).then_inc(projected, 1)
                        pe.wait_ge(g1_ready, i + 1)
                        pe.matmul(ps[:, 5, :], W("wg2", RANK), g1[:, :], start=True, stop=True).then_inc(g_mm, 1)

                @block.scalar
                def _(act):
                    act.preload_act_table(ACT.Silu)
                    with act.Fori(0, NQ) as i:
                        act.wait_ge(turned, i + 1)
                        act.copy(xT[:, :], ps[:, 0, :]).then_inc(xT_ready, 1)
                        act.wait_ge(projected, i * 4 + 1)
                        act.copy(g1[:, :], ps[0:RANK, 4, :]).then_inc(g1_ready, 1)
                        act.wait_ge(projected, i * 4 + 4)
                        for z, w in enumerate(("conv_k", "conv_q", "conv_v")):
                            last = act.activation(cv[:, z], ps[:, 1 + z, :].rearrange("p (s l) -> p s l", s=SQ),
                                                  ACT.Copy, scale=W(w)[:, TAPS - 1:TAPS])
                        last.then_inc(tap_ready, 1)
                        act.wait_ge(g_mm, i + 1)
                        act.activation(gT[:, ds(i * QN, QN)], ps[:, 5, :], ACT.Identity, bias=W("bg2"))
                        act.wait_ge(conv_done, i + 2)
                        for z, dst in enumerate((kT, qT, vT)):
                            act.activation(dst[:, ds(i * QN, QN)], cv[:, z].rearrange("p s l -> p (s l)"), ACT.Silu)

        def gla_chunks(kT, qT, vT, gT):
            with ExitStack() as st:
                v_in = sb("c_v_in", [P, QN], F32, st)
                mag = sb("c_mag", [P, QN], F32, st)
                soft = sb("c_soft", [P, QN], F32, st)
                logsig = sb("c_logsig", [P, QN], F32, st)
                cum = sb("c_cum", [P, QN], F32, st)
                up = sb("c_up", [P, QN], F32, st)
                down = sb("c_down", [P, QN], F32, st)
                sq = sb("c_sq", [P, 2, QN], F32, st)
                qe = sb("c_qe", [P, QN], F32, st)
                ke = sb("c_ke", [P, QN], F32, st)
                norms = sb("c_norms", [P, 2 * QT], F32, st)
                inv = sb("c_inv", [P, 2 * QT], F32, st)
                half = sb("c_half", [P, 2 * QT], F32, st)
                neghalf = sb("c_neghalf", [P, QT], F32, st)
                v_tok = sb("c_v_tok", [P, QT, D], F32, st)
                ke_tok = sb("c_ke_tok", [P, QT, D], F32, st)
                wT = sb("c_wT", [P, QT, P], F32, st)
                state = sb("c_state", [P, NC_SEQ - 1, SQ, D], F32, st)
                oT = sb("c_oT", [P, QN], F32, st)
                osq = sb("c_osq", [P, QN], F32, st)
                ms = sb("c_ms", [P, QT], F32, st)
                fac = sb("c_fac", [P, QT], F32, st)
                v_copied = sem("c_v_copied")
                soft_ready = sem("c_soft_ready")
                cum_ready = sem("c_cum_ready")
                exps_ready = sem("c_exps_ready")
                sq_ready = sem("c_sq_ready")
                qk_ready = sem("c_qk_ready")
                norm_mm = sem("c_norm_mm")
                norms_out = sem("c_norms_out")
                root_ready = sem("c_root_ready")
                v_turned = sem("c_v_turned")
                ke_turned = sem("c_ke_turned")
                v_ready = sem("c_v_ready")
                ke_ready = sem("c_ke_ready")
                w_ready = sem("c_w_ready")
                outer_mm = sem("c_outer_mm")
                state_ready = sem("c_state_ready")
                o_mm = sem("c_o_mm")
                o_ready = sem("c_o_ready")
                ss_mm = sem("c_ss_mm")
                ms_ready = sem("c_ms_ready")
                fac_ready = sem("c_fac_ready")
                out_mm = sem("c_out_mm")
                h_done = sem("c_h_done")
                block = st.enter_context(nc.Block())

                @block.gpsimd
                def _(pool):
                    pool.memset(half[:, :], 0.5)
                    pool.memset(neghalf[:, :], -0.5)
                    pool.drain()
                    pool.sem_inc(h_done, 1)
                    with pool.Fori(0, NQ) as i:
                        pool.wait_ge(h_done, i + 1)
                        pool.tensor_copy(v_in[:, :], vT[:, ds(i * QN, QN)]).then_inc(v_copied, 1)
                        pool.wait_ge(norms_out, i + 1)
                        pool.tensor_tensor(norms[:, :], norms[:, :], half[:, :], ALU.pow)
                        pool.drain()
                        pool.tensor_scalar(norms[:, :], norms[:, :], 1e-5, None, ALU.add).then_inc(root_ready, 1)
                        pool.wait_ge(ms_ready, i + 1)
                        pool.tensor_tensor(ms[:, :], ms[:, :], neghalf[:, :], ALU.pow).then_inc(fac_ready, 1)

                @block.scalar
                def _(act):
                    act.preload_act_table(ACT.Ln)
                    with act.Fori(0, NQ) as i:
                        act.wait_ge(h_done, i + 1)
                        act.activation(mag[:, :], gT[:, ds(i * QN, QN)], ACT.Abs)
                        act.drain()
                        act.activation(soft[:, :], mag[:, :], ACT.Exp, scale=-1.0)
                        act.drain()
                        act.activation(soft[:, :], soft[:, :], ACT.Ln, bias=1.0).then_inc(soft_ready, 1)
                        act.activation(sq[:, 0, :], kT[:, ds(i * QN, QN)], ACT.Square)
                        act.activation(sq[:, 1, :], qT[:, ds(i * QN, QN)], ACT.Square).then_inc(sq_ready, 1)
                        act.wait_ge(cum_ready, i + 1)
                        act.activation(down[:, :], cum[:, :], ACT.Exp, scale=1.0 / GATE_NORM)
                        act.activation(up[:, :], cum[:, :], ACT.Exp, scale=-1.0 / GATE_NORM).then_inc(exps_ready, 1)
                        act.wait_ge(ke_turned, i + 1)
                        act.copy(ke_tok[:, :, :].rearrange("p t d -> p (t d)"), ps[:, 2, :]).then_inc(ke_ready, 1)
                        act.wait_ge(o_mm, i + 1)
                        act.activation(osq[:, :], ps[:, 6, :], ACT.Square)
                        act.activation(oT[:, :], ps[:, 6, :], ACT.Copy, scale=W("norm_w")).then_inc(o_ready, 1)

                @block.vector
                def _(dve):
                    dve.memset(wT[:, :, :], 0.0)
                    dve.drain()
                    with dve.Fori(0, NQ) as i:
                        dve.wait_ge(soft_ready, i + 1)
                        dve.scalar_tensor_tensor(logsig[:, :], gT[:, ds(i * QN, QN)], 0.0, soft[:, :],
                                                 ALU.min, ALU.subtract)
                        dve.drain()
                        dve.tensor_tensor_scan(cum[:, :], C("reset"), logsig[:, :], 0.0, ALU.mult,
                                               ALU.add).then_inc(cum_ready, 1)
                        dve.wait_ge(norm_mm, i + 1)
                        dve.tensor_copy(norms[:, :], ps[:, 0, 0:2 * QT]).then_inc(norms_out, 1)
                        dve.wait_ge(exps_ready, i + 1)
                        dve.tensor_tensor(ke[:, :], kT[:, ds(i * QN, QN)], up[:, :], ALU.mult)
                        dve.tensor_tensor(qe[:, :], qT[:, ds(i * QN, QN)], down[:, :], ALU.mult).then_inc(qk_ready, 1)
                        dve.wait_ge(root_ready, i + 1)
                        dve.reciprocal(inv[:, :], norms[:, :])
                        dve.drain()
                        dve.wait_ge(v_turned, i + 1)
                        for j in range(QT):
                            last = dve.tensor_scalar(v_tok[:, j, :], ps[:, 1, j * D:(j + 1) * D], inv[:, j:j + 1],
                                                     None, ALU.mult)
                        last.then_inc(v_ready, 1)
                        dve.wait_ge(outer_mm, i + 1)
                        ends = down[:, :].rearrange("p (s c l) -> p s c l", s=SQ, c=NC_SEQ)
                        for c in range(NC_SEQ - 1):
                            if c % 2 == 0:
                                prod = ps[:, 4, :].rearrange("p (s c d) -> p s c d", s=SQ, c=2)[:, :, c // 2, :]
                            else:
                                prod = ps[:, 5, 0:SQ * D].rearrange("p (s d) -> p s d", s=SQ)
                            end = ends[:, :, c, CHUNK - 1:CHUNK].to_broadcast([P, SQ, D])
                            if c == 0:
                                dve.tensor_tensor(state[:, c], prod, end, ALU.mult)
                                dve.copy_predicated(wT[:, :, :],
                                                    causal_sb[:, :].unsqueeze(1).to_broadcast([P, QT, P]),
                                                    ps[:, 3, :].rearrange("p (t q) -> p t q", t=QT)
                                                    ).then_inc(w_ready, 1)
                            else:
                                dve.drain()
                                dve.tensor_tensor(state[:, c], state[:, c - 1], prod, ALU.add)
                                dve.drain()
                                last = dve.tensor_tensor(state[:, c], state[:, c], end, ALU.mult)
                        last.then_inc(state_ready, 1)
                        dve.wait_ge(ss_mm, i + 1)
                        dve.tensor_tensor(fac[:, :], inv[:, QT:2 * QT], inv[:, QT:2 * QT], ALU.mult)
                        dve.drain()
                        dve.tensor_tensor(ms[:, :], ps[:, 0, 2 * QT:3 * QT], fac[:, :], ALU.mult)
                        dve.drain()
                        dve.tensor_scalar(ms[:, :], ms[:, :], 1.0 / D, 1e-6, ALU.mult, ALU.add).then_inc(ms_ready, 1)
                        dve.wait_ge(fac_ready, i + 1)
                        dve.tensor_tensor(fac[:, :], ms[:, :], inv[:, QT:2 * QT], ALU.mult)
                        dve.drain()
                        dve.wait_ge(out_mm, i + 1)
                        for j in range(QT):
                            hj = h[:, ds(i * QT + j, 1), :].rearrange("p t d -> p (t d)")
                            last = dve.scalar_tensor_tensor(hj, ps[:, 7, j * D:(j + 1) * D], fac[:, j:j + 1], hj,
                                                            ALU.mult, ALU.add)
                        last.then_inc(h_done, 1)

                @block.tensor
                def _(pe):
                    with pe.Fori(0, NQ) as i:
                        pe.wait_ge(v_copied, i + 1)
                        for j in range(QT):
                            last = pe.transpose(ps[:, 1, j * P:(j + 1) * P], v_in[:, j * P:(j + 1) * P], ident)
                        last.then_inc(v_turned, 1)
                        pe.wait_ge(sq_ready, i + 1)
                        for z in range(2):
                            for j in range(QT):
                                last = pe.matmul(ps[:, 0, z * QT + j:z * QT + j + 1], sq[:, z, j * P:(j + 1) * P],
                                                 ones_col, start=True, stop=True)
                        last.then_inc(norm_mm, 1)
                        pe.wait_ge(qk_ready, i + 1)
                        for j in range(QT):
                            last = pe.transpose(ps[:, 2, j * P:(j + 1) * P], ke[:, j * P:(j + 1) * P], ident)
                        last.then_inc(ke_turned, 1)
                        for j in range(QT):
                            last = pe.matmul(ps[:, 3, j * P:(j + 1) * P], ke[:, j * P:(j + 1) * P],
                                             qe[:, j * P:(j + 1) * P], start=True, stop=True)
                        pe.wait_ge(ke_ready, i + 1)
                        pe.wait_ge(v_ready, i + 1)
                        for s in range(SQ):
                            for c in range(NC_SEQ - 1):
                                rows = slice(CHUNK * (c % 2), CHUNK * (c % 2) + CHUNK)
                                tile = 2 * s + c // 2
                                at = (2 * s + c // 2) * D if c % 2 == 0 else s * D
                                last = pe.matmul(ps[:, 4 + c % 2, at:at + D], ke_tok[rows, tile, :],
                                                 v_tok[rows, tile, :], start=True, stop=True)
                        last.then_inc(outer_mm, 1)
                        pe.wait_ge(w_ready, i + 1)
                        pe.wait_ge(state_ready, i + 1)
                        for j in range(QT):
                            s = j // 2
                            pe.matmul(ps[:, 6, j * P:(j + 1) * P], v_tok[:, j, :], wT[:, j, :], start=True,
                                      stop=False, skip_group_check=True)
                            for half_ in range(2):
                                c = 2 * (j % 2) + half_
                                if c:
                                    at = j * P + half_ * CHUNK
                                    last = pe.matmul(ps[:, 6, at:at + CHUNK], state[:, c - 1, s, :],
                                                     qe[:, at:at + CHUNK], start=False, stop=True,
                                                     skip_group_check=True)
                        last.then_inc(o_mm, 1)
                        pe.wait_ge(o_ready, i + 1)
                        for j in range(QT):
                            last = pe.matmul(ps[:, 0, 2 * QT + j:2 * QT + j + 1], osq[:, j * P:(j + 1) * P], ones_col,
                                             start=True, stop=True)
                        last.then_inc(ss_mm, 1)
                        for j in range(QT):
                            last = pe.matmul(ps[:, 7, j * D:(j + 1) * D], oT[:, j * P:(j + 1) * P], W("wo0"),
                                             start=True, stop=True)
                        last.then_inc(out_mm, 1)

        def moe0_stage(wexp, zeros, sorted_x, zeros_out, wexp_in):
            with ExitStack() as st:
                xT = sb("m_xT", [P, N], F32, st)
                gates = sb("m_gates", [P, T, E0], F32, st)
                ring = sb("m_ring", [P, 2, W0COLS], F32, st)
                slot_in = [sem("m_slot_in0"), sem("m_slot_in1")]
                slot_free = sem("m_slot_free")
                moe0_router(xT, gates, wexp, zeros, sorted_x, zeros_out, wexp_in)
                moe0_experts(xT, gates, ring, slot_in, slot_free)

        def moe0_router(xT, gates, wexp, zeros, sorted_x, zeros_out, wexp_in):
            with ExitStack() as st:
                stats = sb("r_stats", [P, QT, 6], F32, st)
                mv = sb("r_mv", [P, QT, 2], F32, st)
                rstd = sb("r_rstd", [P, QT], F32, st)
                neghalf = sb("r_neghalf", [P, QT], F32, st)
                xn = sb("r_xn", [P, QT, D], F32, st)
                xs = sb("r_xs", [P, QN], F32, st)
                logits = sb("r_logits", [P, QT, E0], F32, st)
                top = sb("r_top", [P, QT, 8], F32, st)
                topi = sb("r_topi", [P, QT, 8], U32, st)
                topf = sb("r_topf", [P, QT, 8], F32, st)
                gap = sb("r_gap", [P, QT], F32, st)
                ex = sb("r_ex", [P, QT], F32, st)
                den = sb("r_den", [P, QT], F32, st)
                wts = sb("r_wts", [P, 2, QT], F32, st)
                g2 = sb("r_g2", [P, 2, QT, E0], F32, st)
                gq = sb("r_gq", [P, QT, E0], F32, st)
                gqT = sb("r_gqT", [E0, QN], F32, st)
                var_ready = sem("r_var_ready")
                rstd_ready = sem("r_rstd_ready")
                xn_ready = sem("r_xn_ready")
                turned = sem("r_turned")
                xs_ready = sem("r_xs_ready")
                xT_stored = sem("r_xT_stored")
                logit_mm = sem("r_logit_mm")
                gap_ready = sem("r_gap_ready")
                ex_ready = sem("r_ex_ready")
                gq_ready = sem("r_gq_ready")
                g_turned = sem("r_g_turned")
                gT_ready = sem("r_gT_ready")
                bias_mm = sem("r_bias_mm")
                h_done = sem("r_h_done")
                zeroed = sem("r_zeroed")
                block = st.enter_context(nc.Block())

                @block.sync
                def _(sp):
                    for n in range(WLOADS):
                        e = n * E1 // WLOADS
                        sp.dma_start(wexp[:, e:e + E1 // WLOADS, :],
                                     w1[:, e:e + E1 // WLOADS, :]).then_inc(wexp_in, 16)
                    sp.wait_ge(zeroed, 1)
                    fill = sorted_x.rearrange("(p n) d -> p (n d)", p=P)
                    for n in range(ZFILLS):
                        sp.dma_start(fill[:, n * ZCOLS:(n + 1) * ZCOLS], zeros[:, :]).then_inc(zeros_out, 16)

                @block.vector
                def _(dve):
                    dve.sem_inc(h_done, 1)
                    with dve.Fori(0, NQ) as i:
                        ln_stats(dve, stats, mv, rstd, QT, i, var_ready)
                        dve.wait_ge(rstd_ready, i + 1)
                        ln_apply(dve, xn, mv, rstd, QT, i).then_inc(xn_ready, 1)
                        dve.wait_ge(logit_mm, i + 1)
                        dve.tensor_copy(logits[:, :, :], ps[:, 1, 0:QT * E0].rearrange("p (t e) -> p t e", t=QT))
                        dve.drain()
                        for j in range(QT):
                            dve.max(top[:, j, :], logits[:, j, :])
                        dve.drain()
                        for j in range(QT):
                            dve.max_index(topi[:, j, :], top[:, j, :], logits[:, j, :])
                        dve.tensor_tensor(gap[:, :], top[:, :, 1], top[:, :, 0], ALU.subtract).then_inc(gap_ready, 1)
                        dve.drain()
                        dve.tensor_copy(topf[:, :, :], topi[:, :, :])
                        dve.wait_ge(ex_ready, i + 1)
                        dve.tensor_scalar(den[:, :], ex[:, :], 1.0, None, ALU.add)
                        dve.drain()
                        dve.reciprocal(wts[:, 0, :], den[:, :])
                        dve.drain()
                        dve.tensor_tensor(wts[:, 1, :], wts[:, 0, :], ex[:, :], ALU.mult)
                        dve.drain()
                        for k in range(2):
                            for j in range(QT):
                                dve.tensor_scalar(g2[:, k, j, :], C("iota")[:, 0:E0], topf[:, j, k:k + 1],
                                                  wts[:, k, j:j + 1], ALU.is_equal, ALU.mult)
                        dve.drain()
                        dve.tensor_tensor(gq[:, :, :], g2[:, 0], g2[:, 1], ALU.add).then_inc(gq_ready, 1)
                        dve.drain()
                        dve.tensor_copy(gates[:, ds(i * QT, QT), :], gq[:, :, :])
                        dve.wait_ge(bias_mm, i + 1)
                        dve.tensor_tensor(h[:, ds(i * QT, QT), :], h[:, ds(i * QT, QT), :],
                                          ps[:, 3, :].rearrange("p (t d) -> p t d", t=QT), ALU.add).then_inc(h_done, 1)

                @block.gpsimd
                def _(pool):
                    pool.memset(zeros[:, :], 0.0).then_inc(zeroed, 1)
                    pool.memset(neghalf[:, :], -0.5)
                    pool.drain()
                    with pool.Fori(0, NQ) as i:
                        pool.wait_ge(var_ready, i + 1)
                        ln_rstd(pool, rstd, neghalf, QT).then_inc(rstd_ready, 1)
                        pool.wait_ge(xs_ready, i + 1)
                        pool.tensor_copy(xT[:, ds(i * QN, QN)], xs[:, :]).then_inc(xT_stored, 1)

                @block.scalar
                def _(act):
                    act.preload_act_table(ACT.Exp)
                    act.sem_inc(xT_stored, 1)
                    with act.Fori(0, NQ) as i:
                        act.wait_ge(xT_stored, i + 1)
                        act.wait_ge(turned, i + 1)
                        act.copy(xs[:, :], ps[:, 0, :]).then_inc(xs_ready, 1)
                        act.wait_ge(gap_ready, i + 1)
                        act.activation(ex[:, :], gap[:, :], ACT.Exp).then_inc(ex_ready, 1)
                        act.wait_ge(g_turned, i + 1)
                        act.copy(gqT[:, :], ps[0:E0, 2, :]).then_inc(gT_ready, 1)

                @block.tensor
                def _(pe):
                    with pe.Fori(0, NQ) as i:
                        pe.wait_ge(h_done, i + 1)
                        pe.wait_ge(xn_ready, i + 1)
                        for j in range(QT):
                            last = pe.transpose(ps[:, 0, j * P:(j + 1) * P], xn[:, j, :], ident)
                        last.then_inc(turned, 1)
                        pe.wait_ge(xs_ready, i + 1)
                        for j in range(QT):
                            pe.matmul(ps[:, 1, j * E0:(j + 1) * E0], xs[:, j * P:(j + 1) * P], W("rw0"), start=True,
                                      stop=False)
                            last = pe.matmul(ps[:, 1, j * E0:(j + 1) * E0], ones_row, W("rb0", 1), start=False,
                                             stop=True)
                        last.then_inc(logit_mm, 1)
                        pe.wait_ge(gq_ready, i + 1)
                        for j in range(QT):
                            last = pe.transpose(ps[0:E0, 2, j * P:(j + 1) * P], gq[:, j, :], ident)
                        last.then_inc(g_turned, 1)
                        pe.wait_ge(gT_ready, i + 1)
                        for j in range(QT):
                            last = pe.matmul(ps[:, 3, j * D:(j + 1) * D], gqT[:, j * P:(j + 1) * P], W("fc2_b", E0),
                                             start=True, stop=True)
                        last.then_inc(bias_mm, 1)

        def moe0_experts(xT, gates, ring, slot_in, slot_free):
            with ExitStack() as st:
                act1 = sb("x_act1", [P, 2, QN], F32, st)
                a = sb("x_a", [P, 2, 2, QN], F32, st)
                hid_mm = sem("x_hid_mm")
                silu_done = sem("x_silu_done")
                a_ready = sem("x_a_ready")
                y_mm = sem("x_y_mm")
                y_used = sem("x_y_used")
                STEPS = 2 * NQ
                block = st.enter_context(nc.Block())

                @block.sync
                def _(sp):
                    sp.sem_inc(slot_free, 2)
                    with sp.Fori(0, E0 // 2) as pair:
                        e = pair * 2
                        for s in range(2):
                            sp.wait_ge(slot_free, e + s + 1)
                            sp.dma_start(ring[:, s, :], w0[:, ds(e + s, 1), :]).then_inc(slot_in[s], 16)

                def w1_of(s, part, f):
                    o = part * F0 + f * P
                    return ring[:, s, o:o + P]

                def bias_of(s, part, f):
                    o = 2 * F0 + 2 * D + part * 2 + f
                    return ring[:, s, o:o + 1]

                @block.tensor
                def _(pe):
                    pe.sem_inc(a_ready, 2)
                    pe.sem_inc(y_mm, 2)
                    pe.sem_inc(y_used, 2)

                    def hidden(e, n):
                        s, c = n // NQ, n % NQ
                        if c == 0:
                            pe.wait_ge(slot_in[s], e * 8 + 16)
                        for f in range(2):
                            pe.wait_ge(a_ready, e * (2 * NQ) + 2 * n + f + 1)
                            for part in range(2):
                                last = pe.matmul(ps[:, 2 * f + part, :], w1_of(s, part, f),
                                                 xT[:, c * QN:(c + 1) * QN], start=True, stop=True)
                            last.then_inc(hid_mm, 1)

                    def output(e, n):
                        s = n // NQ
                        pe.wait_ge(a_ready, e * (2 * NQ) + 2 * n + 4)
                        pe.wait_ge(y_used, e * NQ + n + 1)
                        for j in range(QT):
                            for f in range(2):
                                o = 2 * F0 + f * D
                                last = pe.matmul(ps[:, 4 + n % 2, j * D:(j + 1) * D], a[:, n % 2, f, j * P:(j + 1) * P],
                                                 ring[:, s, o:o + D], start=(f == 0), stop=(f == 1))
                        last.then_inc(y_mm, 1)

                    with pe.Fori(0, E0 // 2) as pair:
                        e = pair * 2
                        for n in range(STEPS):
                            hidden(e, n)
                            if n:
                                output(e, n - 1)
                        output(e, STEPS - 1)

                @block.scalar
                def _(act):
                    act.preload_act_table(ACT.Silu)
                    with act.Fori(0, E0 // 2) as pair:
                        e = pair * 2
                        for n in range(STEPS):
                            s = n // NQ
                            for f in range(2):
                                act.wait_ge(hid_mm, e * (2 * NQ) + 2 * n + f + 1)
                                act.wait_ge(a_ready, e * (2 * NQ) + 2 * n + f + 1)
                                act.activation(act1[:, f, :], ps[:, 2 * f, :], ACT.Silu,
                                               bias=bias_of(s, 0, f)).then_inc(silu_done, 1)

                @block.vector
                def _(dve):
                    def combine(e, n):
                        dve.wait_ge(y_mm, e * NQ + n + 3)
                        s, c = n // NQ, n % NQ
                        for j in range(QT):
                            t = c * QT + j
                            last = dve.scalar_tensor_tensor(h[:, t, :], ps[:, 4 + n % 2, j * D:(j + 1) * D],
                                                            gates[:, t, ds(e + s, 1)], h[:, t, :], ALU.mult, ALU.add)
                        last.then_inc(y_used, 1)
                        if c == NQ - 1:
                            dve.sem_inc(slot_free, 1)

                    with dve.Fori(0, E0 // 2) as pair:
                        e = pair * 2
                        for n in range(STEPS):
                            s = n // NQ
                            dve.wait_ge(y_mm, e * NQ + n + 1)
                            for f in range(2):
                                dve.wait_ge(silu_done, e * (2 * NQ) + 2 * n + f + 1)
                                dve.scalar_tensor_tensor(a[:, n % 2, f, :], ps[:, 2 * f + 1, :], bias_of(s, 1, f),
                                                         act1[:, f, :], ALU.add, ALU.mult).then_inc(a_ready, 1)
                            if n:
                                combine(e, n - 1)
                        combine(e, STEPS - 1)

        def attention_stage():
            with ExitStack() as st:
                AT = 2
                stats = sb("w_stats", [P, AT, 6], F32, st)
                mv = sb("w_mv", [P, AT, 2], F32, st)
                rstd = sb("w_rstd", [P, AT], F32, st)
                neghalf = sb("w_neghalf", [P, AT], F32, st)
                xn = sb("w_xn", [P, AT, D], F32, st)
                xs = sb("w_xs", [P, L], F32, st)
                bq4 = sb("w_bq4", [P, 2], F32, st)
                qs = sb("w_qs", [P, 2, L], F32, st)
                ks = sb("w_ks", [P, 2, L], F32, st)
                vs = sb("w_vs", [P, AT, D], F32, st)
                sc = sb("w_sc", [P, 2, 2, KW], F32, st)
                mx = sb("w_mx", [P, AT, 2, 4], F32, st)
                nm = sb("w_nm", [P, AT, 2, 4], F32, st)
                rs = sb("w_rs", [P, AT, 2, 4], F32, st)
                pr = sb("w_pr", [P, AT, HEADS, L], F32, st)
                pT = sb("w_pT", [P, 2, 2, 2, P], F32, st)
                rr = sb("w_rr", [P, AT, 2, 4], F32, st)
                cx = sb("w_cx", [P, AT, D], F32, st)
                cxT = sb("w_cxT", [P, L], F32, st)
                var_ready = sem("w_var_ready")
                rstd_ready = sem("w_rstd_ready")
                xn_ready = sem("w_xn_ready")
                turned = sem("w_turned")
                xs_ready = sem("w_xs_ready")
                proj_mm = sem("w_proj_mm")
                qk_ready = sem("w_qk_ready")
                v_ready = sem("w_v_ready")
                score_mm = sem("w_score_mm")
                score_used = sem("w_score_used")
                nm_ready = sem("w_nm_ready")
                exp_done = sem("w_exp_done")
                p_turned = sem("w_p_turned")
                pT_ready = sem("w_pT_ready")
                pv_mm = sem("w_pv_mm")
                cx_ready = sem("w_cx_ready")
                cx_turned = sem("w_cx_turned")
                cxT_ready = sem("w_cxT_ready")
                out_mm = sem("w_out_mm")
                h_done = sem("w_h_done")
                zeroed = sem("w_zeroed")
                UNITS = [(tile, s) for tile in range(AT) for s in range(4)]
                NU = len(UNITS)
                block = st.enter_context(nc.Block())

                def key_cols(tile):
                    return (0, P, WIN) if tile == 0 else (WIN, L, 0)

                @block.gpsimd
                def _(pool):
                    pool.memset(neghalf[:, :], -0.5)
                    pool.memset(pr[:, :, :, :], 0.0).then_inc(zeroed, 1)
                    pool.drain()
                    with pool.Fori(0, B) as i:
                        pool.wait_ge(var_ready, i + 1)
                        ln_rstd(pool, rstd, neghalf, AT).then_inc(rstd_ready, 1)

                def copy_pT(dve, i, n):
                    nb = UNITS[n][0] + 1
                    dve.wait_ge(p_turned, i * NU + n + 1)
                    if n >= 2:
                        dve.wait_ge(pv_mm, i * NU + n - 1)
                    dve.tensor_copy(pT[:, n % 2, 0:nb].rearrange("p b g q -> p (b g q)"),
                                    ps[:, 5 + n % 2, 0:nb * 2 * P]).then_inc(pT_ready, 1)

                @block.vector
                def _(dve):
                    dve.wait_ge(band_made, 16)
                    dve.tensor_scalar(bq4[:, :], W("abq"), 0.25, None, ALU.mult)
                    dve.drain().then_inc(zeroed, 1)
                    dve.sem_inc(h_done, 1)
                    with dve.Fori(0, B) as i:
                        ln_stats(dve, stats, mv, rstd, AT, i, var_ready)
                        dve.wait_ge(rstd_ready, i + 1)
                        ln_apply(dve, xn, mv, rstd, AT, i).then_inc(xn_ready, 1)
                        dve.wait_ge(proj_mm, i * 3 + 3)
                        dve.tensor_copy(vs[:, :, :], ps[:, 7, 0:L].rearrange("p (t d) -> p t d", t=AT)
                                        ).then_inc(v_ready, 1)
                        for n, (tile, s) in enumerate(UNITS):
                            lo, hi, b0 = key_cols(tile)
                            w = hi - lo
                            dve.wait_ge(score_mm, i * NU + n + 1)
                            if n >= 2:
                                dve.wait_ge(exp_done, i * NU + n - 1)
                            dve.memset(carrier[:, :], 0.0)
                            for g in range(2):
                                last = dve.tensor_tensor_reduce(sc[:, n % 2, g, 0:w], ps[:, s, 256 * g:256 * g + w],
                                                                band[:, 4 * g + s, b0:b0 + w], 1.0, NEG, ALU.add,
                                                                ALU.max, mx[:, tile, g, s:s + 1])
                            last.then_inc(score_used, 1)
                            dve.drain()
                            dve.tensor_scalar(nm[:, tile, :, s], mx[:, tile, :, s], -1.0, None,
                                              ALU.mult).then_inc(nm_ready, 1)
                            if n:
                                copy_pT(dve, i, n - 1)
                        copy_pT(dve, i, NU - 1)
                        dve.wait_ge(exp_done, i * NU + NU)
                        dve.reciprocal(rr[:, :, :, :], rs[:, :, :, :])
                        dve.drain()
                        dve.wait_ge(pv_mm, i * NU + NU)
                        dve.tensor_tensor(cx[:, :, :].rearrange("p t (h d) -> p (t h) d", h=HEADS),
                                          ps[:, 7, L:2 * L].rearrange("p (t d) -> p t d", d=DH),
                                          rr[:, :, :, :].rearrange("p t g s -> p (t g s)").unsqueeze(2)
                                          .to_broadcast([P, AT * HEADS, DH]), ALU.mult).then_inc(cx_ready, 1)
                        dve.wait_ge(out_mm, i + 1)
                        dve.tensor_tensor(h[:, ds(i * AT, AT), :], h[:, ds(i * AT, AT), :],
                                          ps[:, 4, L:2 * L].rearrange("p (t d) -> p t d", t=AT), ALU.add
                                          ).then_inc(h_done, 1)

                @block.scalar
                def _(act):
                    act.preload_act_table(ACT.Exp)
                    act.wait_ge(zeroed, 2)
                    with act.Fori(0, B) as i:
                        act.wait_ge(turned, i + 1)
                        act.copy(xs[:, :], ps[:, 4, 0:L]).then_inc(xs_ready, 1)
                        act.wait_ge(proj_mm, i * 3 + 2)
                        for g in range(2):
                            act.activation(qs[:, g, :], ps[:, 5, g * L:(g + 1) * L], ACT.Identity, scale=0.25,
                                           bias=bq4[:, g:g + 1])
                            last = act.activation(ks[:, g, :], ps[:, 6, g * L:(g + 1) * L], ACT.Identity,
                                                  bias=W("abk")[:, g:g + 1])
                        last.then_inc(qk_ready, 1)
                        for n, (tile, s) in enumerate(UNITS):
                            lo, hi, b0 = key_cols(tile)
                            act.wait_ge(nm_ready, i * NU + n + 1)
                            for g in range(2):
                                last = act.activation(pr[:, tile, 4 * g + s, lo:hi], sc[:, n % 2, g, 0:hi - lo],
                                                      ACT.Exp, bias=nm[:, tile, g, s:s + 1],
                                                      accum_out=rs[:, tile, g, s:s + 1])
                            last.then_inc(exp_done, 1)
                        act.wait_ge(cx_turned, i + 1)
                        act.copy(cxT[:, :], ps[:, 4, 0:L]).then_inc(cxT_ready, 1)

                @block.tensor
                def _(pe):
                    pe.sem_inc(score_used, 4)

                    def scores(i, n):
                        tile, s = UNITS[n]
                        lo, hi, b0 = key_cols(tile)
                        rows = slice(32 * s, 32 * s + DH)
                        pe.wait_ge(score_used, i * NU + n + 1)
                        for g in range(2):
                            last = pe.matmul(ps[:, s, 256 * g:256 * g + hi - lo], qs[rows, g, tile * P:(tile + 1) * P],
                                             ks[rows, g, lo:hi], start=True, stop=True)
                        last.then_inc(score_mm, 1)

                    def turn(i, n):
                        tile, s = UNITS[n]
                        pe.wait_ge(exp_done, i * NU + n + 1)
                        if n >= 2:
                            pe.wait_ge(pT_ready, i * NU + n - 1)
                        for b in range(tile + 1):
                            for g in range(2):
                                at = (2 * b + g) * P
                                last = pe.transpose(ps[:, 5 + n % 2, at:at + P],
                                                    pr[:, tile, 4 * g + s, b * P:(b + 1) * P], ident)
                        last.then_inc(p_turned, 1)

                    def weigh(i, n):
                        tile, s = UNITS[n]
                        pe.wait_ge(pT_ready, i * NU + n + 1)
                        for g in range(2):
                            hd = 4 * g + s
                            at = L + tile * D + hd * DH
                            for b in range(tile + 1):
                                last = pe.matmul(ps[:, 7, at:at + DH], pT[:, n % 2, b, g, :],
                                                 vs[:, b, hd * DH:(hd + 1) * DH], start=(b == 0), stop=(b == tile))
                        last.then_inc(pv_mm, 1)

                    pe.wait_ge(zeroed, 2)
                    with pe.Fori(0, B) as i:
                        pe.wait_ge(xn_ready, i + 1)
                        pe.wait_ge(h_done, i + 1)
                        for j in range(AT):
                            last = pe.transpose(ps[:, 4, j * P:(j + 1) * P], xn[:, j, :], ident)
                        last.then_inc(turned, 1)
                        pe.wait_ge(xs_ready, i + 1)
                        for b, w in ((5, "aq"), (6, "ak")):
                            for g in range(2):
                                last = pe.matmul(ps[:, b, g * L:(g + 1) * L], W(w)[:, g * P:(g + 1) * P], xs[:, :],
                                                 start=True, stop=True)
                            last.then_inc(proj_mm, 1)
                        for j in range(AT):
                            pe.matmul(ps[:, 7, j * D:(j + 1) * D], xs[:, j * P:(j + 1) * P], W("av"), start=True,
                                      stop=False)
                            last = pe.matmul(ps[:, 7, j * D:(j + 1) * D], ones_row, W("abv", 1), start=False, stop=True)
                        last.then_inc(proj_mm, 1)
                        pe.wait_ge(qk_ready, i + 1)
                        pe.wait_ge(v_ready, i + 1)
                        for n in range(3):
                            scores(i, n)
                        for n in range(NU):
                            if n + 3 < NU:
                                scores(i, n + 3)
                            turn(i, n)
                            if n:
                                weigh(i, n - 1)
                        weigh(i, NU - 1)
                        pe.wait_ge(cx_ready, i + 1)
                        for j in range(AT):
                            last = pe.transpose(ps[:, 4, j * P:(j + 1) * P], cx[:, j, :], ident)
                        last.then_inc(cx_turned, 1)
                        pe.wait_ge(cxT_ready, i + 1)
                        for j in range(AT):
                            at = L + j * D
                            pe.matmul(ps[:, 4, at:at + D], cxT[:, j * P:(j + 1) * P], W("awo"), start=True, stop=False)
                            last = pe.matmul(ps[:, 4, at:at + D], ones_row, W("abo", 1), start=False, stop=True)
                        last.then_inc(out_mm, 1)

        def moe1_stage(wexp, sorted_x, zeros_out, wexp_in):
            with ExitStack() as st:
                xn_all = sb("n_xn_all", [P, T, D], F32, st)
                xT = sb("n_xT", [P, N], F32, st)
                pick = sb("n_pick", [P, T, 8], F32, st)
                wts = sb("n_wts", [P, T, TOPK1], F32, st)
                rank = sb("n_rank", [P, T, E1], F32, st)
                seen = sb("n_seen", [P, E1], F32, st)
                pos_i = sb("n_pos_i", [P, T, TOPK1], I32, st)
                erow = sb("n_erow", [1, NTILE], I32, st)
                ysorted = nc.dram_tensor("y_sorted", (NTILE * P, D), F32, kind="Internal").ap()
                moe1_router(xn_all, xT, pick, wts, rank, seen)
                moe1_dispatch(xn_all, xT, pick, rank, seen, pos_i, erow, sorted_x, zeros_out)
                moe1_tiles(wexp, erow, sorted_x, ysorted, wexp_in)
                moe1_combine(pos_i, wts, ysorted)

        def moe1_router(xn_all, xT, pick, wts, rank, seen):
            with ExitStack() as st:
                stats = sb("s_stats", [P, QT, 6], F32, st)
                mv = sb("s_mv", [P, QT, 2], F32, st)
                rstd = sb("s_rstd", [P, QT], F32, st)
                neghalf = sb("s_neghalf", [P, QT], F32, st)
                xn = sb("s_xn", [P, QT, D], F32, st)
                xs = sb("s_xs", [P, QN], F32, st)
                nmx = sb("s_nmx", [P, QT], F32, st)
                ex = sb("s_ex", [P, QT, E1], F32, st)
                top = sb("s_top", [P, QT, 8], F32, st)
                topi = sb("s_topi", [P, QT, 8], U32, st)
                topf = sb("s_topf", [P, QT, 8], F32, st)
                tot = sb("s_tot", [P, QT], F32, st)
                eq = sb("s_eq", [P, QT, TOPK1, E1], F32, st)
                chosen = sb("s_chosen", [P, QT, E1], F32, st)
                more = sb("s_more", [P, E1], F32, st)
                var_ready = sem("s_var_ready")
                rstd_ready = sem("s_rstd_ready")
                xn_ready = sem("s_xn_ready")
                turned = sem("s_turned")
                xs_ready = sem("s_xs_ready")
                xT_stored = sem("s_xT_stored")
                logit_mm = sem("s_logit_mm")
                nmx_ready = sem("s_nmx_ready")
                ex_ready = sem("s_ex_ready")
                chosen_ready = sem("s_chosen_ready")
                rank_mm = sem("s_rank_mm")
                block = st.enter_context(nc.Block())

                @block.vector
                def _(dve):
                    dve.memset(seen[:, :], 0.0)
                    dve.drain()
                    with dve.Fori(0, NQ) as i:
                        ln_stats(dve, stats, mv, rstd, QT, i, var_ready)
                        dve.wait_ge(rstd_ready, i + 1)
                        ln_apply(dve, xn, mv, rstd, QT, i).then_inc(xn_ready, 1)
                        dve.drain()
                        dve.tensor_tensor(h[:, ds(i * QT, QT), :], h[:, ds(i * QT, QT), :], xn[:, :, :], ALU.add)
                        dve.wait_ge(logit_mm, i + 1)
                        lg = ps[:, 1, 0:QT * E1].rearrange("p (t e) -> p t e", t=QT)
                        dve.tensor_reduce(nmx[:, :], lg, AX.X, ALU.max)
                        dve.drain()
                        dve.tensor_scalar(nmx[:, :], nmx[:, :], -1.0, None, ALU.mult).then_inc(nmx_ready, 1)
                        dve.wait_ge(ex_ready, i + 1)
                        dve.memset(carrier[:, :], 0.0)
                        for j in range(QT):
                            dve.max(top[:, j, :], ex[:, j, :])
                        dve.drain()
                        for j in range(QT):
                            dve.max_index(topi[:, j, :], top[:, j, :], ex[:, j, :])
                        dve.tensor_reduce(tot[:, :], top[:, :, 0:TOPK1], AX.X, ALU.add)
                        dve.drain()
                        dve.reciprocal(tot[:, :], tot[:, :])
                        dve.tensor_copy(topf[:, :, :], topi[:, :, :])
                        dve.drain()
                        dve.tensor_tensor(wts[:, ds(i * QT, QT), :], top[:, :, 0:TOPK1],
                                          tot[:, :].unsqueeze(2).to_broadcast([P, QT, TOPK1]), ALU.mult)
                        dve.tensor_copy(pick[:, ds(i * QT, QT), :], topf[:, :, :])
                        for j in range(QT):
                            dve.tensor_tensor(eq[:, j], C("iota")[:, 0:E1].unsqueeze(1).to_broadcast([P, TOPK1, E1]),
                                              topf[:, j, 0:TOPK1].unsqueeze(2).to_broadcast([P, TOPK1, E1]),
                                              ALU.is_equal)
                        dve.drain()
                        dve.tensor_reduce(chosen[:, :, :], eq[:, :, :, :].rearrange("p t k e -> p t e k"), AX.X,
                                          ALU.add).then_inc(chosen_ready, 1)
                        dve.drain()
                        dve.tensor_reduce(more[:, :], chosen[:, :, :].rearrange("p t e -> p e t"), AX.X, ALU.add)
                        dve.wait_ge(rank_mm, i + 1)
                        dve.tensor_copy(rank[:, ds(i * QT, QT), :],
                                        ps[:, 2, 0:QT * E1].rearrange("p (t e) -> p t e", t=QT))
                        dve.drain()
                        dve.tensor_tensor(seen[:, :], seen[:, :], more[:, :], ALU.add)
                        dve.drain()

                @block.gpsimd
                def _(pool):
                    pool.memset(neghalf[:, :], -0.5)
                    pool.drain()
                    with pool.Fori(0, NQ) as i:
                        pool.wait_ge(var_ready, i + 1)
                        ln_rstd(pool, rstd, neghalf, QT).then_inc(rstd_ready, 1)
                        pool.wait_ge(xn_ready, i + 1)
                        pool.tensor_copy(xn_all[:, ds(i * QT, QT), :], xn[:, :, :])
                        pool.wait_ge(xs_ready, i + 1)
                        pool.tensor_copy(xT[:, ds(i * QN, QN)], xs[:, :]).then_inc(xT_stored, 1)

                @block.scalar
                def _(act):
                    act.preload_act_table(ACT.Exp)
                    act.sem_inc(xT_stored, 1)
                    with act.Fori(0, NQ) as i:
                        act.wait_ge(xT_stored, i + 1)
                        act.wait_ge(turned, i + 1)
                        act.copy(xs[:, :], ps[:, 0, :]).then_inc(xs_ready, 1)
                        act.wait_ge(nmx_ready, i + 1)
                        for j in range(QT):
                            last = act.activation(ex[:, j, :], ps[:, 1, j * E1:(j + 1) * E1], ACT.Exp,
                                                  bias=nmx[:, j:j + 1])
                        last.then_inc(ex_ready, 1)

                @block.tensor
                def _(pe):
                    with pe.Fori(0, NQ) as i:
                        pe.wait_ge(xn_ready, i + 1)
                        for j in range(QT):
                            last = pe.transpose(ps[:, 0, j * P:(j + 1) * P], xn[:, j, :], ident)
                        last.then_inc(turned, 1)
                        pe.wait_ge(xs_ready, i + 1)
                        for j in range(QT):
                            last = pe.matmul(ps[:, 1, j * E1:(j + 1) * E1], xs[:, j * P:(j + 1) * P], W("wr1"),
                                             start=True, stop=True)
                        last.then_inc(logit_mm, 1)
                        pe.wait_ge(chosen_ready, i + 1)
                        for j in range(QT):
                            dst = ps[:, 2, j * E1:(j + 1) * E1]
                            pe.matmul(dst, C("full"), seen[:, :], start=True, stop=False)
                            for before in range(j):
                                pe.matmul(dst, C("full"), chosen[:, before, :], start=False, stop=False)
                            last = pe.matmul(dst, C("earlier"), chosen[:, j, :], start=False, stop=True)
                        last.then_inc(rank_mm, 1)

        def moe1_dispatch(xn_all, xT, pick, rank, seen, pos_i, erow, sorted_x, zeros_out):
            with ExitStack() as st:
                tiles_f = sb("d_tiles_f", [P, E1], F32, st)
                tiles_i = sb("d_tiles_i", [P, E1], I32, st)
                ends = sb("d_ends", [P, E1], F32, st)
                base = sb("d_base", [P, E1], F32, st)
                junk = sb("d_junk", [P, E1], F32, st)
                end_col = sb("d_end_col", [E1, 1], F32, st)
                past = sb("d_past", [E1, NTILE], F32, st)
                pos = sb("d_pos", [P, T, TOPK1], F32, st)
                pick_junk = sb("d_pick_junk", [P, T, TOPK1, E1], F32, st)
                wsh = sb("d_wsh", [P, NS1, W1COLS], F32, st)
                act1 = sb("d_act1", [P, 2, QN], F32, st)
                a = sb("d_a", [P, 2, QN], F32, st)
                wsh_in = sem("d_wsh_in")
                count_mm = sem("d_count_mm")
                past_ready = sem("d_past_ready")
                erow_mm = sem("d_erow_mm")
                pos_ready = sem("d_pos_ready")
                scattered = sem("d_scattered")
                hid_mm = sem("d_hid_mm")
                silu_done = sem("d_silu_done")
                a_ready = sem("d_a_ready")
                y_mm = sem("d_y_mm")
                y_used = sem("d_y_used")
                SH = NS1 * NQ
                block = st.enter_context(nc.Block())

                @block.sync
                def _(sp):
                    sp.dma_start(wsh[:, :, :], w1[:, E1:EXP1, :]).then_inc(wsh_in, 16)

                @block.vector
                def _(dve):
                    dve.wait_ge(count_mm, 1)
                    dve.tensor_scalar(tiles_i[:, :], ps[:, 6, 0:E1], 63.5, 1.0 / P, ALU.add, ALU.mult)
                    dve.drain()
                    dve.tensor_copy(tiles_f[:, :], tiles_i[:, :])
                    dve.drain()
                    dve.tensor_tensor_scan(ends[:, :], C("ones")[:, 0:E1], tiles_f[:, :], 0.0, ALU.mult, ALU.add)
                    dve.drain()
                    dve.tensor_tensor(base[:, :], ends[:, :], tiles_f[:, :], ALU.subtract)
                    dve.scalar_tensor_tensor(junk[0:E1, :], ends[0:E1, :], 1.0, ident[0:E1, 0:E1], ALU.mult, ALU.mult,
                                             accum_out=end_col[:, :])
                    dve.drain()
                    dve.tensor_scalar(base[:, :], base[:, :], float(P), None, ALU.mult)
                    dve.tensor_scalar(past[:, :], C("iota_tiles", E1), end_col[:, :], None,
                                      ALU.is_ge).then_inc(past_ready, 1)
                    dve.drain()
                    dve.tensor_tensor(rank[:, :, :], rank[:, :, :], base[:, :].unsqueeze(1).to_broadcast([P, T, E1]),
                                      ALU.add)
                    dve.drain()
                    for q in range(NQ):
                        for t in range(q * QT, (q + 1) * QT):
                            for k in range(TOPK1):
                                dve.scalar_tensor_tensor(pick_junk[:, t, k, :], C("iota")[:, 0:E1], pick[:, t, k:k + 1],
                                                         rank[:, t, :], ALU.is_equal, ALU.mult,
                                                         accum_out=pos[:, t, k:k + 1])
                        dve.drain()
                        dve.tensor_copy(pos_i[:, q * QT:(q + 1) * QT, :],
                                        pos[:, q * QT:(q + 1) * QT, :]).then_inc(pos_ready, 1)
                    dve.wait_ge(erow_mm, 1)
                    dve.tensor_scalar(erow[:, :], ps[0:1, 7, 0:NTILE], float(E1 - 1), float(W1COLS),
                                      ALU.min, ALU.mult)

                    def combine(n):
                        dve.wait_ge(y_mm, n + 1)
                        c = n % NQ
                        hq = h[:, c * QT:(c + 1) * QT, :].rearrange("p t d -> p (t d)")
                        dve.tensor_tensor(hq, hq, ps[:, 4 + n % 2, :], ALU.add).then_inc(y_used, 1)

                    for n in range(SH):
                        dve.wait_ge(silu_done, n + 1)
                        if n >= 2:
                            dve.wait_ge(y_mm, n - 1)
                        dve.tensor_tensor(a[:, n % 2, :], act1[:, n % 2, :], ps[:, 2 * (n % 2) + 1, :],
                                          ALU.mult).then_inc(a_ready, 1)
                        if n:
                            combine(n - 1)
                    combine(SH - 1)

                @block.gpsimd
                def _(pool):
                    pool.wait_ge(zeros_out, 16 * ZFILLS)
                    for t in range(T):
                        if t % QT == 0:
                            pool.wait_ge(pos_ready, t // QT + 1)
                        for k in range(TOPK1):
                            pool.indirect_dma_start(sorted_x, bass.IndirectOffsetOnAxis(ap=pos_i[:, t, k:k + 1], axis=0),
                                                    xn_all[:, t, :], None).then_inc(scattered, 16)
                    pool.wait_ge(scattered, 16 * T * TOPK1)

                @block.scalar
                def _(act):
                    act.preload_act_table(ACT.Silu)
                    for n in range(SH):
                        act.wait_ge(hid_mm, n + 1)
                        if n >= 2:
                            act.wait_ge(a_ready, n - 1)
                        act.activation(act1[:, n % 2, :], ps[:, 2 * (n % 2), :], ACT.Silu).then_inc(silu_done, 1)

                @block.tensor
                def _(pe):
                    pe.matmul(ps[:, 6, 0:E1], C("full"), seen[:, :], start=True, stop=True).then_inc(count_mm, 1)

                    def hidden(n):
                        e, c = n // NQ, n % NQ
                        if n >= 2:
                            pe.wait_ge(a_ready, n - 1)
                        for part in range(2):
                            last = pe.matmul(ps[:, 2 * (n % 2) + part, :], wsh[:, e, part * D:(part + 1) * D],
                                             xT[:, c * QN:(c + 1) * QN], start=True, stop=True)
                        last.then_inc(hid_mm, 1)

                    def output(n):
                        e = n // NQ
                        pe.wait_ge(a_ready, n + 1)
                        if n >= 2:
                            pe.wait_ge(y_used, n - 1)
                        for j in range(QT):
                            last = pe.matmul(ps[:, 4 + n % 2, j * D:(j + 1) * D], a[:, n % 2, j * P:(j + 1) * P],
                                             wsh[:, e, 2 * D:3 * D], start=True, stop=True)
                        last.then_inc(y_mm, 1)

                    pe.wait_ge(past_ready, 1)
                    pe.matmul(ps[0:1, 7, 0:NTILE], C("ones", E1)[:, 0:1], past[:, :], start=True,
                              stop=True).then_inc(erow_mm, 1)
                    pe.wait_ge(wsh_in, 16)
                    for n in range(SH):
                        hidden(n)
                        if n:
                            output(n - 1)
                    output(SH - 1)

        def moe1_tiles(wexp, erow, sorted_x, ysorted, wexp_in):
            with ExitStack() as st:
                xin = sb("t_xin", [P, 2, QT, D], F32, st)
                xT = sb("t_xT", [P, 2, QT, P], F32, st)
                act1 = sb("t_act1", [P, 2, QT, F1], F32, st)
                a = sb("t_a", [P, 2, QT, F1], F32, st)
                aT = sb("t_aT", [P, 2, QT, P], F32, st)
                y = sb("t_y", [P, 2, QT, D], F32, st)
                x_in = [sem("t_x_in0"), sem("t_x_in1")]
                y_out = [sem("t_y_out0"), sem("t_y_out1")]
                x_turned = sem("t_x_turned")
                xT_ready = sem("t_xT_ready")
                hid_mm = sem("t_hid_mm")
                silu_done = sem("t_silu_done")
                a_ready = sem("t_a_ready")
                a_turned = sem("t_a_turned")
                aT_ready = sem("t_aT_ready")
                down_mm = sem("t_down_mm")
                y_ready = sem("t_y_ready")
                NG = NTILE // QT
                wflat = wexp[:, :, :].rearrange("p e c -> p (e c)")
                block = st.enter_context(nc.Block())
                xg = sorted_x.rearrange("(n p) d -> p n d", p=P)
                yg = ysorted.rearrange("(n p) d -> p n d", p=P)

                def run(eng, step):
                    for m in range(4):
                        step(m, m % 2, m // 2)
                    with eng.Fori(0, NG // 2 - 3) as pair:
                        step(pair * 2 + 4, 0, pair + 2)
                        step(pair * 2 + 5, 1, pair + 2)
                    step(NG - 2, 0, NG // 2 - 1)
                    step(NG - 1, 1, NG // 2 - 1)
                    step(NG, 0, NG // 2)
                    step(NG + 1, 1, NG // 2)

                def isnum(m, lo, hi):
                    return isinstance(m, int) and lo <= m <= hi

                @block.sync
                def _(sp):
                    def load(m, s):
                        sp.dma_start(xin[:, s], xg[:, ds(m * QT, QT), :]).then_inc(x_in[s], 16)

                    def step(m, s, r):
                        if not isnum(m, NG - 2, NG + 1):
                            sp.wait_ge(x_turned, m + 1)
                            load(m + 2, s)
                        if not isnum(m, 0, 1):
                            sp.wait_ge(y_ready, m - 1)
                            sp.dma_start(yg[:, ds((m - 2) * QT, QT), :], y[:, s]).then_inc(y_out[s], 16)

                    load(0, 0)
                    load(1, 1)
                    run(sp, step)
                    for s in range(2):
                        sp.wait_ge(y_out[s], 16 * (NG // 2))

                @block.tensor
                def _(pe):
                    def turn(m, s, r):
                        pe.wait_ge(x_in[s], r * 16 + 16)
                        if not isnum(m, 0, 0):
                            pe.wait_ge(xT_ready, m)
                        for j in range(QT):
                            last = pe.transpose(ps[:, 0, j * P:(j + 1) * P], xin[:, s, j, :], ident)
                        last.then_inc(x_turned, 1)

                    def experts(m):
                        _, starts = nc.values_load_multi_w_load_instructions(
                            erow[0:1, ds(m * QT, QT)], engines=(mybir.EngineType.PE,), min_val=0,
                            max_val=(E1 - 1) * W1COLS,
                            skip_runtime_bounds_check_because="the row holds min(count, E1 - 1) * W1COLS, count >= 0")
                        return starts

                    def step(m, s, r):
                        if not isnum(m, NG, NG + 1):
                            pe.wait_ge(xT_ready, m + 1)
                            if not isnum(m, 0, 1):
                                pe.wait_ge(a_ready, m - 1)
                            starts = experts(m)
                            for j in range(QT):
                                last = pe.matmul(ps[:, 2 + 2 * s + j // 2, (j % 2) * 2 * F1:(j % 2 + 1) * 2 * F1],
                                                 xT[:, s, j, :], wflat[:, ds(starts[j], 2 * F1)], start=True, stop=True)
                            last.then_inc(hid_mm, 1)
                        if not isnum(m, 0, 0) and not isnum(m, NG + 1, NG + 1):
                            pe.wait_ge(a_ready, m)
                            if not isnum(m, 1, 1):
                                pe.wait_ge(aT_ready, m - 1)
                            for j in range(QT):
                                last = pe.transpose(ps[:, 1, j * P:(j + 1) * P], a[:, 1 - s, j, :], ident)
                            last.then_inc(a_turned, 1)
                        if not isnum(m, NG - 1, NG + 1):
                            turn(m + 1, 1 - s, r + s)
                        if not isnum(m, 0, 1):
                            pe.wait_ge(aT_ready, m - 1)
                            if not isnum(m, 2, 3):
                                pe.wait_ge(y_ready, m - 3)
                            starts = experts(m - 2)
                            for j in range(QT):
                                last = pe.matmul(ps[:, 6 + s, j * D:(j + 1) * D], aT[:, s, j, :],
                                                 wflat[:, ds(starts[j] + 2 * F1, D)], start=True, stop=True)
                            last.then_inc(down_mm, 1)

                    pe.wait_ge(wexp_in, 16 * WLOADS)
                    turn(0, 0, 0)
                    run(pe, step)

                @block.scalar
                def _(act):
                    def take_xT(m, s):
                        act.wait_ge(x_turned, m + 1)
                        if not isnum(m, 0, 1):
                            act.wait_ge(hid_mm, m - 1)
                        act.copy(xT[:, s].rearrange("p t q -> p (t q)"), ps[:, 0, :]).then_inc(xT_ready, 1)

                    def step(m, s, r):
                        if not isnum(m, NG, NG + 1):
                            act.wait_ge(hid_mm, m + 1)
                            if not isnum(m, 0, 1):
                                act.wait_ge(a_ready, m - 1)
                            gate = ps[:, 2 + 2 * s:4 + 2 * s, :].rearrange("p b (t c) -> p (b t) c", t=2)[:, :, 0:F1]
                            act.activation(act1[:, s], gate, ACT.Silu).then_inc(silu_done, 1)
                        if not isnum(m, NG - 1, NG + 1):
                            take_xT(m + 1, 1 - s)
                        if not isnum(m, 0, 1):
                            act.wait_ge(down_mm, m - 1)
                            if not isnum(m, 2, 3):
                                act.wait_ge(y_out[s], r * 16 - 16)
                            act.copy(y[:, s].rearrange("p t d -> p (t d)"), ps[:, 6 + s, :]).then_inc(y_ready, 1)

                    act.preload_act_table(ACT.Silu)
                    take_xT(0, 0)
                    run(act, step)

                @block.vector
                def _(dve):
                    def step(m, s, r):
                        if not isnum(m, 0, 0) and not isnum(m, NG + 1, NG + 1):
                            dve.wait_ge(a_turned, m)
                            if not isnum(m, 1, 2):
                                dve.wait_ge(down_mm, m - 2)
                            dve.tensor_copy(aT[:, 1 - s].rearrange("p t q -> p (t q)"), ps[:, 1, :]
                                            ).then_inc(aT_ready, 1)
                        if not isnum(m, NG, NG + 1):
                            dve.wait_ge(silu_done, m + 1)
                            if not isnum(m, 0, 1):
                                dve.wait_ge(a_turned, m - 1)
                            up = ps[:, 2 + 2 * s:4 + 2 * s, :].rearrange("p b (t c) -> p (b t) c", t=2)[:, :, F1:2 * F1]
                            dve.tensor_tensor(a[:, s], act1[:, s], up, ALU.mult).then_inc(a_ready, 1)

                    run(dve, step)

        def moe1_combine(pos_i, wts, ysorted):
            with ExitStack() as st:
                SLOTS = 4
                got = sb("g_got", [P, SLOTS, TOPK1, D], F32, st)
                got_in = [sem(f"g_got_in{s}") for s in range(SLOTS)]
                added = sem("g_added")
                out_done = sem("g_out_done")
                block = st.enter_context(nc.Block())

                @block.gpsimd
                def _(pool):
                    for t in range(T):
                        if t >= SLOTS:
                            pool.wait_ge(added, t - SLOTS + 1)
                        for k in range(TOPK1):
                            pool.indirect_dma_start(got[:, t % SLOTS, k, :], None, ysorted,
                                                    bass.IndirectOffsetOnAxis(ap=pos_i[:, t, k:k + 1], axis=0)
                                                    ).then_inc(got_in[t % SLOTS], 16)

                @block.vector
                def _(dve):
                    for t in range(T):
                        dve.wait_ge(got_in[t % SLOTS], 16 * TOPK1 * (t // SLOTS + 1))
                        for k in range(TOPK1):
                            last = dve.scalar_tensor_tensor(h[:, t, :], got[:, t % SLOTS, k, :], wts[:, t, k:k + 1],
                                                            h[:, t, :], ALU.mult, ALU.add)
                            if k < TOPK1 - 1:
                                dve.drain()
                        last.then_inc(added, 1)

                @block.sync
                def _(sp):
                    for q in range(NQ):
                        sp.wait_ge(added, QT * (q + 1))
                        sp.dma_start(out[:, q * QT:(q + 1) * QT, :], h[:, q * QT:(q + 1) * QT, :]).then_inc(out_done, 16)
                    sp.wait_ge(out_done, 16 * NQ)

        token_stage()
        gla_stage()
        wexp = sb("wexp", [P, E1, W1COLS])
        zeros = sb("zeros", [P, ZCOLS])
        sorted_x = nc.dram_tensor("x_sorted", (NTILE * P, D), F32, kind="Internal").ap()
        zeros_out = sem("zeros_out")
        wexp_in = sem("wexp_in")
        moe0_stage(wexp, zeros, sorted_x, zeros_out, wexp_in)
        attention_stage()
        moe1_stage(wexp, sorted_x, zeros_out, wexp_in)


def layouts(inputs):
    import numpy as np

    g = {k: np.asarray(v) for k, v in inputs.items()}
    weights = np.zeros((P, WCOLS), np.float32)

    def put(name, a):
        o, n = _cols[name]
        assert a.shape[1] == n, (name, a.shape)
        weights[0:a.shape[0], o:o + n] = a

    put("tok_w", g["L0_tok_expert_w"].transpose(2, 0, 1).reshape(D, E_TOK * D))
    put("tok_b", g["L0_tok_expert_b"])
    put("wk", g["L0_attn_Wk"].T)
    put("wq", g["L0_attn_Wq"].T)
    put("wv", g["L0_attn_Wv"].T)
    put("wo0", g["L0_attn_Wo"].T)
    put("wg1", g["L0_attn_Wg1"].T)
    put("wg2", g["L0_attn_Wg2"].T)
    for z in "kqv":
        put("conv_" + z, g["L0_attn_conv_" + z][:, 0, :])
    put("bg2", g["L0_attn_bg2"][:, None])
    put("norm_w", g["L0_attn_norm_w"][:, None])
    put("rw0", g["L0_ffn_router_w"].T)
    put("rb0", g["L0_ffn_router_b"][None])
    put("fc2_b", g["L0_ffn_fc2_b"])
    qkv, bqkv = g["L1_attn_Wqkv"], g["L1_attn_bqkv"]
    for name, bname, part in (("aq", "abq", 0), ("ak", "abk", 1)):
        w = qkv[:, part * D:(part + 1) * D].reshape(D, 2, 4, DH)
        b = bqkv[part * D:(part + 1) * D].reshape(2, 4, DH)
        put(name, np.pad(w, ((0, 0), (0, 0), (0, 0), (0, 32 - DH))).reshape(D, 2 * P))
        put(bname, np.pad(b, ((0, 0), (0, 0), (0, 32 - DH))).reshape(2, P).T)
    put("av", qkv[:, 2 * D:3 * D])
    put("abv", bqkv[None, 2 * D:3 * D])
    put("awo", g["L1_attn_Wo"])
    put("abo", g["L1_attn_bo"][None])
    put("wr1", g["L1_ffn_Wr"])

    consts = np.zeros((P, CCOLS), np.float32)

    def cput(name, a):
        o, n = _ccols[name]
        consts[:, o:o + n] = a

    cput("ident", np.eye(P))
    cput("iota", np.arange(P)[None])
    cput("reset", (np.arange(QN) % CHUNK != 0)[None])
    cput("ones", 1.0)
    cput("full", 1.0)
    cput("earlier", np.triu(np.ones((P, P)), 1))
    cput("iota_tiles", np.arange(NTILE)[None])
    step = D // E_TOK
    cput("thr", np.tile([-3.0e38] + [step * e - 1 for e in range(1, E_TOK)] + [3.0e38], QT)[None])
    j, i = np.arange(P)[:, None], np.arange(P)[None]
    causal = ((j <= i) & (j // CHUNK == i // CHUNK)).astype(np.uint32)

    fc1 = g["L0_ffn_fc1_w"].transpose(2, 0, 1)
    fc2 = g["L0_ffn_fc2_w"].reshape(E0, D, 2, P).transpose(3, 0, 2, 1).reshape(P, E0, 2 * D)
    b1 = g["L0_ffn_fc1_b"].reshape(E0, 4, P).transpose(2, 0, 1)
    w0 = np.concatenate([fc1, fc2, b1], axis=2)
    w1 = np.concatenate([
        np.concatenate([g["L1_ffn_Wg"], g["L1_ffn_sWg"]]), np.concatenate([g["L1_ffn_Wu"], g["L1_ffn_sWu"]]),
        np.concatenate([g["L1_ffn_Wd"], g["L1_ffn_sWd"]])], axis=2).transpose(1, 0, 2)
    return {
        "ids": g["x"].reshape(T, P).T,
        "emb_gate": np.concatenate([g["L0_tok_emb_table"], g["L0_tok_gate_table"]], axis=1),
        "weights": weights,
        "consts": consts,
        "causal": causal,
        "rel": g["L1_attn_rel_pos_bias"].T,
        "w0": w0,
        "w1": w1,
    }


def kernel(**inputs):
    import numpy as np
    import concourse.bacc as bacc
    from concourse.bass_utils import run_bass_kernel_spmd

    nc = bacc.Bacc("TRN2", target_bir_lowering=False, num_devices=1)
    arrays, args = {}, []
    for name, a in layouts(inputs).items():
        a = np.ascontiguousarray(a)
        arrays["in_" + name] = a
        args.append(nc.dram_tensor("in_" + name, a.shape, mybir.dt.from_np(a.dtype), kind="ExternalInput").ap())
    out = nc.dram_tensor("out_0", (P, T, D), F32, kind="ExternalOutput").ap()
    tower_kernel(nc, *args, out)
    r = run_bass_kernel_spmd(nc, [arrays], core_ids=[0])
    return r.results[0]["out_0"].transpose(1, 0, 2).reshape(B, L, D)
```

```python
from contextlib import ExitStack

import concourse.bass as bass
from concourse import mybir
from concourse.alu_op_type import AluOpType as ALU

F32 = mybir.dt.float32
I32 = mybir.dt.int32
U32 = mybir.dt.uint32
F16 = mybir.dt.float16
ACT = mybir.ActivationFunctionType
AX = mybir.AxisListType
ds = bass.ds

P = 128
D = 128
B, L = 8, 256
N = B * L
T = N // P
QT = 4
QN = QT * P
NQ = T // QT
SQ = QN // L
EPS_LN = 1e-5

E_TOK = 5
CHUNK = 64
NC_SEQ = L // CHUNK
GATE_NORM = 16.0
TAPS = 4
RANK = 16

E0, F0 = 8, 256
W0COLS = 2 * F0 + 2 * D + 4
HEADS, DH, WIN = 8, 16, 64
KW = P + WIN
NEG = -1.0e30

E1, F1, TOPK1, NS1 = 64, 128, 6, 2
EXP1 = E1 + NS1
W1COLS = 3 * D
NTILE = -(-((N * TOPK1 - E1) // P + E1) // (2 * QT)) * 2 * QT
WLOADS = 8

_cols = {}
WCOLS = 0
for _name, _n in (("tok_w", E_TOK * D), ("tok_b", D), ("wk", D), ("wq", D), ("wv", D), ("wo0", D), ("wg1", RANK),
                  ("wg2", D), ("conv_k", TAPS), ("conv_q", TAPS), ("conv_v", TAPS), ("bg2", 1), ("norm_w", 1),
                  ("rw0", E0), ("rb0", E0), ("fc2_b", D), ("aq", 2 * P), ("ak", 2 * P), ("av", D), ("abq", 2),
                  ("abk", 2), ("abv", D), ("awo", D), ("abo", D), ("wr1", E1)):
    _cols[_name] = (WCOLS, _n)
    WCOLS += _n
_ccols = {}
CCOLS = 0
for _name, _n in (("ident", P), ("iota", P), ("reset", QN), ("ones", P), ("full", P), ("earlier", P), ("iota_tiles", NTILE), ("token", T), ("thr", QT * (E_TOK + 1))):
    _ccols[_name] = (CCOLS, _n)
    CCOLS += _n


def tower_kernel(nc, ids, emb_gate, weights, consts, causal, rel, w0, w1, out):
    ctx = ExitStack()
    with ctx:
        def sb(name, shape, dt=F32, scope=ctx):
            return scope.enter_context(nc.sbuf_tensor(name, shape, dt))

        def sem(name):
            return ctx.enter_context(nc.semaphore(name))

        ps = ctx.enter_context(nc.psum_tensor("ps", [P, 8, 512], F32))
        h = sb("h", [P, T, D])
        wsb = sb("wsb", [P, WCOLS])
        csb = sb("csb", [P, CCOLS])
        causal_sb = sb("causal_sb", [P, P], U32)
        band = sb("band", [P, HEADS, KW])
        carrier = sb("carrier", [P, 1])

        def W(name, rows=P):
            o, n = _cols[name]
            return wsb[0:rows, o:o + n]

        def C(name, rows=P):
            o, n = _ccols[name]
            return csb[0:rows, o:o + n]

        ident = C("ident")
        ones_col = C("ones")[:, 0:1]
        ones_row = C("ones", 1)

        loaded = sem("loaded")
        band_made = sem("band_made")

        def ln_stats(dve, stats, mv, rstd, tiles, i, var_ready):
            for j in range(tiles):
                dve.bn_stats(stats[:, j, :], h[:, ds(i * tiles + j, 1), :])
            dve.drain()
            for j in range(tiles):
                dve.bn_aggr(mv[:, j, :], stats[:, j, :])
            dve.drain()
            dve.tensor_scalar(rstd[:, 0:tiles], mv[:, 0:tiles, 1], EPS_LN, None, ALU.add).then_inc(var_ready, 1)

        def ln_rstd(pool, rstd, neghalf, tiles):
            return pool.tensor_tensor(rstd[:, 0:tiles], rstd[:, 0:tiles], neghalf[:, 0:tiles], ALU.pow)

        def ln_apply(dve, xn, mv, rstd, tiles, i):
            for j in range(tiles):
                last = dve.tensor_scalar(xn[:, j, :], h[:, ds(i * tiles + j, 1), :], mv[:, j, 0:1], rstd[:, j:j + 1],
                                         ALU.subtract, ALU.mult)
            return last

        def token_stage():
            with ExitStack() as st:
                idx = sb("idx", [P, T], I32, st)
                emb = sb("emb", [P, T, D + 1], F32, st)
                gate = sb("gate", [P, NQ, QT], F32, st)
                scaled = sb("scaled", [P, NQ, QT], F32, st)
                whole_i = sb("whole_i", [P, NQ, QT], I32, st)
                whole = sb("whole", [P, NQ, QT], F32, st)
                frac = sb("frac", [P, NQ, QT], F32, st)
                above = sb("above", [P, NQ, QT, E_TOK + 1], F32, st)
                onehot = sb("onehot", [P, NQ, QT, E_TOK], F32, st)
                mask = sb("mask", [P, QT, D], F32, st)
                xm = sb("xm", [P, 2, QT, D], F32, st)
                xmT = sb("xmT", [P, 2, QN], F32, st)
                ohT = sb("ohT", [E_TOK, 2, QN], F32, st)
                ids_in = sem("ids_in")
                emb_in = [sem(f"emb_in{q}") for q in range(NQ)]
                xm_ready = sem("xm_ready")
                turned = sem("tok_turned")
                moved = sem("tok_moved")
                tok_mm = sem("tok_mm")
                bias_in_h = sem("bias_in_h")
                h_ready = sem("tok_h_ready")
                neg_fill = sem("neg_fill")
                neg_out = sem("neg_out")
                diag_out = sem("diag_out")
                thr = C("thr").rearrange("p (t e) -> p t e", t=QT)
                scratch = nc.dram_tensor("band_scratch", (P, HEADS, KW), F32, kind="Internal").ap()

                block = st.enter_context(nc.Block())

                @block.sync
                def _(sp):
                    sp.dma_start(idx[:, :], ids).then_inc(ids_in, 16)
                    sp.dma_start(csb[:, :], consts).then_inc(loaded, 16)
                    sp.dma_start(wsb[:, :], weights).then_inc(loaded, 16)
                    sp.dma_start(causal_sb[:, :], causal).then_inc(loaded, 16)
                    sp.wait_ge(neg_fill, 1)
                    sp.dma_start(scratch, band[:, :, :]).then_inc(neg_out, 16)
                    sp.wait_ge(neg_out, 16)
                    diagonal = bass.AP(scratch.tensor, 1, [[HEADS * KW + 1, P], [KW, HEADS], [1, WIN]])
                    source = bass.AP(rel.tensor, 0, [[0, P], [WIN, HEADS], [1, WIN]])
                    sp.dma_start(diagonal, source).then_inc(diag_out, 16)
                    sp.wait_ge(diag_out, 16)
                    sp.dma_start(band[:, :, :], scratch).then_inc(band_made, 16)

                @block.gpsimd
                def _(pool):
                    pool.wait_ge(ids_in, 16)
                    for t in range(T):
                        pool.indirect_dma_start(emb[:, t, :], None, emb_gate,
                                                bass.IndirectOffsetOnAxis(ap=idx[:, t:t + 1], axis=0)
                                                ).then_inc(emb_in[t // QT], 16)
                        if t == 0:
                            pool.memset(band[:, :, :], NEG).then_inc(neg_fill, 1)

                def select(dve, q):
                    dve.wait_ge(tok_mm, q + 1)
                    dve.wait_ge(bias_in_h, q + 1)
                    for e in range(E_TOK):
                        for j in range(QT):
                            y = ps[:, j, e * D:(e + 1) * D] if e < 4 else ps[:, 4, j * D:(j + 1) * D]
                            t = QT * q + j
                            last = dve.scalar_tensor_tensor(h[:, t, :], y, onehot[:, q, j, e:e + 1], h[:, t, :],
                                                            ALU.mult, ALU.add)
                        if e < E_TOK - 1:
                            dve.drain()
                    last.then_inc(h_ready, 1)

                @block.vector
                def _(dve):
                    dve.wait_ge(loaded, 48)
                    for q in range(NQ):
                        dve.wait_ge(emb_in[q], 16 * QT)
                        raw = emb[:, QT * q:QT * (q + 1), D]
                        dve.tensor_scalar(gate[:, q, :], raw, float(D), None, ALU.mult)
                        dve.drain()
                        dve.tensor_scalar(scaled[:, q, :], gate[:, q, :], 1.0e9, float(2 ** 23), ALU.mult, ALU.min)
                        dve.tensor_tensor(above[:, q], gate[:, q, :].unsqueeze(2).to_broadcast([P, QT, E_TOK + 1]),
                                          thr, ALU.is_gt)
                        dve.drain()
                        dve.tensor_copy(whole_i[:, q, :], scaled[:, q, :])
                        dve.tensor_tensor(onehot[:, q], above[:, q, :, 0:E_TOK], above[:, q, :, 1:E_TOK + 1],
                                          ALU.subtract)
                        dve.drain()
                        dve.tensor_copy(whole[:, q, :], whole_i[:, q, :])
                        dve.drain()
                        dve.tensor_tensor(frac[:, q, :], scaled[:, q, :], whole[:, q, :], ALU.subtract)
                        dve.drain()
                        dve.scalar_tensor_tensor(frac[:, q, :], frac[:, q, :], 0.0, frac[:, q, :], ALU.is_lt, ALU.add)
                        dve.drain()
                        dve.tensor_scalar(frac[:, q, :], frac[:, q, :], 1.0e-9, None, ALU.mult)
                        dve.drain()
                        for j in range(QT):
                            dve.tensor_scalar(mask[:, j, :], C("iota"), gate[:, q, j:j + 1], frac[:, q, j:j + 1],
                                              ALU.is_lt, ALU.add)
                        dve.drain()
                        if q >= 2:
                            dve.wait_ge(turned, q - 1)
                        dve.tensor_tensor(xm[:, q % 2], emb[:, QT * q:QT * (q + 1), 0:D], mask[:, :, :],
                                          ALU.mult).then_inc(xm_ready, 1)
                        if q >= 1:
                            select(dve, q - 1)
                    select(dve, NQ - 1)

                @block.tensor
                def _(pe):
                    for q in range(NQ):
                        pe.wait_ge(xm_ready, q + 1)
                        if q >= 1:
                            pe.wait_ge(moved, q)
                        for j in range(QT):
                            pe.transpose(ps[:, 6, j * P:(j + 1) * P], xm[:, q % 2, j, :], ident)
                        for j in range(QT):
                            last = pe.transpose(ps[0:E_TOK, 7, j * P:(j + 1) * P], onehot[:, q, j, :], ident)
                        last.then_inc(turned, 1)
                        pe.wait_ge(moved, q + 1)
                        if q >= 1:
                            pe.wait_ge(h_ready, q)
                            pe.wait_ge(bias_in_h, q)
                        for j in range(QT):
                            x = xmT[:, q % 2, j * P:(j + 1) * P]
                            pe.matmul(ps[:, j, :], x, W("tok_w")[:, 0:4 * D], start=True, stop=True)
                            pe.matmul(ps[:, 4, j * D:(j + 1) * D], x, W("tok_w")[:, 4 * D:5 * D], start=True, stop=True)
                            last = pe.matmul(ps[:, 5, j * D:(j + 1) * D], ohT[:, q % 2, j * P:(j + 1) * P],
                                             W("tok_b", E_TOK), start=True, stop=True)
                        last.then_inc(tok_mm, 1)

                @block.scalar
                def _(act):
                    for q in range(NQ):
                        act.wait_ge(turned, q + 1)
                        act.copy(xmT[:, q % 2, :], ps[:, 6, :])
                        act.copy(ohT[:, q % 2, :], ps[0:E_TOK, 7, :]).then_inc(moved, 1)
                        act.wait_ge(tok_mm, q + 1)
                        act.copy(h[:, QT * q:QT * (q + 1), :],
                                 ps[:, 5, :].rearrange("p (t d) -> p t d", t=QT)).then_inc(bias_in_h, 1)

        def gla_stage():
            with ExitStack() as st:
                kT = sb("kT", [P, N], F32, st)
                qT = sb("qT", [P, N], F32, st)
                vT = sb("vT", [P, N], F32, st)
                gT = sb("gT", [P, N], F32, st)
                gla_projections(kT, qT, vT, gT)
                gla_chunks(kT, qT, vT, gT)

        def gla_projections(kT, qT, vT, gT):
            with ExitStack() as st:
                stats = sb("a_stats", [P, QT, 6], F32, st)
                mv = sb("a_mv", [P, QT, 2], F32, st)
                rstd = sb("a_rstd", [P, QT], F32, st)
                neghalf = sb("a_neghalf", [P, QT], F32, st)
                xn = sb("a_xn", [P, QT, D], F32, st)
                xT = sb("a_xT", [P, QN], F32, st)
                g1 = sb("a_g1", [RANK, QN], F32, st)
                cv = sb("a_cv", [P, 3, SQ, L], F32, st)
                var_ready = sem("a_var_ready")
                rstd_ready = sem("a_rstd_ready")
                xn_ready = sem("a_xn_ready")
                turned = sem("a_turned")
                xT_ready = sem("a_xT_ready")
                projected = sem("a_projected")
                g1_ready = sem("a_g1_ready")
                g_mm = sem("a_g_mm")
                tap_ready = sem("a_tap_ready")
                conv_done = sem("a_conv_done")
                block = st.enter_context(nc.Block())

                def run(eng, quad):
                    with eng.Fori(0, NQ - 1) as i:
                        quad(i, True)
                    quad(NQ - 1, False)

                @block.vector
                def _(dve):
                    def normalise(i):
                        ln_stats(dve, stats, mv, rstd, QT, i, var_ready)
                        dve.wait_ge(turned, i + 1)
                        dve.wait_ge(rstd_ready, i + 1)
                        ln_apply(dve, xn, mv, rstd, QT, i).then_inc(xn_ready, 1)

                    def quad(i, has_next):
                        if has_next:
                            normalise(i + 1)
                        for z, w in enumerate(("conv_k", "conv_q", "conv_v")):
                            dve.wait_ge(tap_ready, i * 3 + z + 1)
                            for back in range(1, TAPS):
                                src = ps[:, 1 + z, :].rearrange("p (s l) -> p s l", s=SQ)[:, :, 0:L - back]
                                dst = cv[:, z, :, back:L]
                                last = dve.scalar_tensor_tensor(dst, src, W(w)[:, TAPS - 1 - back:TAPS - back], dst,
                                                                ALU.mult, ALU.add)
                                if back < TAPS - 1:
                                    dve.drain()
                            last.then_inc(conv_done, 1)

                    normalise(0)
                    run(dve, quad)

                @block.gpsimd
                def _(pool):
                    pool.memset(neghalf[:, :], -0.5)
                    pool.drain()
                    with pool.Fori(0, NQ) as i:
                        pool.wait_ge(var_ready, i + 1)
                        ln_rstd(pool, rstd, neghalf, QT).then_inc(rstd_ready, 1)

                @block.tensor
                def _(pe):
                    def turn(i):
                        pe.wait_ge(xn_ready, i + 1)
                        for j in range(QT):
                            last = pe.transpose(ps[:, 0, j * P:(j + 1) * P], xn[:, j, :], ident)
                        last.then_inc(turned, 1)

                    def quad(i, has_next):
                        pe.wait_ge(xT_ready, i + 1)
                        pe.matmul(ps[0:RANK, 4, :], W("wg1"), xT[:, :], start=True, stop=True).then_inc(projected, 1)
                        for z, w in enumerate(("wk", "wq", "wv")):
                            pe.wait_ge(conv_done, i * 3 + z + 1)
                            pe.matmul(ps[:, 1 + z, :], W(w), xT[:, :], start=True, stop=True).then_inc(projected, 1)
                        pe.wait_ge(g1_ready, i + 1)
                        pe.matmul(ps[:, 5, :], W("wg2", RANK), g1[:, :], start=True, stop=True).then_inc(g_mm, 1)
                        if has_next:
                            turn(i + 1)

                    pe.sem_inc(conv_done, 3)
                    pe.sem_inc(turned, 1)
                    turn(0)
                    run(pe, quad)

                @block.scalar
                def _(act):
                    def take_xT(i):
                        act.wait_ge(turned, i + 2)
                        act.copy(xT[:, :], ps[:, 0, :]).then_inc(xT_ready, 1)

                    def quad(i, has_next):
                        act.wait_ge(projected, i * 4 + 1)
                        act.copy(g1[:, :], ps[0:RANK, 4, :]).then_inc(g1_ready, 1)
                        for z, w in enumerate(("conv_k", "conv_q", "conv_v")):
                            act.wait_ge(projected, i * 4 + 2 + z)
                            act.activation(cv[:, z], ps[:, 1 + z, :].rearrange("p (s l) -> p s l", s=SQ),
                                           ACT.Copy, scale=W(w)[:, TAPS - 1:TAPS]).then_inc(tap_ready, 1)
                        act.wait_ge(g_mm, i + 1)
                        act.activation(gT[:, ds(i * QN, QN)], ps[:, 5, :], ACT.Identity, bias=W("bg2"))
                        if has_next:
                            take_xT(i + 1)
                        for z, dst in enumerate((kT, qT, vT)):
                            act.wait_ge(conv_done, i * 3 + z + 4)
                            act.activation(dst[:, ds(i * QN, QN)], cv[:, z].rearrange("p s l -> p (s l)"), ACT.Silu)
                        act.drain()

                    act.preload_act_table(ACT.Silu)
                    take_xT(0)
                    run(act, quad)

        def gla_chunks(kT, qT, vT, gT):
            with ExitStack() as st:
                v_in = sb("c_v_in", [P, QN], F32, st)
                mag = sb("c_mag", [P, QN], F32, st)
                soft = sb("c_soft", [P, QN], F32, st)
                logsig = sb("c_logsig", [P, QN], F32, st)
                cum = sb("c_cum", [P, QN], F32, st)
                up = sb("c_up", [P, QN], F32, st)
                down = sb("c_down", [P, 2, QN], F32, st)
                sq = sb("c_sq", [P, 2, QN], F32, st)
                qe = sb("c_qe", [P, 2, QN], F32, st)
                ke = sb("c_ke", [P, QN], F32, st)
                norms = sb("c_norms", [P, 2 * QT], F32, st)
                inv = sb("c_inv", [P, 2, 2 * QT], F32, st)
                half = sb("c_half", [P, 2 * QT], F32, st)
                neghalf = sb("c_neghalf", [P, QT], F32, st)
                v_tok = sb("c_v_tok", [P, QT, D], F32, st)
                ke_tok = sb("c_ke_tok", [P, QT, D], F32, st)
                wT = sb("c_wT", [P, QT, P], F32, st)
                state = sb("c_state", [P, NC_SEQ - 1, SQ, D], F32, st)
                oT = sb("c_oT", [P, QN], F32, st)
                osq = sb("c_osq", [P, QN], F32, st)
                ms = sb("c_ms", [P, QT], F32, st)
                fac = sb("c_fac", [P, QT], F32, st)
                v_copied = sem("c_v_copied")
                soft_ready = sem("c_soft_ready")
                cum_ready = sem("c_cum_ready")
                exps_ready = sem("c_exps_ready")
                sq_ready = sem("c_sq_ready")
                qk_ready = sem("c_qk_ready")
                norm_mm = sem("c_norm_mm")
                norms_out = sem("c_norms_out")
                root_ready = sem("c_root_ready")
                v_turned = sem("c_v_turned")
                ke_turned = sem("c_ke_turned")
                v_ready = sem("c_v_ready")
                ke_ready = sem("c_ke_ready")
                w_ready = sem("c_w_ready")
                outer_mm = sem("c_outer_mm")
                state_ready = sem("c_state_ready")
                o_mm = sem("c_o_mm")
                o_ready = sem("c_o_ready")
                ss_mm = sem("c_ss_mm")
                ms_ready = sem("c_ms_ready")
                fac_ready = sem("c_fac_ready")
                out_mm = sem("c_out_mm")
                h_done = sem("c_h_done")
                block = st.enter_context(nc.Block())

                SS = SQ * D

                def run(eng, quad):
                    quad(0, 0, True)
                    with eng.Fori(0, NQ // 2 - 1) as pair:
                        quad(pair * 2 + 1, 1, True)
                        quad(pair * 2 + 2, 0, True)
                    quad(NQ - 1, 1, False)

                def past_first(i):
                    return not isinstance(i, int) or i > 0

                @block.gpsimd
                def _(pool):
                    def copy_v(i):
                        if past_first(i):
                            pool.wait_ge(v_turned, i)
                        pool.tensor_copy(v_in[:, :], vT[:, ds(i * QN, QN)]).then_inc(v_copied, 1)

                    def roots(i):
                        pool.wait_ge(norms_out, i + 1)
                        pool.tensor_tensor(norms[:, :], norms[:, :], half[:, :], ALU.pow)
                        pool.drain()
                        pool.tensor_scalar(norms[:, :], norms[:, :], 1e-5, None, ALU.add).then_inc(root_ready, 1)

                    def quad(i, par, has_next):
                        if has_next:
                            copy_v(i + 1)
                            roots(i + 1)
                        pool.wait_ge(ms_ready, i + 1)
                        pool.tensor_tensor(ms[:, :], ms[:, :], neghalf[:, :], ALU.pow).then_inc(fac_ready, 1)

                    pool.memset(half[:, :], 0.5)
                    pool.memset(neghalf[:, :], -0.5)
                    pool.drain()
                    copy_v(0)
                    roots(0)
                    run(pool, quad)

                @block.scalar
                def _(act):
                    def softplus(i):
                        act.activation(mag[:, :], gT[:, ds(i * QN, QN)], ACT.Abs)
                        act.drain()
                        act.activation(soft[:, :], mag[:, :], ACT.Exp, scale=-1.0)
                        act.drain()
                        act.activation(soft[:, :], soft[:, :], ACT.Ln, bias=1.0).then_inc(soft_ready, 1)

                    def squares(i):
                        act.activation(sq[:, 0, :], kT[:, ds(i * QN, QN)], ACT.Square)
                        act.activation(sq[:, 1, :], qT[:, ds(i * QN, QN)], ACT.Square).then_inc(sq_ready, 1)

                    def decays(i, par):
                        act.wait_ge(cum_ready, i + 1)
                        act.activation(up[:, :], cum[:, :], ACT.Exp, scale=-1.0 / GATE_NORM)
                        act.activation(down[:, par, :], cum[:, :], ACT.Exp, scale=1.0 / GATE_NORM
                                       ).then_inc(exps_ready, 1)

                    def quad(i, par, has_next):
                        if has_next:
                            softplus(i + 1)
                        act.wait_ge(ke_turned, i + 1)
                        act.copy(ke_tok[:, :, :].rearrange("p t d -> p (t d)"), ps[:, 2, :]).then_inc(ke_ready, 1)
                        if has_next:
                            squares(i + 1)
                            decays(i + 1, 1 - par)
                        act.wait_ge(o_mm, i + 1)
                        act.activation(osq[:, :], ps[:, 6, :], ACT.Square)
                        act.activation(oT[:, :], ps[:, 6, :], ACT.Copy, scale=W("norm_w")).then_inc(o_ready, 1)

                    act.preload_act_table(ACT.Ln)
                    softplus(0)
                    squares(0)
                    decays(0, 0)
                    run(act, quad)

                @block.vector
                def _(dve):
                    def accumulate(i):
                        dve.wait_ge(soft_ready, i + 1)
                        dve.scalar_tensor_tensor(logsig[:, :], gT[:, ds(i * QN, QN)], 0.0, soft[:, :],
                                                 ALU.min, ALU.subtract)
                        dve.drain()
                        dve.tensor_tensor_scan(cum[:, :], C("reset"), logsig[:, :], 0.0, ALU.mult,
                                               ALU.add).then_inc(cum_ready, 1)

                    def take_norms(i):
                        dve.wait_ge(norm_mm, i + 1)
                        dve.tensor_copy(norms[:, :], ps[:, 0, 0:2 * QT]).then_inc(norms_out, 1)

                    def decayed(i, par):
                        dve.wait_ge(exps_ready, i + 1)
                        dve.tensor_tensor(ke[:, :], kT[:, ds(i * QN, QN)], up[:, :], ALU.mult)
                        dve.tensor_tensor(qe[:, par, :], qT[:, ds(i * QN, QN)], down[:, par, :],
                                          ALU.mult).then_inc(qk_ready, 1)

                    def scale_v(i, par):
                        dve.wait_ge(root_ready, i + 1)
                        dve.reciprocal(inv[:, par, :], norms[:, :])
                        dve.drain()
                        dve.wait_ge(v_turned, i + 1)
                        for j in range(QT):
                            last = dve.tensor_scalar(v_tok[:, j, :], ps[:, 1, j * D:(j + 1) * D],
                                                     inv[:, par, j:j + 1], None, ALU.mult)
                        last.then_inc(v_ready, 1)

                    def states(i, par):
                        dve.wait_ge(outer_mm, i + 1)
                        ends = down[:, par, :].rearrange("p (s c l) -> p s c l", s=SQ, c=NC_SEQ)
                        for c in range(NC_SEQ - 1):
                            if c % 2 == 0:
                                prod = ps[:, 4, :].rearrange("p (s c d) -> p s c d", s=SQ, c=2)[:, :, c // 2, :]
                            else:
                                prod = ps[:, 5, 0:SQ * D].rearrange("p (s d) -> p s d", s=SQ)
                            end = ends[:, :, c, CHUNK - 1:CHUNK].to_broadcast([P, SQ, D])
                            if c == 0:
                                dve.tensor_tensor(state[:, c], prod, end, ALU.mult)
                                dve.copy_predicated(wT[:, :, :],
                                                    causal_sb[:, :].unsqueeze(1).to_broadcast([P, QT, P]),
                                                    ps[:, 3, :].rearrange("p (t q) -> p t q", t=QT)
                                                    ).then_inc(w_ready, 1)
                            else:
                                dve.drain()
                                dve.tensor_tensor(state[:, c], state[:, c - 1], prod, ALU.add)
                                dve.drain()
                                last = dve.tensor_tensor(state[:, c], state[:, c], end, ALU.mult)
                        last.then_inc(state_ready, 1)

                    def quad(i, par, has_next):
                        if has_next:
                            accumulate(i + 1)
                        states(i, par)
                        if has_next:
                            take_norms(i + 1)
                            decayed(i + 1, 1 - par)
                            scale_v(i + 1, 1 - par)
                        dve.wait_ge(ss_mm, i + 1)
                        dve.tensor_tensor(fac[:, :], inv[:, par, QT:2 * QT], inv[:, par, QT:2 * QT], ALU.mult)
                        dve.drain()
                        dve.tensor_tensor(ms[:, :], ps[:, 5, SS:SS + QT], fac[:, :], ALU.mult)
                        dve.drain()
                        dve.tensor_scalar(ms[:, :], ms[:, :], 1.0 / D, 1e-6, ALU.mult, ALU.add).then_inc(ms_ready, 1)
                        dve.wait_ge(fac_ready, i + 1)
                        dve.tensor_tensor(fac[:, :], ms[:, :], inv[:, par, QT:2 * QT], ALU.mult)
                        dve.drain()
                        dve.wait_ge(out_mm, i + 1)
                        for j in range(QT):
                            hj = h[:, ds(i * QT + j, 1), :].rearrange("p t d -> p (t d)")
                            last = dve.scalar_tensor_tensor(hj, ps[:, 7, j * D:(j + 1) * D], fac[:, j:j + 1], hj,
                                                            ALU.mult, ALU.add)
                        last.then_inc(h_done, 1)

                    dve.memset(wT[:, :, :], 0.0)
                    dve.drain()
                    accumulate(0)
                    take_norms(0)
                    decayed(0, 0)
                    scale_v(0, 0)
                    run(dve, quad)

                @block.tensor
                def _(pe):
                    def turn_v(i):
                        pe.wait_ge(v_copied, i + 1)
                        for j in range(QT):
                            last = pe.transpose(ps[:, 1, j * P:(j + 1) * P], v_in[:, j * P:(j + 1) * P], ident)
                        last.then_inc(v_turned, 1)

                    def sum_squares(i):
                        pe.wait_ge(sq_ready, i + 1)
                        for z in range(2):
                            for j in range(QT):
                                last = pe.matmul(ps[:, 0, z * QT + j:z * QT + j + 1], sq[:, z, j * P:(j + 1) * P],
                                                 ones_col, start=True, stop=True)
                        last.then_inc(norm_mm, 1)

                    def quad(i, par, has_next):
                        pe.wait_ge(qk_ready, i + 1)
                        for j in range(QT):
                            last = pe.transpose(ps[:, 2, j * P:(j + 1) * P], ke[:, j * P:(j + 1) * P], ident)
                        last.then_inc(ke_turned, 1)
                        for j in range(QT):
                            last = pe.matmul(ps[:, 3, j * P:(j + 1) * P], ke[:, j * P:(j + 1) * P],
                                             qe[:, par, j * P:(j + 1) * P], start=True, stop=True)
                        pe.wait_ge(ke_ready, i + 1)
                        pe.wait_ge(v_ready, i + 1)
                        if past_first(i):
                            pe.wait_ge(ms_ready, i)
                        for s in range(SQ):
                            for c in range(NC_SEQ - 1):
                                rows = slice(CHUNK * (c % 2), CHUNK * (c % 2) + CHUNK)
                                tile = 2 * s + c // 2
                                at = (2 * s + c // 2) * D if c % 2 == 0 else s * D
                                last = pe.matmul(ps[:, 4 + c % 2, at:at + D], ke_tok[rows, tile, :],
                                                 v_tok[rows, tile, :], start=True, stop=True)
                        last.then_inc(outer_mm, 1)
                        if has_next:
                            sum_squares(i + 1)
                        pe.wait_ge(w_ready, i + 1)
                        pe.wait_ge(state_ready, i + 1)
                        for j in range(QT):
                            s = j // 2
                            pe.matmul(ps[:, 6, j * P:(j + 1) * P], v_tok[:, j, :], wT[:, j, :], start=True,
                                      stop=False, skip_group_check=True)
                            for half_ in range(2):
                                c = 2 * (j % 2) + half_
                                if c:
                                    at = j * P + half_ * CHUNK
                                    last = pe.matmul(ps[:, 6, at:at + CHUNK], state[:, c - 1, s, :],
                                                     qe[:, par, at:at + CHUNK], start=False, stop=True,
                                                     skip_group_check=True)
                        last.then_inc(o_mm, 1)
                        if has_next:
                            turn_v(i + 1)
                        pe.wait_ge(o_ready, i + 1)
                        for j in range(QT):
                            last = pe.matmul(ps[:, 5, SS + j:SS + j + 1], osq[:, j * P:(j + 1) * P], ones_col,
                                             start=True, stop=True)
                        last.then_inc(ss_mm, 1)
                        if past_first(i):
                            pe.wait_ge(h_done, i)
                        for j in range(QT):
                            last = pe.matmul(ps[:, 7, j * D:(j + 1) * D], oT[:, j * P:(j + 1) * P], W("wo0"),
                                             start=True, stop=True)
                        last.then_inc(out_mm, 1)

                    turn_v(0)
                    sum_squares(0)
                    run(pe, quad)

        def moe0_stage(wexp, wexp_in):
            with ExitStack() as st:
                xT = sb("m_xT", [P, N], F32, st)
                gates = sb("m_gates", [P, T, E0], F32, st)
                ring = sb("m_ring", [P, 2, W0COLS], F32, st)
                slot_in = [sem("m_slot_in0"), sem("m_slot_in1")]
                slot_free = sem("m_slot_free")
                moe0_router(xT, gates, wexp, wexp_in)
                moe0_experts(xT, gates, ring, slot_in, slot_free)

        def moe0_router(xT, gates, wexp, wexp_in):
            with ExitStack() as st:
                stats = sb("r_stats", [P, QT, 6], F32, st)
                mv = sb("r_mv", [P, QT, 2], F32, st)
                rstd = sb("r_rstd", [P, QT], F32, st)
                neghalf = sb("r_neghalf", [P, QT], F32, st)
                xn = sb("r_xn", [P, QT, D], F32, st)
                xs = sb("r_xs", [P, QN], F32, st)
                logits = sb("r_logits", [P, QT, E0], F32, st)
                top = sb("r_top", [P, QT, 8], F32, st)
                topi = sb("r_topi", [P, QT, 8], U32, st)
                topf = sb("r_topf", [P, QT, 8], F32, st)
                gap = sb("r_gap", [P, QT], F32, st)
                ex = sb("r_ex", [P, QT], F32, st)
                den = sb("r_den", [P, QT], F32, st)
                wts = sb("r_wts", [P, 2, QT], F32, st)
                g2 = sb("r_g2", [P, 2, QT, E0], F32, st)
                gq = sb("r_gq", [P, QT, E0], F32, st)
                gqT = sb("r_gqT", [E0, QN], F32, st)
                var_ready = sem("r_var_ready")
                rstd_ready = sem("r_rstd_ready")
                xn_ready = sem("r_xn_ready")
                turned = sem("r_turned")
                xs_ready = sem("r_xs_ready")
                xT_stored = sem("r_xT_stored")
                logit_mm = sem("r_logit_mm")
                gap_ready = sem("r_gap_ready")
                ex_ready = sem("r_ex_ready")
                gq_ready = sem("r_gq_ready")
                g_turned = sem("r_g_turned")
                gT_ready = sem("r_gT_ready")
                bias_mm = sem("r_bias_mm")
                h_done = sem("r_h_done")
                zeroed = sem("r_zeroed")
                block = st.enter_context(nc.Block())

                @block.sync
                def _(sp):
                    for n in range(WLOADS):
                        e = n * E1 // WLOADS
                        sp.dma_start(wexp[:, e:e + E1 // WLOADS, :],
                                     w1[:, e:e + E1 // WLOADS, :]).then_inc(wexp_in, 16)

                @block.vector
                def _(dve):
                    dve.sem_inc(h_done, 1)
                    with dve.Fori(0, NQ) as i:
                        ln_stats(dve, stats, mv, rstd, QT, i, var_ready)
                        dve.wait_ge(rstd_ready, i + 1)
                        ln_apply(dve, xn, mv, rstd, QT, i).then_inc(xn_ready, 1)
                        dve.wait_ge(logit_mm, i + 1)
                        dve.tensor_copy(logits[:, :, :], ps[:, 1, 0:QT * E0].rearrange("p (t e) -> p t e", t=QT))
                        dve.drain()
                        for j in range(QT):
                            dve.max(top[:, j, :], logits[:, j, :])
                        dve.drain()
                        for j in range(QT):
                            dve.max_index(topi[:, j, :], top[:, j, :], logits[:, j, :])
                        dve.tensor_tensor(gap[:, :], top[:, :, 1], top[:, :, 0], ALU.subtract).then_inc(gap_ready, 1)
                        dve.drain()
                        dve.tensor_copy(topf[:, :, :], topi[:, :, :])
                        dve.wait_ge(ex_ready, i + 1)
                        dve.tensor_scalar(den[:, :], ex[:, :], 1.0, None, ALU.add)
                        dve.drain()
                        dve.reciprocal(wts[:, 0, :], den[:, :])
                        dve.drain()
                        dve.tensor_tensor(wts[:, 1, :], wts[:, 0, :], ex[:, :], ALU.mult)
                        dve.drain()
                        for k in range(2):
                            for j in range(QT):
                                dve.tensor_scalar(g2[:, k, j, :], C("iota")[:, 0:E0], topf[:, j, k:k + 1],
                                                  wts[:, k, j:j + 1], ALU.is_equal, ALU.mult)
                        dve.drain()
                        dve.tensor_tensor(gq[:, :, :], g2[:, 0], g2[:, 1], ALU.add).then_inc(gq_ready, 1)
                        dve.drain()
                        dve.tensor_copy(gates[:, ds(i * QT, QT), :], gq[:, :, :])
                        dve.wait_ge(bias_mm, i + 1)
                        dve.tensor_tensor(h[:, ds(i * QT, QT), :], h[:, ds(i * QT, QT), :],
                                          ps[:, 3, :].rearrange("p (t d) -> p t d", t=QT), ALU.add).then_inc(h_done, 1)

                @block.gpsimd
                def _(pool):
                    pool.memset(neghalf[:, :], -0.5)
                    pool.drain()
                    with pool.Fori(0, NQ) as i:
                        pool.wait_ge(var_ready, i + 1)
                        ln_rstd(pool, rstd, neghalf, QT).then_inc(rstd_ready, 1)
                        pool.wait_ge(xs_ready, i + 1)
                        pool.tensor_copy(xT[:, ds(i * QN, QN)], xs[:, :]).then_inc(xT_stored, 1)

                @block.scalar
                def _(act):
                    act.preload_act_table(ACT.Exp)
                    act.sem_inc(xT_stored, 1)
                    with act.Fori(0, NQ) as i:
                        act.wait_ge(xT_stored, i + 1)
                        act.wait_ge(turned, i + 1)
                        act.copy(xs[:, :], ps[:, 0, :]).then_inc(xs_ready, 1)
                        act.wait_ge(gap_ready, i + 1)
                        act.activation(ex[:, :], gap[:, :], ACT.Exp).then_inc(ex_ready, 1)
                        act.wait_ge(g_turned, i + 1)
                        act.copy(gqT[:, :], ps[0:E0, 2, :]).then_inc(gT_ready, 1)

                @block.tensor
                def _(pe):
                    with pe.Fori(0, NQ) as i:
                        pe.wait_ge(h_done, i + 1)
                        pe.wait_ge(xn_ready, i + 1)
                        for j in range(QT):
                            last = pe.transpose(ps[:, 0, j * P:(j + 1) * P], xn[:, j, :], ident)
                        last.then_inc(turned, 1)
                        pe.wait_ge(xs_ready, i + 1)
                        for j in range(QT):
                            pe.matmul(ps[:, 1, j * E0:(j + 1) * E0], xs[:, j * P:(j + 1) * P], W("rw0"), start=True,
                                      stop=False)
                            last = pe.matmul(ps[:, 1, j * E0:(j + 1) * E0], ones_row, W("rb0", 1), start=False,
                                             stop=True)
                        last.then_inc(logit_mm, 1)
                        pe.wait_ge(gq_ready, i + 1)
                        for j in range(QT):
                            last = pe.transpose(ps[0:E0, 2, j * P:(j + 1) * P], gq[:, j, :], ident)
                        last.then_inc(g_turned, 1)
                        pe.wait_ge(gT_ready, i + 1)
                        for j in range(QT):
                            last = pe.matmul(ps[:, 3, j * D:(j + 1) * D], gqT[:, j * P:(j + 1) * P], W("fc2_b", E0),
                                             start=True, stop=True)
                        last.then_inc(bias_mm, 1)

        def moe0_experts(xT, gates, ring, slot_in, slot_free):
            with ExitStack() as st:
                act1 = sb("x_act1", [P, 2, QN], F32, st)
                a = sb("x_a", [P, 2, 2, QN], F32, st)
                hid_mm = sem("x_hid_mm")
                silu_done = sem("x_silu_done")
                a_ready = sem("x_a_ready")
                y_mm = sem("x_y_mm")
                y_used = sem("x_y_used")
                STEPS = 2 * NQ
                block = st.enter_context(nc.Block())

                @block.sync
                def _(sp):
                    sp.sem_inc(slot_free, 2)
                    with sp.Fori(0, E0 // 2) as pair:
                        e = pair * 2
                        for s in range(2):
                            sp.wait_ge(slot_free, e + s + 1)
                            sp.dma_start(ring[:, s, :], w0[:, ds(e + s, 1), :]).then_inc(slot_in[s], 16)

                def w1_of(s, part, f):
                    o = part * F0 + f * P
                    return ring[:, s, o:o + P]

                def bias_of(s, part, f):
                    o = 2 * F0 + 2 * D + part * 2 + f
                    return ring[:, s, o:o + 1]

                @block.tensor
                def _(pe):
                    pe.sem_inc(a_ready, 2)
                    pe.sem_inc(y_mm, 2)
                    pe.sem_inc(y_used, 2)

                    def hidden(e, n):
                        s, c = n // NQ, n % NQ
                        if c == 0:
                            pe.wait_ge(slot_in[s], e * 8 + 16)
                        for f in range(2):
                            pe.wait_ge(a_ready, e * (2 * NQ) + 2 * n + f + 1)
                            for part in range(2):
                                last = pe.matmul(ps[:, 2 * f + part, :], w1_of(s, part, f),
                                                 xT[:, c * QN:(c + 1) * QN], start=True, stop=True)
                            last.then_inc(hid_mm, 1)

                    def output(e, n):
                        s = n // NQ
                        pe.wait_ge(a_ready, e * (2 * NQ) + 2 * n + 4)
                        pe.wait_ge(y_used, e * NQ + n + 1)
                        for j in range(QT):
                            for f in range(2):
                                o = 2 * F0 + f * D
                                last = pe.matmul(ps[:, 4 + n % 2, j * D:(j + 1) * D], a[:, n % 2, f, j * P:(j + 1) * P],
                                                 ring[:, s, o:o + D], start=(f == 0), stop=(f == 1))
                        last.then_inc(y_mm, 1)

                    with pe.Fori(0, E0 // 2) as pair:
                        e = pair * 2
                        for n in range(STEPS):
                            hidden(e, n)
                            if n:
                                output(e, n - 1)
                        output(e, STEPS - 1)

                @block.scalar
                def _(act):
                    act.preload_act_table(ACT.Silu)
                    with act.Fori(0, E0 // 2) as pair:
                        e = pair * 2
                        for n in range(STEPS):
                            s = n // NQ
                            for f in range(2):
                                act.wait_ge(hid_mm, e * (2 * NQ) + 2 * n + f + 1)
                                act.wait_ge(a_ready, e * (2 * NQ) + 2 * n + f + 1)
                                act.activation(act1[:, f, :], ps[:, 2 * f, :], ACT.Silu,
                                               bias=bias_of(s, 0, f)).then_inc(silu_done, 1)

                @block.vector
                def _(dve):
                    def combine(e, n):
                        dve.wait_ge(y_mm, e * NQ + n + 3)
                        s, c = n // NQ, n % NQ
                        for j in range(QT):
                            t = c * QT + j
                            last = dve.scalar_tensor_tensor(h[:, t, :], ps[:, 4 + n % 2, j * D:(j + 1) * D],
                                                            gates[:, t, ds(e + s, 1)], h[:, t, :], ALU.mult, ALU.add)
                        last.then_inc(y_used, 1)
                        if c == NQ - 1:
                            dve.sem_inc(slot_free, 1)

                    with dve.Fori(0, E0 // 2) as pair:
                        e = pair * 2
                        for n in range(STEPS):
                            s = n // NQ
                            dve.wait_ge(y_mm, e * NQ + n + 1)
                            for f in range(2):
                                dve.wait_ge(silu_done, e * (2 * NQ) + 2 * n + f + 1)
                                dve.scalar_tensor_tensor(a[:, n % 2, f, :], ps[:, 2 * f + 1, :], bias_of(s, 1, f),
                                                         act1[:, f, :], ALU.add, ALU.mult).then_inc(a_ready, 1)
                            if n:
                                combine(e, n - 1)
                        combine(e, STEPS - 1)

        def attention_stage():
            with ExitStack() as st:
                AT = 2
                stats = sb("w_stats", [P, AT, 6], F32, st)
                mv = sb("w_mv", [P, AT, 2], F32, st)
                rstd = sb("w_rstd", [P, AT], F32, st)
                neghalf = sb("w_neghalf", [P, AT], F32, st)
                xn = sb("w_xn", [P, AT, D], F32, st)
                xs = sb("w_xs", [P, L], F32, st)
                bq4 = sb("w_bq4", [P, 2], F32, st)
                qs = sb("w_qs", [P, 2, 2, L], F32, st)
                ks = sb("w_ks", [P, 2, 2, L], F32, st)
                vs = sb("w_vs", [P, 2, AT, D], F32, st)
                sc = sb("w_sc", [P, 2, 2, KW], F32, st)
                mx = sb("w_mx", [P, AT, 2, 4], F32, st)
                nm = sb("w_nm", [P, AT, 2, 4], F32, st)
                rs = sb("w_rs", [P, 2, AT, 2, 4], F32, st)
                pr = sb("w_pr", [P, AT, HEADS, L], F32, st)
                pT = sb("w_pT", [P, 2, 2, 2, P], F32, st)
                rr = sb("w_rr", [P, AT, 2, 4], F32, st)
                cx = sb("w_cx", [P, AT, D], F32, st)
                cxT = sb("w_cxT", [P, L], F32, st)
                bv = sb("w_bv", [P, D], F32, st)
                bias_in = sem("w_bias_in")
                var_ready = sem("w_var_ready")
                rstd_ready = sem("w_rstd_ready")
                xn_ready = sem("w_xn_ready")
                turned = sem("w_turned")
                xs_ready = sem("w_xs_ready")
                q_mm = sem("w_q_mm")
                k_mm = sem("w_k_mm")
                v_mm = sem("w_v_mm")
                q_ready = sem("w_q_ready")
                k_ready = sem("w_k_ready")
                v_ready = sem("w_v_ready")
                score_mm = sem("w_score_mm")
                score_used = sem("w_score_used")
                nm_ready = sem("w_nm_ready")
                exp_done = sem("w_exp_done")
                p_turned = sem("w_p_turned")
                pT_ready = sem("w_pT_ready")
                pv_mm = sem("w_pv_mm")
                cx_ready = sem("w_cx_ready")
                cx_turned = sem("w_cx_turned")
                cxT_ready = sem("w_cxT_ready")
                out_mm = sem("w_out_mm")
                h_done = sem("w_h_done")
                zeroed = sem("w_zeroed")
                UNITS = [(tile, s) for tile in range(AT) for s in range(4)]
                NU = len(UNITS)
                block = st.enter_context(nc.Block())

                def key_cols(tile):
                    return (0, P, WIN) if tile == 0 else (WIN, L, 0)

                def run(eng, sequence):
                    sequence(0, 0, False, True)
                    with eng.Fori(0, B // 2 - 1) as pair:
                        sequence(pair * 2 + 1, 1, True, True)
                        sequence(pair * 2 + 2, 0, True, True)
                    sequence(B - 1, 1, True, False)

                @block.sync
                def _(sp):
                    o = _cols["abv"][0]
                    row = bass.AP(weights.tensor, o, [[0, P], [1, D]])
                    sp.dma_start(bv[:, :], row).then_inc(bias_in, 16)

                @block.gpsimd
                def _(pool):
                    pool.memset(neghalf[:, :], -0.5)
                    pool.memset(pr[:, :, :, :], 0.0).then_inc(zeroed, 1)
                    pool.drain()
                    with pool.Fori(0, B) as i:
                        pool.wait_ge(var_ready, i + 1)
                        ln_rstd(pool, rstd, neghalf, AT).then_inc(rstd_ready, 1)

                @block.vector
                def _(dve):
                    def stats_of(i):
                        for j in range(AT):
                            dve.bn_stats(stats[:, j, :], h[:, ds(i * AT + j, 1), :])
                        dve.drain()
                        for j in range(AT):
                            dve.bn_aggr(mv[:, j, :], stats[:, j, :])
                        dve.drain()
                        dve.tensor_scalar(rstd[:, :], mv[:, :, 1], EPS_LN, None, ALU.add).then_inc(var_ready, 1)

                    def normalise(i):
                        dve.wait_ge(rstd_ready, i + 1)
                        ln_apply(dve, xn, mv, rstd, AT, i).then_inc(xn_ready, 1)

                    def take_v(i, s):
                        dve.wait_ge(v_mm, i + 1)
                        dve.tensor_tensor(vs[:, s], ps[:, 7, 0:L].rearrange("p (t d) -> p t d", t=AT),
                                          bv[:, :].unsqueeze(1).to_broadcast([P, AT, D]), ALU.add).then_inc(v_ready, 1)

                    def largest(i, n):
                        tile, s = UNITS[n]
                        lo, hi, b0 = key_cols(tile)
                        w = hi - lo
                        dve.wait_ge(score_mm, i * NU + n + 1)
                        if n >= 2 or not isinstance(i, int) or i:
                            dve.wait_ge(exp_done, i * NU + n - 1)
                        dve.memset(carrier[:, :], 0.0)
                        for g in range(2):
                            last = dve.tensor_tensor_reduce(sc[:, n % 2, g, 0:w], ps[:, n % 3, 256 * g:256 * g + w],
                                                            band[:, 4 * g + s, b0:b0 + w], 1.0, NEG, ALU.add,
                                                            ALU.max, mx[:, tile, g, s:s + 1])
                        last.then_inc(score_used, 1)
                        dve.drain()
                        dve.tensor_scalar(nm[:, tile, :, s], mx[:, tile, :, s], -1.0, None,
                                          ALU.mult).then_inc(nm_ready, 1)

                    def copy_pT(i, n):
                        nb = UNITS[n][0] + 1
                        dve.wait_ge(p_turned, i * NU + n + 1)
                        if n >= 2 or not isinstance(i, int) or i:
                            dve.wait_ge(pv_mm, i * NU + n - 1)
                        dve.tensor_copy(pT[:, n % 2, 0:nb].rearrange("p b g q -> p (b g q)"),
                                        ps[:, 3 + n % 2, 0:nb * 2 * P]).then_inc(pT_ready, 1)

                    def context(i, par):
                        dve.wait_ge(exp_done, (i + 1) * NU)
                        dve.reciprocal(rr[:, :, :, :], rs[:, par])
                        dve.drain()
                        dve.wait_ge(pv_mm, (i + 1) * NU)
                        dve.tensor_tensor(cx[:, :, :].rearrange("p t (h d) -> p (t h) d", h=HEADS),
                                          ps[:, 5, 0:L].rearrange("p (t d) -> p t d", d=DH),
                                          rr[:, :, :, :].rearrange("p t g s -> p (t g s)").unsqueeze(2)
                                          .to_broadcast([P, AT * HEADS, DH]), ALU.mult).then_inc(cx_ready, 1)

                    def finish(i):
                        dve.wait_ge(out_mm, i + 1)
                        dve.tensor_tensor(h[:, ds(i * AT, AT), :], h[:, ds(i * AT, AT), :],
                                          ps[:, 5, L:2 * L].rearrange("p (t d) -> p t d", t=AT), ALU.add
                                          ).then_inc(h_done, 1)

                    def sequence(i, par, has_tail, has_front):
                        if has_tail:
                            context(i - 1, 1 - par)
                        for n in range(NU):
                            largest(i, n)
                            if n:
                                copy_pT(i, n - 1)
                            if n == 1 and has_tail:
                                finish(i - 1)
                            if n == 2 and has_front:
                                stats_of(i + 1)
                            if n == 3 and has_front:
                                normalise(i + 1)
                        if has_front:
                            take_v(i + 1, 1 - par)
                        copy_pT(i, NU - 1)

                    dve.wait_ge(band_made, 16)
                    dve.wait_ge(bias_in, 16)
                    dve.tensor_scalar(bq4[:, :], W("abq"), 0.25, None, ALU.mult).then_inc(zeroed, 1)
                    stats_of(0)
                    normalise(0)
                    take_v(0, 0)
                    run(dve, sequence)
                    context(B - 1, 1)
                    finish(B - 1)

                @block.scalar
                def _(act):
                    def take_xs(i):
                        act.wait_ge(turned, i + 1)
                        act.copy(xs[:, :], ps[:, 6, 0:L]).then_inc(xs_ready, 1)

                    def take_q(i, s):
                        act.wait_ge(q_mm, i + 1)
                        for g in range(2):
                            last = act.activation(qs[:, s, g, :], ps[:, 7, g * L:(g + 1) * L], ACT.Identity,
                                                  scale=0.25, bias=bq4[:, g:g + 1])
                        last.then_inc(q_ready, 1)

                    def take_k(i, s):
                        act.wait_ge(k_mm, i + 1)
                        for g in range(2):
                            last = act.activation(ks[:, s, g, :], ps[:, 6, g * L:(g + 1) * L], ACT.Identity,
                                                  bias=W("abk")[:, g:g + 1])
                        last.then_inc(k_ready, 1)

                    def sequence(i, par, has_tail, has_front):
                        for n, (tile, s) in enumerate(UNITS):
                            lo, hi, b0 = key_cols(tile)
                            act.wait_ge(nm_ready, i * NU + n + 1)
                            if has_tail:
                                act.wait_ge(p_turned, (i - 1) * NU + n + 1)
                            for g in range(2):
                                last = act.activation(pr[:, tile, 4 * g + s, lo:hi], sc[:, n % 2, g, 0:hi - lo],
                                                      ACT.Exp, bias=nm[:, tile, g, s:s + 1],
                                                      accum_out=rs[:, par, tile, g, s:s + 1])
                            last.then_inc(exp_done, 1)
                            if n == 0 and has_tail:
                                act.wait_ge(cx_turned, i)
                                act.copy(cxT[:, :], ps[:, 5, 0:L]).then_inc(cxT_ready, 1)
                            if has_front and n == 3:
                                take_xs(i + 1)
                            if has_front and n == 4:
                                take_q(i + 1, 1 - par)
                            if has_front and n == 5:
                                take_k(i + 1, 1 - par)

                    act.preload_act_table(ACT.Exp)
                    act.wait_ge(zeroed, 2)
                    take_xs(0)
                    take_q(0, 0)
                    take_k(0, 0)
                    run(act, sequence)
                    act.wait_ge(cx_turned, B)
                    act.copy(cxT[:, :], ps[:, 5, 0:L]).then_inc(cxT_ready, 1)

                @block.tensor
                def _(pe):
                    def turn_xn(i):
                        pe.wait_ge(xn_ready, i + 1)
                        if not isinstance(i, int) or i:
                            pe.wait_ge(k_ready, i)
                        for j in range(AT):
                            last = pe.transpose(ps[:, 6, j * P:(j + 1) * P], xn[:, j, :], ident)
                        last.then_inc(turned, 1)

                    def project_q(i):
                        pe.wait_ge(xs_ready, i + 1)
                        if not isinstance(i, int) or i:
                            pe.wait_ge(v_ready, i)
                        for g in range(2):
                            last = pe.matmul(ps[:, 7, g * L:(g + 1) * L], W("aq")[:, g * P:(g + 1) * P], xs[:, :],
                                             start=True, stop=True)
                        last.then_inc(q_mm, 1)

                    def project_k(i):
                        for g in range(2):
                            last = pe.matmul(ps[:, 6, g * L:(g + 1) * L], W("ak")[:, g * P:(g + 1) * P], xs[:, :],
                                             start=True, stop=True)
                        last.then_inc(k_mm, 1)

                    def project_v(i):
                        pe.wait_ge(q_ready, i + 1)
                        for j in range(AT):
                            last = pe.matmul(ps[:, 7, j * D:(j + 1) * D], xs[:, j * P:(j + 1) * P], W("av"),
                                             start=True, stop=True)
                        last.then_inc(v_mm, 1)

                    def turn_cx(i):
                        pe.wait_ge(cx_ready, i + 1)
                        for j in range(AT):
                            last = pe.transpose(ps[:, 5, j * P:(j + 1) * P], cx[:, j, :], ident)
                        last.then_inc(cx_turned, 1)

                    def output(i):
                        pe.wait_ge(cxT_ready, i + 1)
                        for j in range(AT):
                            at = L + j * D
                            pe.matmul(ps[:, 5, at:at + D], cxT[:, j * P:(j + 1) * P], W("awo"), start=True, stop=False)
                            last = pe.matmul(ps[:, 5, at:at + D], ones_row, W("abo", 1), start=False, stop=True)
                        last.then_inc(out_mm, 1)

                    def scores(i, par, n):
                        tile, s = UNITS[n]
                        lo, hi, b0 = key_cols(tile)
                        rows = slice(32 * s, 32 * s + DH)
                        pe.wait_ge(score_used, i * NU + n + 1)
                        for g in range(2):
                            last = pe.matmul(ps[:, n % 3, 256 * g:256 * g + hi - lo],
                                             qs[rows, par, g, tile * P:(tile + 1) * P], ks[rows, par, g, lo:hi],
                                             start=True, stop=True)
                        last.then_inc(score_mm, 1)

                    def turn(i, n):
                        tile, s = UNITS[n]
                        pe.wait_ge(exp_done, i * NU + n + 1)
                        if n >= 2 or not isinstance(i, int) or i:
                            pe.wait_ge(pT_ready, i * NU + n - 1)
                        for b in range(tile + 1):
                            for g in range(2):
                                at = (2 * b + g) * P
                                last = pe.transpose(ps[:, 3 + n % 2, at:at + P],
                                                    pr[:, tile, 4 * g + s, b * P:(b + 1) * P], ident)
                        last.then_inc(p_turned, 1)

                    def weigh(i, par, n):
                        tile, s = UNITS[n]
                        pe.wait_ge(pT_ready, i * NU + n + 1)
                        if n == 0 and (not isinstance(i, int) or i):
                            pe.wait_ge(h_done, i)
                        for g in range(2):
                            hd = 4 * g + s
                            at = tile * D + hd * DH
                            for b in range(tile + 1):
                                last = pe.matmul(ps[:, 5, at:at + DH], pT[:, n % 2, b, g, :],
                                                 vs[:, par, b, hd * DH:(hd + 1) * DH], start=(b == 0), stop=(b == tile))
                        last.then_inc(pv_mm, 1)

                    def sequence(i, par, has_tail, has_front):
                        pe.wait_ge(q_ready, i + 1)
                        pe.wait_ge(k_ready, i + 1)
                        pe.wait_ge(v_ready, i + 1)
                        scores(i, par, 0)
                        scores(i, par, 1)
                        if has_tail:
                            turn_cx(i - 1)
                        for n in range(NU):
                            if n + 2 < NU:
                                scores(i, par, n + 2)
                            turn(i, n)
                            if n == 0 and has_tail:
                                output(i - 1)
                            if n:
                                weigh(i, par, n - 1)
                            if has_front and n == 3:
                                turn_xn(i + 1)
                            if has_front and n == 4:
                                project_q(i + 1)
                                project_k(i + 1)
                            if has_front and n == 6:
                                project_v(i + 1)
                        weigh(i, par, NU - 1)

                    pe.sem_inc(score_used, 3)
                    pe.wait_ge(zeroed, 2)
                    turn_xn(0)
                    project_q(0)
                    project_k(0)
                    project_v(0)
                    run(pe, sequence)
                    turn_cx(B - 1)
                    output(B - 1)

        def moe1_stage(wexp, wexp_in):
            with ExitStack() as st:
                xn_all = sb("n_xn_all", [P, T, D], F32, st)
                xT = sb("n_xT", [P, N], F32, st)
                pick = sb("n_pick", [P, T, 8], F32, st)
                wts = sb("n_wts", [P, T, TOPK1], F32, st)
                rank = sb("n_rank", [P, T, E1], F32, st)
                seen = sb("n_seen", [P, E1], F32, st)
                pos_i = sb("n_pos_i", [P, T, TOPK1], I32, st)
                erow = sb("n_erow", [1, NTILE], I32, st)
                source = sb("n_source", [P, NTILE], I32, st)
                x_out = sem("n_x_out")
                x_rows = nc.dram_tensor("x_rows", (N, D), F32, kind="Internal").ap()
                ysorted = nc.dram_tensor("y_sorted", (NTILE * P, D), F32, kind="Internal").ap()
                moe1_router(xn_all, xT, pick, wts, rank, seen)
                moe1_dispatch(xn_all, xT, pick, rank, seen, pos_i, erow, source, x_rows, x_out)
                moe1_tiles(wexp, erow, source, x_rows, x_out, ysorted, wexp_in)
                moe1_combine(pos_i, wts, ysorted)

        def moe1_router(xn_all, xT, pick, wts, rank, seen):
            with ExitStack() as st:
                stats = sb("s_stats", [P, QT, 6], F32, st)
                mv = sb("s_mv", [P, QT, 2], F32, st)
                rstd = sb("s_rstd", [P, QT], F32, st)
                neghalf = sb("s_neghalf", [P, QT], F32, st)
                xn = sb("s_xn", [P, QT, D], F32, st)
                xs = sb("s_xs", [P, QN], F32, st)
                nmx = sb("s_nmx", [P, QT], F32, st)
                ex = sb("s_ex", [P, QT, E1], F32, st)
                top = sb("s_top", [P, QT, 8], F32, st)
                topi = sb("s_topi", [P, QT, 8], U32, st)
                topf = sb("s_topf", [P, QT, 8], F32, st)
                tot = sb("s_tot", [P, QT], F32, st)
                eq = sb("s_eq", [P, QT, TOPK1, E1], F32, st)
                chosen = sb("s_chosen", [P, QT, E1], F32, st)
                more = sb("s_more", [P, E1], F32, st)
                var_ready = sem("s_var_ready")
                rstd_ready = sem("s_rstd_ready")
                xn_ready = sem("s_xn_ready")
                turned = sem("s_turned")
                xs_ready = sem("s_xs_ready")
                xT_stored = sem("s_xT_stored")
                logit_mm = sem("s_logit_mm")
                nmx_ready = sem("s_nmx_ready")
                ex_ready = sem("s_ex_ready")
                chosen_ready = sem("s_chosen_ready")
                rank_mm = sem("s_rank_mm")
                block = st.enter_context(nc.Block())

                def run(eng, quad):
                    quad(0, False, True)
                    with eng.Fori(0, NQ - 2) as i:
                        quad(i + 1, True, True)
                    quad(NQ - 1, True, False)

                @block.vector
                def _(dve):
                    def normalise(i):
                        ln_stats(dve, stats, mv, rstd, QT, i, var_ready)
                        dve.wait_ge(rstd_ready, i + 1)
                        dve.wait_ge(xT_stored, i + 1)
                        ln_apply(dve, xn, mv, rstd, QT, i).then_inc(xn_ready, 1)
                        dve.drain()
                        dve.tensor_tensor(h[:, ds(i * QT, QT), :], h[:, ds(i * QT, QT), :], xn[:, :, :], ALU.add)

                    def largest(i):
                        dve.wait_ge(logit_mm, i + 1)
                        lg = ps[:, 1, 0:QT * E1].rearrange("p (t e) -> p t e", t=QT)
                        dve.tensor_reduce(nmx[:, :], lg, AX.X, ALU.max)
                        dve.drain()
                        dve.tensor_scalar(nmx[:, :], nmx[:, :], -1.0, None, ALU.mult).then_inc(nmx_ready, 1)

                    def take_ranks(i):
                        dve.wait_ge(rank_mm, i + 1)
                        dve.tensor_copy(rank[:, ds(i * QT, QT), :],
                                        ps[:, 2, 0:QT * E1].rearrange("p (t e) -> p t e", t=QT))
                        dve.tensor_tensor(seen[:, :], seen[:, :], more[:, :], ALU.add)
                        dve.drain()

                    def quad(i, has_last, has_next):
                        if has_next:
                            normalise(i + 1)
                        if has_last:
                            take_ranks(i - 1)
                        dve.wait_ge(ex_ready, i + 1)
                        dve.memset(carrier[:, :], 0.0)
                        for j in range(QT):
                            dve.max(top[:, j, :], ex[:, j, :])
                        dve.drain()
                        for j in range(QT):
                            dve.max_index(topi[:, j, :], top[:, j, :], ex[:, j, :])
                        dve.tensor_reduce(tot[:, :], top[:, :, 0:TOPK1], AX.X, ALU.add)
                        dve.drain()
                        if has_next:
                            largest(i + 1)
                        dve.reciprocal(tot[:, :], tot[:, :])
                        dve.tensor_copy(topf[:, :, :], topi[:, :, :])
                        dve.drain()
                        dve.tensor_tensor(wts[:, ds(i * QT, QT), :], top[:, :, 0:TOPK1],
                                          tot[:, :].unsqueeze(2).to_broadcast([P, QT, TOPK1]), ALU.mult)
                        dve.tensor_copy(pick[:, ds(i * QT, QT), :], topf[:, :, :])
                        for j in range(QT):
                            dve.tensor_tensor(eq[:, j], C("iota")[:, 0:E1].unsqueeze(1).to_broadcast([P, TOPK1, E1]),
                                              topf[:, j, 0:TOPK1].unsqueeze(2).to_broadcast([P, TOPK1, E1]),
                                              ALU.is_equal)
                        dve.drain()
                        dve.tensor_reduce(chosen[:, :, :], eq[:, :, :, :].rearrange("p t k e -> p t e k"), AX.X,
                                          ALU.add).then_inc(chosen_ready, 1)
                        dve.drain()
                        dve.tensor_reduce(more[:, :], chosen[:, :, :].rearrange("p t e -> p e t"), AX.X, ALU.add)
                        dve.drain()

                    dve.memset(seen[:, :], 0.0)
                    normalise(0)
                    largest(0)
                    run(dve, quad)
                    take_ranks(NQ - 1)

                @block.gpsimd
                def _(pool):
                    pool.memset(neghalf[:, :], -0.5)
                    pool.drain()
                    pool.sem_inc(xT_stored, 1)
                    with pool.Fori(0, NQ) as i:
                        pool.wait_ge(var_ready, i + 1)
                        ln_rstd(pool, rstd, neghalf, QT).then_inc(rstd_ready, 1)
                        pool.wait_ge(xn_ready, i + 1)
                        pool.tensor_copy(xn_all[:, ds(i * QT, QT), :], xn[:, :, :])
                        pool.wait_ge(xs_ready, i + 1)
                        pool.tensor_copy(xT[:, ds(i * QN, QN)], xs[:, :]).then_inc(xT_stored, 1)

                @block.scalar
                def _(act):
                    act.preload_act_table(ACT.Exp)
                    with act.Fori(0, NQ) as i:
                        act.wait_ge(xT_stored, i + 1)
                        act.wait_ge(turned, i + 1)
                        act.copy(xs[:, :], ps[:, 0, :]).then_inc(xs_ready, 1)
                        act.wait_ge(nmx_ready, i + 1)
                        for j in range(QT):
                            last = act.activation(ex[:, j, :], ps[:, 1, j * E1:(j + 1) * E1], ACT.Exp,
                                                  bias=nmx[:, j:j + 1])
                        last.then_inc(ex_ready, 1)

                @block.tensor
                def _(pe):
                    def logits(i):
                        pe.wait_ge(xn_ready, i + 1)
                        for j in range(QT):
                            last = pe.transpose(ps[:, 0, j * P:(j + 1) * P], xn[:, j, :], ident)
                        last.then_inc(turned, 1)
                        pe.wait_ge(xs_ready, i + 1)
                        if not isinstance(i, int) or i:
                            pe.wait_ge(ex_ready, i)
                        for j in range(QT):
                            last = pe.matmul(ps[:, 1, j * E1:(j + 1) * E1], xs[:, j * P:(j + 1) * P], W("wr1"),
                                             start=True, stop=True)
                        last.then_inc(logit_mm, 1)

                    def quad(i, has_last, has_next):
                        if has_next:
                            logits(i + 1)
                        pe.wait_ge(chosen_ready, i + 1)
                        for j in range(QT):
                            dst = ps[:, 2, j * E1:(j + 1) * E1]
                            pe.matmul(dst, C("full"), seen[:, :], start=True, stop=False)
                            for before in range(j):
                                pe.matmul(dst, C("full"), chosen[:, before, :], start=False, stop=False)
                            last = pe.matmul(dst, C("earlier"), chosen[:, j, :], start=False, stop=True)
                        last.then_inc(rank_mm, 1)

                    logits(0)
                    run(pe, quad)

        def moe1_dispatch(xn_all, xT, pick, rank, seen, pos_i, erow, source, x_rows, x_out):
            with ExitStack() as st:
                tiles_f = sb("d_tiles_f", [P, E1], F32, st)
                tiles_i = sb("d_tiles_i", [P, E1], I32, st)
                ends = sb("d_ends", [P, E1], F32, st)
                base = sb("d_base", [P, E1], F32, st)
                junk = sb("d_junk", [P, E1], F32, st)
                end_col = sb("d_end_col", [E1, 1], F32, st)
                past = sb("d_past", [E1, NTILE], F32, st)
                pos = sb("d_pos", [P, T, TOPK1], F32, st)
                tile_i = sb("d_tile_i", [P, T, TOPK1], I32, st)
                tile_f = sb("d_tile_f", [P, T, TOPK1], F32, st)
                row_f = sb("d_row_f", [P, T, TOPK1], F32, st)
                row_hot = sb("d_row_hot", [P, 2, TOPK1, P], F16, st)
                row_token = sb("d_row_token", [P, 2, TOPK1, P], F16, st)
                tile_hot = sb("d_tile_hot", [P, 2, TOPK1, NTILE], F16, st)
                pick_junk = sb("d_pick_junk", [P, T, TOPK1, E1], F32, st)
                wsh = sb("d_wsh", [P, NS1, W1COLS], F32, st)
                act1 = sb("d_act1", [P, 2, QN], F32, st)
                a = sb("d_a", [P, 2, QN], F32, st)
                wsh_in = sem("d_wsh_in")
                count_mm = sem("d_count_mm")
                past_ready = sem("d_past_ready")
                erow_mm = sem("d_erow_mm")
                row_ready = sem("d_row_ready")
                token_ready = sem("d_token_ready")
                tile_ready = sem("d_tile_ready")
                source_mm = sem("d_source_mm")
                hid_mm = sem("d_hid_mm")
                silu_done = sem("d_silu_done")
                a_ready = sem("d_a_ready")
                y_mm = sem("d_y_mm")
                y_used = sem("d_y_used")
                SH = NS1 * NQ
                PT = T // SH
                block = st.enter_context(nc.Block())

                @block.sync
                def _(sp):
                    sp.dma_start(wsh[:, :, :], w1[:, E1:EXP1, :]).then_inc(wsh_in, 16)
                    sp.dma_start(x_rows.rearrange("(t p) d -> p t d", p=P), xn_all[:, :, :]).then_inc(x_out, 16)

                @block.vector
                def _(dve):
                    dve.wait_ge(count_mm, 1)
                    dve.tensor_scalar(tiles_i[:, :], ps[:, 6, 0:E1], 63.5, 1.0 / P, ALU.add, ALU.mult)
                    dve.drain()
                    dve.tensor_copy(tiles_f[:, :], tiles_i[:, :])
                    dve.drain()
                    dve.tensor_tensor_scan(ends[:, :], C("ones")[:, 0:E1], tiles_f[:, :], 0.0, ALU.mult, ALU.add)
                    dve.drain()
                    dve.tensor_tensor(base[:, :], ends[:, :], tiles_f[:, :], ALU.subtract)
                    dve.scalar_tensor_tensor(junk[0:E1, :], ends[0:E1, :], 1.0, ident[0:E1, 0:E1], ALU.mult, ALU.mult,
                                             accum_out=end_col[:, :])
                    dve.drain()
                    dve.tensor_scalar(base[:, :], base[:, :], float(P), None, ALU.mult)
                    dve.tensor_scalar(past[:, :], C("iota_tiles", E1), end_col[:, :], None,
                                      ALU.is_ge).then_inc(past_ready, 1)
                    dve.drain()
                    dve.tensor_tensor(rank[:, :, :], rank[:, :, :], base[:, :].unsqueeze(1).to_broadcast([P, T, E1]),
                                      ALU.add)
                    dve.drain()

                    def place(n):
                        at = slice(n * PT, (n + 1) * PT)
                        for t in range(n * PT, (n + 1) * PT):
                            for k in range(TOPK1):
                                dve.scalar_tensor_tensor(pick_junk[:, t, k, :], C("iota")[:, 0:E1], pick[:, t, k:k + 1],
                                                         rank[:, t, :], ALU.is_equal, ALU.mult,
                                                         accum_out=pos[:, t, k:k + 1])
                        dve.drain()
                        dve.tensor_copy(pos_i[:, at, :], pos[:, at, :])
                        dve.tensor_scalar(tile_i[:, at, :], pos[:, at, :], -63.5, 1.0 / P, ALU.add, ALU.mult)
                        dve.drain()
                        dve.tensor_copy(tile_f[:, at, :], tile_i[:, at, :])
                        dve.drain()
                        dve.scalar_tensor_tensor(row_f[:, at, :], tile_f[:, at, :], -float(P), pos[:, at, :], ALU.mult,
                                                 ALU.add)
                        dve.drain()

                    def mark(t):
                        if t >= 2:
                            dve.wait_ge(token_ready, t - 1)
                        dve.tensor_tensor(row_hot[:, t % 2], C("iota").unsqueeze(1).to_broadcast([P, TOPK1, P]),
                                          row_f[:, t, :].unsqueeze(2).to_broadcast([P, TOPK1, P]), ALU.is_equal
                                          ).then_inc(row_ready, 1)
                        if t >= 2:
                            dve.wait_ge(source_mm, t - 1)
                        dve.tensor_tensor(tile_hot[:, t % 2],
                                          C("iota_tiles").unsqueeze(1).to_broadcast([P, TOPK1, NTILE]),
                                          tile_f[:, t, :].unsqueeze(2).to_broadcast([P, TOPK1, NTILE]), ALU.is_equal
                                          ).then_inc(tile_ready, 1)

                    def combine(n):
                        dve.wait_ge(y_mm, n + 1)
                        c = n % NQ
                        hq = h[:, c * QT:(c + 1) * QT, :].rearrange("p t d -> p (t d)")
                        dve.tensor_tensor(hq, hq, ps[:, 4 + n % 2, :], ALU.add).then_inc(y_used, 1)

                    for n in range(SH):
                        place(n)
                        for t in range(n * PT, (n + 1) * PT):
                            mark(t)
                        if n == 0:
                            dve.wait_ge(erow_mm, 1)
                            dve.tensor_scalar(erow[:, :], ps[0:1, 7, 0:NTILE], float(E1 - 1), float(W1COLS),
                                              ALU.min, ALU.mult)
                        dve.wait_ge(silu_done, n + 1)
                        if n >= 2:
                            dve.wait_ge(y_mm, n - 1)
                        dve.tensor_tensor(a[:, n % 2, :], act1[:, n % 2, :], ps[:, 2 * (n % 2) + 1, :],
                                          ALU.mult).then_inc(a_ready, 1)
                        if n:
                            combine(n - 1)
                    dve.wait_ge(source_mm, T)
                    dve.tensor_copy(source[:, :], ps[:, 6, 0:NTILE])
                    combine(SH - 1)

                @block.scalar
                def _(act):
                    act.preload_act_table(ACT.Silu)
                    for n in range(SH):
                        act.wait_ge(hid_mm, n + 1)
                        if n >= 2:
                            act.wait_ge(a_ready, n - 1)
                        act.activation(act1[:, n % 2, :], ps[:, 2 * (n % 2), :], ACT.Silu).then_inc(silu_done, 1)
                        for t in range(n * PT, (n + 1) * PT):
                            act.wait_ge(row_ready, t + 1)
                            if t >= 2:
                                act.wait_ge(source_mm, t - 1)
                            act.activation(row_token[:, t % 2], row_hot[:, t % 2], ACT.Copy,
                                           scale=C("token")[:, t:t + 1]).then_inc(token_ready, 1)

                @block.tensor
                def _(pe):
                    pe.matmul(ps[:, 6, 0:E1], C("full"), seen[:, :], start=True, stop=True).then_inc(count_mm, 1)

                    def hidden(n):
                        e, c = n // NQ, n % NQ
                        if n >= 2:
                            pe.wait_ge(a_ready, n - 1)
                        for part in range(2):
                            last = pe.matmul(ps[:, 2 * (n % 2) + part, :], wsh[:, e, part * D:(part + 1) * D],
                                             xT[:, c * QN:(c + 1) * QN], start=True, stop=True)
                        last.then_inc(hid_mm, 1)

                    def output(n):
                        e = n // NQ
                        pe.wait_ge(a_ready, n + 1)
                        if n >= 2:
                            pe.wait_ge(y_used, n - 1)
                        for j in range(QT):
                            last = pe.matmul(ps[:, 4 + n % 2, j * D:(j + 1) * D], a[:, n % 2, j * P:(j + 1) * P],
                                             wsh[:, e, 2 * D:3 * D], start=True, stop=True)
                        last.then_inc(y_mm, 1)

                    def tokens(t):
                        pe.wait_ge(token_ready, t + 1)
                        pe.wait_ge(tile_ready, t + 1)
                        for k in range(TOPK1):
                            last = pe.matmul(ps[:, 6, 0:NTILE], row_token[:, t % 2, k, :], tile_hot[:, t % 2, k, :],
                                             start=(t == 0 and k == 0), stop=(t == T - 1 and k == TOPK1 - 1))
                        last.then_inc(source_mm, 1)

                    pe.wait_ge(wsh_in, 16)
                    hidden(0)
                    pe.wait_ge(past_ready, 1)
                    pe.matmul(ps[0:1, 7, 0:NTILE], C("ones", E1)[:, 0:1], past[:, :], start=True,
                              stop=True).then_inc(erow_mm, 1)
                    for n in range(SH):
                        if n:
                            output(n - 1)
                        if n + 1 < SH:
                            hidden(n + 1)
                        for t in range(n * PT, (n + 1) * PT):
                            tokens(t)
                    output(SH - 1)

        def moe1_tiles(wexp, erow, source, x_rows, x_out, ysorted, wexp_in):
            with ExitStack() as st:
                xin = sb("t_xin", [P, 2, QT, D], F32, st)
                xT = sb("t_xT", [P, 2, QT, P], F32, st)
                act1 = sb("t_act1", [P, 2, QT, F1], F32, st)
                a = sb("t_a", [P, 2, QT, F1], F32, st)
                aT = sb("t_aT", [P, 2, QT, P], F32, st)
                y = sb("t_y", [P, 2, QT, D], F32, st)
                x_in = [sem("t_x_in0"), sem("t_x_in1")]
                y_out = [sem("t_y_out0"), sem("t_y_out1")]
                x_turned = sem("t_x_turned")
                xT_ready = sem("t_xT_ready")
                hid_mm = sem("t_hid_mm")
                silu_done = sem("t_silu_done")
                a_ready = sem("t_a_ready")
                a_turned = sem("t_a_turned")
                aT_ready = sem("t_aT_ready")
                down_mm = sem("t_down_mm")
                y_ready = sem("t_y_ready")
                NG = NTILE // QT
                wflat = wexp[:, :, :].rearrange("p e c -> p (e c)")
                block = st.enter_context(nc.Block())
                yg = ysorted.rearrange("(n p) d -> p n d", p=P)

                def run(eng, step):
                    for m in range(4):
                        step(m, m % 2, m // 2)
                    with eng.Fori(0, NG // 2 - 3) as pair:
                        step(pair * 2 + 4, 0, pair + 2)
                        step(pair * 2 + 5, 1, pair + 2)
                    step(NG - 2, 0, NG // 2 - 1)
                    step(NG - 1, 1, NG // 2 - 1)
                    step(NG, 0, NG // 2)
                    step(NG + 1, 1, NG // 2)

                def isnum(m, lo, hi):
                    return isinstance(m, int) and lo <= m <= hi

                @block.gpsimd
                def _(pool):
                    pool.wait_ge(x_out, 16)
                    for m in range(NG):
                        s = m % 2
                        if m >= 2:
                            pool.wait_ge(x_turned, m - 1)
                        for j in range(QT):
                            t = m * QT + j
                            pool.indirect_dma_start(xin[:, s, j, :], None, x_rows,
                                                    bass.IndirectOffsetOnAxis(ap=source[:, t:t + 1], axis=0)
                                                    ).then_inc(x_in[s], 16)

                @block.sync
                def _(sp):
                    def step(m, s, r):
                        if not isnum(m, 0, 1):
                            sp.wait_ge(y_ready, m - 1)
                            sp.dma_start(yg[:, ds((m - 2) * QT, QT), :], y[:, s]).then_inc(y_out[s], 16)

                    run(sp, step)
                    for s in range(2):
                        sp.wait_ge(y_out[s], 16 * (NG // 2))

                @block.tensor
                def _(pe):
                    def turn(m, s, r):
                        pe.wait_ge(x_in[s], r * (16 * QT) + 16 * QT)
                        if not isnum(m, 0, 0):
                            pe.wait_ge(xT_ready, m)
                        for j in range(QT):
                            last = pe.transpose(ps[:, 0, j * P:(j + 1) * P], xin[:, s, j, :], ident)
                        last.then_inc(x_turned, 1)

                    def experts(m):
                        _, starts = nc.values_load_multi_w_load_instructions(
                            erow[0:1, ds(m * QT, QT)], engines=(mybir.EngineType.PE,), min_val=0,
                            max_val=(E1 - 1) * W1COLS,
                            skip_runtime_bounds_check_because="the row holds min(count, E1 - 1) * W1COLS, count >= 0")
                        return starts

                    def step(m, s, r):
                        if not isnum(m, 0, 1):
                            down_starts = experts(m - 2)
                        if not isnum(m, NG, NG + 1):
                            starts = experts(m)
                            pe.wait_ge(xT_ready, m + 1)
                            if not isnum(m, 0, 1):
                                pe.wait_ge(a_ready, m - 1)
                            for j in range(QT):
                                last = pe.matmul(ps[:, 2 + 2 * s + j // 2, (j % 2) * 2 * F1:(j % 2 + 1) * 2 * F1],
                                                 xT[:, s, j, :], wflat[:, ds(starts[j], 2 * F1)], start=True, stop=True)
                            last.then_inc(hid_mm, 1)
                        if not isnum(m, 0, 0) and not isnum(m, NG + 1, NG + 1):
                            pe.wait_ge(a_ready, m)
                            if not isnum(m, 1, 1):
                                pe.wait_ge(aT_ready, m - 1)
                            for j in range(QT):
                                last = pe.transpose(ps[:, 1, j * P:(j + 1) * P], a[:, 1 - s, j, :], ident)
                            last.then_inc(a_turned, 1)
                        if not isnum(m, NG - 1, NG + 1):
                            turn(m + 1, 1 - s, r + s)
                        if not isnum(m, 0, 1):
                            pe.wait_ge(aT_ready, m - 1)
                            if not isnum(m, 2, 3):
                                pe.wait_ge(y_ready, m - 3)
                            for j in range(QT):
                                last = pe.matmul(ps[:, 6 + s, j * D:(j + 1) * D], aT[:, s, j, :],
                                                 wflat[:, ds(down_starts[j] + 2 * F1, D)], start=True, stop=True)
                            last.then_inc(down_mm, 1)

                    pe.wait_ge(wexp_in, 16 * WLOADS)
                    turn(0, 0, 0)
                    run(pe, step)

                @block.scalar
                def _(act):
                    def take_xT(m, s):
                        act.wait_ge(x_turned, m + 1)
                        if not isnum(m, 0, 1):
                            act.wait_ge(hid_mm, m - 1)
                        act.copy(xT[:, s].rearrange("p t q -> p (t q)"), ps[:, 0, :]).then_inc(xT_ready, 1)

                    def step(m, s, r):
                        if not isnum(m, NG, NG + 1):
                            act.wait_ge(hid_mm, m + 1)
                            if not isnum(m, 0, 1):
                                act.wait_ge(a_ready, m - 1)
                            gate = ps[:, 2 + 2 * s:4 + 2 * s, :].rearrange("p b (t c) -> p (b t) c", t=2)[:, :, 0:F1]
                            act.activation(act1[:, s], gate, ACT.Silu).then_inc(silu_done, 1)
                        if not isnum(m, NG - 1, NG + 1):
                            take_xT(m + 1, 1 - s)
                        if not isnum(m, 0, 1):
                            act.wait_ge(down_mm, m - 1)
                            if not isnum(m, 2, 3):
                                act.wait_ge(y_out[s], r * 16 - 16)
                            act.copy(y[:, s].rearrange("p t d -> p (t d)"), ps[:, 6 + s, :]).then_inc(y_ready, 1)

                    act.preload_act_table(ACT.Silu)
                    take_xT(0, 0)
                    run(act, step)

                @block.vector
                def _(dve):
                    def step(m, s, r):
                        if not isnum(m, 0, 0) and not isnum(m, NG + 1, NG + 1):
                            dve.wait_ge(a_turned, m)
                            if not isnum(m, 1, 2):
                                dve.wait_ge(down_mm, m - 2)
                            dve.tensor_copy(aT[:, 1 - s].rearrange("p t q -> p (t q)"), ps[:, 1, :]
                                            ).then_inc(aT_ready, 1)
                        if not isnum(m, NG, NG + 1):
                            dve.wait_ge(silu_done, m + 1)
                            if not isnum(m, 0, 1):
                                dve.wait_ge(a_turned, m - 1)
                            up = ps[:, 2 + 2 * s:4 + 2 * s, :].rearrange("p b (t c) -> p (b t) c", t=2)[:, :, F1:2 * F1]
                            dve.tensor_tensor(a[:, s], act1[:, s], up, ALU.mult).then_inc(a_ready, 1)

                    run(dve, step)

        def moe1_combine(pos_i, wts, ysorted):
            with ExitStack() as st:
                SLOTS = 4
                got = sb("g_got", [P, SLOTS, TOPK1, D], F32, st)
                got_in = [sem(f"g_got_in{s}") for s in range(SLOTS)]
                added = sem("g_added")
                out_done = sem("g_out_done")
                block = st.enter_context(nc.Block())

                @block.gpsimd
                def _(pool):
                    for t in range(T):
                        if t >= SLOTS:
                            pool.wait_ge(added, t - SLOTS + 1)
                        for k in range(TOPK1):
                            pool.indirect_dma_start(got[:, t % SLOTS, k, :], None, ysorted,
                                                    bass.IndirectOffsetOnAxis(ap=pos_i[:, t, k:k + 1], axis=0)
                                                    ).then_inc(got_in[t % SLOTS], 16)

                @block.vector
                def _(dve):
                    for t in range(T):
                        dve.wait_ge(got_in[t % SLOTS], 16 * TOPK1 * (t // SLOTS + 1))
                        for k in range(TOPK1):
                            last = dve.scalar_tensor_tensor(h[:, t, :], got[:, t % SLOTS, k, :], wts[:, t, k:k + 1],
                                                            h[:, t, :], ALU.mult, ALU.add)
                            if k < TOPK1 - 1:
                                dve.drain()
                        last.then_inc(added, 1)

                @block.sync
                def _(sp):
                    for q in range(NQ):
                        sp.wait_ge(added, QT * (q + 1))
                        sp.dma_start(out[:, q * QT:(q + 1) * QT, :], h[:, q * QT:(q + 1) * QT, :]).then_inc(out_done, 16)
                    sp.wait_ge(out_done, 16 * NQ)

        token_stage()
        gla_stage()
        wexp = sb("wexp", [P, E1, W1COLS])
        wexp_in = sem("wexp_in")
        moe0_stage(wexp, wexp_in)
        attention_stage()
        moe1_stage(wexp, wexp_in)


def layouts(inputs):
    import numpy as np

    g = {k: np.asarray(v) for k, v in inputs.items()}
    weights = np.zeros((P, WCOLS), np.float32)

    def put(name, a):
        o, n = _cols[name]
        assert a.shape[1] == n, (name, a.shape)
        weights[0:a.shape[0], o:o + n] = a

    put("tok_w", g["L0_tok_expert_w"].transpose(2, 0, 1).reshape(D, E_TOK * D))
    put("tok_b", g["L0_tok_expert_b"])
    put("wk", g["L0_attn_Wk"].T)
    put("wq", g["L0_attn_Wq"].T)
    put("wv", g["L0_attn_Wv"].T)
    put("wo0", g["L0_attn_Wo"].T)
    put("wg1", g["L0_attn_Wg1"].T)
    put("wg2", g["L0_attn_Wg2"].T)
    for z in "kqv":
        put("conv_" + z, g["L0_attn_conv_" + z][:, 0, :])
    put("bg2", g["L0_attn_bg2"][:, None])
    put("norm_w", g["L0_attn_norm_w"][:, None])
    put("rw0", g["L0_ffn_router_w"].T)
    put("rb0", g["L0_ffn_router_b"][None])
    put("fc2_b", g["L0_ffn_fc2_b"])
    qkv, bqkv = g["L1_attn_Wqkv"], g["L1_attn_bqkv"]
    for name, bname, part in (("aq", "abq", 0), ("ak", "abk", 1)):
        w = qkv[:, part * D:(part + 1) * D].reshape(D, 2, 4, DH)
        b = bqkv[part * D:(part + 1) * D].reshape(2, 4, DH)
        put(name, np.pad(w, ((0, 0), (0, 0), (0, 0), (0, 32 - DH))).reshape(D, 2 * P))
        put(bname, np.pad(b, ((0, 0), (0, 0), (0, 32 - DH))).reshape(2, P).T)
    put("av", qkv[:, 2 * D:3 * D])
    put("abv", bqkv[None, 2 * D:3 * D])
    put("awo", g["L1_attn_Wo"])
    put("abo", g["L1_attn_bo"][None])
    put("wr1", g["L1_ffn_Wr"])

    consts = np.zeros((P, CCOLS), np.float32)

    def cput(name, a):
        o, n = _ccols[name]
        consts[:, o:o + n] = a

    cput("ident", np.eye(P))
    cput("iota", np.arange(P)[None])
    cput("reset", (np.arange(QN) % CHUNK != 0)[None])
    cput("ones", 1.0)
    cput("full", 1.0)
    cput("earlier", np.triu(np.ones((P, P)), 1))
    cput("iota_tiles", np.arange(NTILE)[None])
    cput("token", np.arange(N).reshape(T, P).T)
    step = D // E_TOK
    cput("thr", np.tile([-3.0e38] + [step * e - 1 for e in range(1, E_TOK)] + [3.0e38], QT)[None])
    j, i = np.arange(P)[:, None], np.arange(P)[None]
    causal = ((j <= i) & (j // CHUNK == i // CHUNK)).astype(np.uint32)

    fc1 = g["L0_ffn_fc1_w"].transpose(2, 0, 1)
    fc2 = g["L0_ffn_fc2_w"].reshape(E0, D, 2, P).transpose(3, 0, 2, 1).reshape(P, E0, 2 * D)
    b1 = g["L0_ffn_fc1_b"].reshape(E0, 4, P).transpose(2, 0, 1)
    w0 = np.concatenate([fc1, fc2, b1], axis=2)
    w1 = np.concatenate([
        np.concatenate([g["L1_ffn_Wg"], g["L1_ffn_sWg"]]), np.concatenate([g["L1_ffn_Wu"], g["L1_ffn_sWu"]]),
        np.concatenate([g["L1_ffn_Wd"], g["L1_ffn_sWd"]])], axis=2).transpose(1, 0, 2)
    return {
        "ids": g["x"].reshape(T, P).T,
        "emb_gate": np.concatenate([g["L0_tok_emb_table"], g["L0_tok_gate_table"]], axis=1),
        "weights": weights,
        "consts": consts,
        "causal": causal,
        "rel": g["L1_attn_rel_pos_bias"].T,
        "w0": w0,
        "w1": w1,
    }


def kernel(**inputs):
    import numpy as np
    import concourse.bacc as bacc
    from concourse.bass_utils import run_bass_kernel_spmd

    nc = bacc.Bacc("TRN2", target_bir_lowering=False, num_devices=1)
    arrays, args = {}, []
    for name, a in layouts(inputs).items():
        a = np.ascontiguousarray(a)
        arrays["in_" + name] = a
        args.append(nc.dram_tensor("in_" + name, a.shape, mybir.dt.from_np(a.dtype), kind="ExternalInput").ap())
    out = nc.dram_tensor("out_0", (P, T, D), F32, kind="ExternalOutput").ap()
    tower_kernel(nc, *args, out)
    r = run_bass_kernel_spmd(nc, [arrays], core_ids=[0])
    return r.results[0]["out_0"].transpose(1, 0, 2).reshape(B, L, D)
```
